# Optimizing a Trainium2 kernel written in Bass

```python
import numpy as np
import jax
import jax.numpy as jnp

def _softmax(x, axis=-1):
    return jax.nn.softmax(x, axis=axis)

def _gelu(x):
    return jax.nn.gelu(x, approximate=True)

def _silu(x):
    return jax.nn.silu(x)

def _sigmoid(x):
    return jax.nn.sigmoid(x)

def _layernorm(x, axis=-1, eps=1e-05):
    m = jnp.mean(x, axis=axis, keepdims=True)
    v = jnp.var(x, axis=axis, keepdims=True)
    return (x - m) / jnp.sqrt(v + eps)

def _scatter_add(tgt, idx, src, axis=0):
    return tgt.at[idx].add(src)

def _segment_sum(src, seg, n):
    return jax.ops.segment_sum(src, seg, n)
kernel_name = 'mk_decoder_postln_d2_seqx_r8_df2844'

def setup_inputs(seed: int=0):
    np.random.seed(seed)
    _w = jnp.asarray

    def _rec_inputs():
        import jax
        import jax.numpy as jnp
        _rk = jax.random.key(seed)
        x = -0.0002928 + 1 * jax.random.normal(jax.random.fold_in(_rk, 1), (1, 1024, 128), jnp.float32)
        _lenS = 1024 - jax.random.randint(jax.random.fold_in(_rk, 7), (1,), 0, max(1, 1024 // 4) + 1, jnp.int32)
        _lenS2 = 6404 - jax.random.randint(jax.random.fold_in(_rk, 8), (1,), 0, max(1, 6404 // 4) + 1, jnp.int32)
        _ctx_1024P = jax.random.normal(jax.random.fold_in(_rk, 11), (1, 16, 128), jnp.float32)
        _ctx_1024c = jax.random.dirichlet(jax.random.fold_in(_rk, 511), 0.3 * jnp.ones((16,), jnp.float32), (1, 6404))
        _ctx_1024t = jnp.einsum('bsk,bkd->bsd', _ctx_1024c, _ctx_1024P)
        _ctx_1024t = _ctx_1024t * jax.lax.rsqrt(jnp.mean(jnp.square(_ctx_1024t)) + 1e-12) * 0.953939
        ctx_1024 = -1.39393e-06 + 0.999914 * (_ctx_1024t + 0.3 * jax.random.normal(jax.random.fold_in(_rk, 611), (1, 6404, 128), jnp.float32))
        return (x, ctx_1024)
    x, ctx_1024 = _rec_inputs()

    def _L0_attn_setup():
        import jax, jax.numpy as jnp
        import numpy as np
        from jax import lax
        D_MODEL = 128
        D_STATE = 16
        D_CONV = 4
        EXPAND = 2
        D_INNER = EXPAND * D_MODEL
        DT_RANK = (D_MODEL + 15) // 16
        BATCH, LENGTH = (2, 128)
        DT_MIN, DT_MAX = (0.001, 0.1)

        def silu(v):
            return v * jax.nn.sigmoid(v)
        key = jax.random.key(seed)
        ks = jax.random.split(key, 8)
        s = lambda n: 1.0 / np.sqrt(n)
        x = jax.random.normal(ks[0], (BATCH, LENGTH, D_MODEL), jnp.float32)
        W_in = jax.random.normal(ks[1], (2 * D_INNER, D_MODEL), jnp.float32) * s(D_MODEL)
        W_conv = jax.random.normal(ks[2], (D_INNER, 1, D_CONV), jnp.float32) * s(D_CONV)
        W_xproj = jax.random.normal(ks[3], (DT_RANK + 2 * D_STATE, D_INNER), jnp.float32) * s(D_INNER)
        dt_init_std = DT_RANK ** (-0.5)
        W_dt = jax.random.uniform(ks[4], (D_INNER, DT_RANK), jnp.float32, minval=-dt_init_std, maxval=dt_init_std)
        dt = jnp.exp(jax.random.uniform(ks[5], (D_INNER,), jnp.float32) * (np.log(DT_MAX) - np.log(DT_MIN)) + np.log(DT_MIN))
        dt = jnp.maximum(dt, dt_init_std)
        b_dt = dt + jnp.log(-jnp.expm1(-dt))
        A_log = jnp.log(jnp.broadcast_to(jnp.arange(1, D_STATE + 1, dtype=jnp.float32), (D_INNER, D_STATE)))
        D = jnp.ones((D_INNER,), jnp.float32)
        W_out = jax.random.normal(ks[6], (D_MODEL, D_INNER), jnp.float32) * s(D_INNER)
        return dict(x=x, W_in=W_in, W_conv=W_conv, W_xproj=W_xproj, W_dt=W_dt, b_dt=b_dt, A_log=A_log, D=D, W_out=W_out)
    _L0_attn_all = _L0_attn_setup()
    _L0_attn_in = {k: v for k, v in _L0_attn_all.items() if k in ('W_in', 'W_conv', 'W_xproj', 'W_dt', 'b_dt', 'A_log', 'D', 'W_out')}
    del _L0_attn_all

    def _L0_xattn_setup():
        import jax, jax.numpy as jnp
        import numpy as np
        D_MODEL = 128
        N_HEAD = 16
        D_HEAD = D_MODEL // N_HEAD
        key = jax.random.key(seed)
        ks = jax.random.split(key, 6)
        B, L, M = (2, 256, 256)
        q = jax.random.normal(ks[0], (B, L, D_MODEL), dtype=jnp.float32)
        kv = jax.random.normal(ks[1], (B, L, D_MODEL), dtype=jnp.float32)
        mem = jax.random.normal(ks[2], (B, M, D_MODEL), dtype=jnp.float32)
        s = 1.0 / np.sqrt(D_MODEL)
        w_q = jax.random.normal(ks[3], (D_MODEL, D_MODEL), dtype=jnp.float32) * s
        w_kv = jax.random.normal(ks[4], (D_MODEL, 2 * D_HEAD), dtype=jnp.float32) * s
        w_concat = jax.random.normal(ks[5], (D_MODEL, D_MODEL), dtype=jnp.float32) * s
        return {'q': q, 'kv': kv, 'mem': mem, 'w_q': w_q, 'w_kv': w_kv, 'w_concat': w_concat}
    _L0_xattn_all = _L0_xattn_setup()
    _L0_xattn_in = {k: v for k, v in _L0_xattn_all.items() if k in ('w_q', 'w_kv', 'w_concat')}
    del _L0_xattn_all

    def _L0_ffn_setup():
        import jax, jax.numpy as jnp
        import numpy as np
        D_MODEL = 128
        D_FF = 512
        NUM_M = 2
        E_ROUTER = 8 * NUM_M - 1
        D_FF_R = D_FF // NUM_M
        TOP_K = NUM_M * 2 - 1
        B, T = (2, 256)

        def _expert_stack(x, W1, b1, W2, b2):
            h = jax.nn.gelu(jnp.einsum('btd,edf->ebtf', x, W1) + b1[:, None, None, :], approximate=False)
            return jnp.einsum('ebtf,efd->ebtd', h, W2) + b2[:, None, None, :]
        key = jax.random.key(seed)
        ks = jax.random.split(key, 12)
        s = lambda fan_in: 1.0 / np.sqrt(fan_in)
        x = jax.random.normal(ks[0], (B, T, D_MODEL), dtype=jnp.float32)
        sW1 = jax.random.uniform(ks[1], (1, D_MODEL, D_FF), jnp.float32, -s(D_MODEL), s(D_MODEL))
        sb1 = jax.random.uniform(ks[2], (1, D_FF), jnp.float32, -s(D_MODEL), s(D_MODEL))
        sW2 = jax.random.uniform(ks[3], (1, D_FF, D_MODEL), jnp.float32, -s(D_FF), s(D_FF))
        sb2 = jax.random.uniform(ks[4], (1, D_MODEL), jnp.float32, -s(D_FF), s(D_FF))
        rW1 = jax.random.uniform(ks[5], (E_ROUTER, D_MODEL, D_FF_R), jnp.float32, -s(D_MODEL), s(D_MODEL))
        rb1 = jax.random.uniform(ks[6], (E_ROUTER, D_FF_R), jnp.float32, -s(D_MODEL), s(D_MODEL))
        rW2 = jax.random.uniform(ks[7], (E_ROUTER, D_FF_R, D_MODEL), jnp.float32, -s(D_FF_R), s(D_FF_R))
        rb2 = jax.random.uniform(ks[8], (E_ROUTER, D_MODEL), jnp.float32, -s(D_FF_R), s(D_FF_R))
        gW = jax.random.uniform(ks[9], (D_MODEL, E_ROUTER), jnp.float32, -s(D_MODEL), s(D_MODEL))
        gb = jax.random.uniform(ks[10], (E_ROUTER,), jnp.float32, -s(D_MODEL), s(D_MODEL))
        return {'x': x, 'sW1': sW1, 'sb1': sb1, 'sW2': sW2, 'sb2': sb2, 'rW1': rW1, 'rb1': rb1, 'rW2': rW2, 'rb2': rb2, 'gW': gW, 'gb': gb}
    _L0_ffn_all = _L0_ffn_setup()
    _L0_ffn_in = {k: v for k, v in _L0_ffn_all.items() if k in ('sW1', 'sb1', 'sW2', 'sb2', 'rW1', 'rb1', 'rW2', 'rb2', 'gW', 'gb')}
    del _L0_ffn_all

    def _L1_attn_setup():
        import jax, jax.numpy as jnp
        import numpy as np
        B, N, C = (2, 256, 128)
        H = 16
        HD = C // H
        R = 16
        LORA_SCALE = 32.0 / R
        ATTN_SCALE = HD ** (-0.5)
        key = jax.random.key(seed)
        ks = jax.random.split(key, 10)
        s = lambda fan_in: 1.0 / np.sqrt(fan_in)
        return {'x': jax.random.normal(ks[0], (B, N, C), dtype=jnp.float32), 'w_qkv': jax.random.normal(ks[1], (C, 3 * C), dtype=jnp.float32) * s(C), 'b_qkv': jax.random.normal(ks[2], (3 * C,), dtype=jnp.float32) * 0.02, 'a_q': jax.random.normal(ks[3], (HD, R), dtype=jnp.float32) * s(HD), 'b_q': jax.random.normal(ks[4], (R, HD), dtype=jnp.float32) * 0.02, 'a_v': jax.random.normal(ks[5], (HD, R), dtype=jnp.float32) * s(HD), 'b_v': jax.random.normal(ks[6], (R, HD), dtype=jnp.float32) * 0.02, 'w_proj': jax.random.normal(ks[7], (C, C), dtype=jnp.float32) * s(C), 'b_proj': jax.random.normal(ks[8], (C,), dtype=jnp.float32) * 0.02}
    _L1_attn_all = _L1_attn_setup()
    _L1_attn_in = {k: v for k, v in _L1_attn_all.items() if k in ('w_qkv', 'b_qkv', 'a_q', 'b_q', 'a_v', 'b_v', 'w_proj', 'b_proj')}
    del _L1_attn_all

    def _L1_xattn_setup():
        import jax, jax.numpy as jnp
        import numpy as np
        D_MODEL = 128
        B, S = (4, 256)
        key = jax.random.key(seed)
        ks = jax.random.split(key, 10)
        s = 1.0 / np.sqrt(D_MODEL)
        return {'k': jax.random.normal(ks[0], (B, S, D_MODEL), jnp.float32), 'v': jax.random.normal(ks[1], (B, S, D_MODEL), jnp.float32), 'q': jax.random.normal(ks[2], (B, S, D_MODEL), jnp.float32), 'Wk': jax.random.normal(ks[3], (D_MODEL, D_MODEL), jnp.float32) * s, 'Wv': jax.random.normal(ks[4], (D_MODEL, D_MODEL), jnp.float32) * s, 'bv': jnp.zeros((D_MODEL,), jnp.float32), 'Wq': jax.random.normal(ks[5], (D_MODEL, D_MODEL), jnp.float32) * s, 'bq': jnp.zeros((D_MODEL,), jnp.float32), 'Wo': jax.random.normal(ks[6], (D_MODEL, D_MODEL), jnp.float32) * s, 'bo': jnp.zeros((D_MODEL,), jnp.float32)}
    _L1_xattn_all = _L1_xattn_setup()
    _L1_xattn_in = {k: v for k, v in _L1_xattn_all.items() if k in ('Wk', 'Wv', 'bv', 'Wq', 'bq', 'Wo', 'bo')}
    del _L1_xattn_all

    def _L1_ffn_setup():
        import jax, jax.numpy as jnp
        import numpy as np
        B, S, H, DFF, E, K = (2, 256, 128, 256, 8, 2)

        def _moe(x, Wg, W1, b1, W2, b2, W3, b3):
            Bm, Sm, Hm = x.shape
            xt = x.reshape(-1, Hm)
            gout = xt @ Wg.T
            topv, topi = jax.lax.top_k(gout, K)
            w = jax.nn.softmax(topv, axis=-1)
            comb = jnp.einsum('tke,tk->te', jax.nn.one_hot(topi, E, dtype=x.dtype), w)
            g = jnp.einsum('th,efh->etf', xt, W1) + b1[:, None, :]
            v = jnp.einsum('th,efh->etf', xt, W2) + b2[:, None, :]
            h = jax.nn.silu(g) * v
            eo = jnp.einsum('etf,ehf->eth', h, W3) + b3[:, None, :]
            out = jnp.einsum('eth,te->th', eo, comb)
            return out.reshape(Bm, Sm, Hm)
        key = jax.random.key(seed)
        ks = jax.random.split(key, 8)
        sc_h = 1.0 / np.sqrt(H)
        sc_f = 1.0 / np.sqrt(DFF)
        x = jax.random.normal(ks[0], (B, S, H), dtype=jnp.float32)
        Wg = jax.random.uniform(ks[1], (E, H), jnp.float32, -sc_h, sc_h)
        W1 = jax.random.uniform(ks[2], (E, DFF, H), jnp.float32, -sc_h, sc_h)
        b1 = jax.random.uniform(ks[3], (E, DFF), jnp.float32, -sc_h, sc_h)
        W2 = jax.random.uniform(ks[4], (E, DFF, H), jnp.float32, -sc_h, sc_h)
        b2 = jax.random.uniform(ks[5], (E, DFF), jnp.float32, -sc_h, sc_h)
        W3 = jax.random.uniform(ks[6], (E, H, DFF), jnp.float32, -sc_f, sc_f)
        b3 = jax.random.uniform(ks[7], (E, H), jnp.float32, -sc_f, sc_f)
        return {'x': x, 'Wg': Wg, 'W1': W1, 'b1': b1, 'W2': W2, 'b2': b2, 'W3': W3, 'b3': b3}
    _L1_ffn_all = _L1_ffn_setup()
    _L1_ffn_in = {k: v for k, v in _L1_ffn_all.items() if k in ('Wg', 'W1', 'b1', 'W2', 'b2', 'W3', 'b3')}
    del _L1_ffn_all
    return {'x': x, 'ctx_1024': ctx_1024, 'L0_attn_W_in': _L0_attn_in['W_in'], 'L0_attn_W_conv': _L0_attn_in['W_conv'], 'L0_attn_W_xproj': _L0_attn_in['W_xproj'], 'L0_attn_W_dt': _L0_attn_in['W_dt'], 'L0_attn_b_dt': _L0_attn_in['b_dt'], 'L0_attn_A_log': _L0_attn_in['A_log'], 'L0_attn_D': _L0_attn_in['D'], 'L0_attn_W_out': _L0_attn_in['W_out'], 'L0_xattn_w_q': _L0_xattn_in['w_q'], 'L0_xattn_w_kv': _L0_xattn_in['w_kv'], 'L0_xattn_w_concat': _L0_xattn_in['w_concat'], 'L0_ffn_sW1': _L0_ffn_in['sW1'], 'L0_ffn_sb1': _L0_ffn_in['sb1'], 'L0_ffn_sW2': _L0_ffn_in['sW2'], 'L0_ffn_sb2': _L0_ffn_in['sb2'], 'L0_ffn_rW1': _L0_ffn_in['rW1'], 'L0_ffn_rb1': _L0_ffn_in['rb1'], 'L0_ffn_rW2': _L0_ffn_in['rW2'], 'L0_ffn_rb2': _L0_ffn_in['rb2'], 'L0_ffn_gW': _L0_ffn_in['gW'], 'L0_ffn_gb': _L0_ffn_in['gb'], 'L1_attn_w_qkv': _L1_attn_in['w_qkv'], 'L1_attn_b_qkv': _L1_attn_in['b_qkv'], 'L1_attn_a_q': _L1_attn_in['a_q'], 'L1_attn_b_q': _L1_attn_in['b_q'], 'L1_attn_a_v': _L1_attn_in['a_v'], 'L1_attn_b_v': _L1_attn_in['b_v'], 'L1_attn_w_proj': _L1_attn_in['w_proj'], 'L1_attn_b_proj': _L1_attn_in['b_proj'], 'L1_xattn_Wk': _L1_xattn_in['Wk'], 'L1_xattn_Wv': _L1_xattn_in['Wv'], 'L1_xattn_bv': _L1_xattn_in['bv'], 'L1_xattn_Wq': _L1_xattn_in['Wq'], 'L1_xattn_bq': _L1_xattn_in['bq'], 'L1_xattn_Wo': _L1_xattn_in['Wo'], 'L1_xattn_bo': _L1_xattn_in['bo'], 'L1_ffn_Wg': _L1_ffn_in['Wg'], 'L1_ffn_W1': _L1_ffn_in['W1'], 'L1_ffn_b1': _L1_ffn_in['b1'], 'L1_ffn_W2': _L1_ffn_in['W2'], 'L1_ffn_b2': _L1_ffn_in['b2'], 'L1_ffn_W3': _L1_ffn_in['W3'], 'L1_ffn_b3': _L1_ffn_in['b3']}

def reference(x, ctx_1024, L0_attn_W_in, L0_attn_W_conv, L0_attn_W_xproj, L0_attn_W_dt, L0_attn_b_dt, L0_attn_A_log, L0_attn_D, L0_attn_W_out, L0_xattn_w_q, L0_xattn_w_kv, L0_xattn_w_concat, L0_ffn_sW1, L0_ffn_sb1, L0_ffn_sW2, L0_ffn_sb2, L0_ffn_rW1, L0_ffn_rb1, L0_ffn_rW2, L0_ffn_rb2, L0_ffn_gW, L0_ffn_gb, L1_attn_w_qkv, L1_attn_b_qkv, L1_attn_a_q, L1_attn_b_q, L1_attn_a_v, L1_attn_b_v, L1_attn_w_proj, L1_attn_b_proj, L1_xattn_Wk, L1_xattn_Wv, L1_xattn_bv, L1_xattn_Wq, L1_xattn_bq, L1_xattn_Wo, L1_xattn_bo, L1_ffn_Wg, L1_ffn_W1, L1_ffn_b1, L1_ffn_W2, L1_ffn_b2, L1_ffn_W3, L1_ffn_b3):
    import jax
    import jax.numpy as jnp

    def _L0_attn_ref(x, W_in, W_conv, W_xproj, W_dt, b_dt, A_log, D, W_out):
        import jax, jax.numpy as jnp
        import numpy as np
        from jax import lax
        D_MODEL = 128
        D_STATE = 16
        D_CONV = 4
        EXPAND = 2
        D_INNER = EXPAND * D_MODEL
        DT_RANK = (D_MODEL + 15) // 16
        BATCH, LENGTH = (2, 128)
        DT_MIN, DT_MAX = (0.001, 0.1)

        def silu(v):
            return v * jax.nn.sigmoid(v)
        xz = x @ W_in.T
        xc, z = jnp.split(xz, 2, axis=-1)
        xc = lax.conv_general_dilated(xc.transpose(0, 2, 1), W_conv, window_strides=(1,), padding=[(D_CONV - 1, 0)], feature_group_count=D_INNER, dimension_numbers=('NCH', 'OIH', 'NCH')).transpose(0, 2, 1)
        xc = silu(xc)
        dbc = xc @ W_xproj.T
        dlt = dbc[..., :DT_RANK]
        Bm = dbc[..., DT_RANK:DT_RANK + D_STATE]
        Cm = dbc[..., DT_RANK + D_STATE:]
        delta = jax.nn.softplus(dlt @ W_dt.T + b_dt)
        A = -jnp.exp(A_log)
        deltaA = jnp.exp(delta[..., None] * A)
        deltaBx = delta[..., None] * Bm[:, :, None, :] * xc[..., None]

        def step(h, inp):
            dA, dBx, c = inp
            h = dA * h + dBx
            return (h, jnp.einsum('bdn,bn->bd', h, c))
        h0 = jnp.zeros((x.shape[0], D_INNER, D_STATE), xc.dtype)
        _, ys = lax.scan(step, h0, (deltaA.swapaxes(0, 1), deltaBx.swapaxes(0, 1), Cm.swapaxes(0, 1)))
        y = ys.swapaxes(0, 1) + xc * D
        y = y * silu(z)
        return y @ W_out.T

    def _L0_xattn_ref(q, kv, mem, w_q, w_kv, w_concat):
        import jax, jax.numpy as jnp
        import numpy as np
        D_MODEL = 128
        N_HEAD = 16
        D_HEAD = D_MODEL // N_HEAD
        B, L, D = q.shape
        c = jnp.concatenate([mem, kv], axis=1)
        qh = (q @ w_q).reshape(B, L, N_HEAD, D_HEAD).transpose(0, 2, 1, 3)
        kvp = c @ w_kv
        k, v = (kvp[..., :D_HEAD], kvp[..., D_HEAD:])
        attn_score = jnp.einsum('bhid,bjd->bhij', qh, k) / np.sqrt(D_HEAD)
        attn_prob = jax.nn.softmax(attn_score, axis=-1)
        out = jnp.einsum('bhij,bjd->bhid', attn_prob, v)
        out = out.transpose(0, 2, 1, 3).reshape(B, L, D)
        return out @ w_concat

    def _L0_ffn_ref(x, sW1, sb1, sW2, sb2, rW1, rb1, rW2, rb2, gW, gb):
        import jax, jax.numpy as jnp
        import numpy as np
        D_MODEL = 128
        D_FF = 512
        NUM_M = 2
        E_ROUTER = 8 * NUM_M - 1
        D_FF_R = D_FF // NUM_M
        TOP_K = NUM_M * 2 - 1
        B, T = (2, 256)

        def _expert_stack(x, W1, b1, W2, b2):
            h = jax.nn.gelu(jnp.einsum('btd,edf->ebtf', x, W1) + b1[:, None, None, :], approximate=False)
            return jnp.einsum('ebtf,efd->ebtd', h, W2) + b2[:, None, None, :]
        shared_enc = _expert_stack(x, sW1, sb1, sW2, sb2).sum(0)
        weights = jax.nn.softmax(x @ gW + gb, axis=-1)
        topv, topi = jax.lax.top_k(weights, TOP_K)
        gated = (jax.nn.one_hot(topi, E_ROUTER, dtype=weights.dtype) * topv[..., None]).sum(axis=-2)
        router_out = _expert_stack(x, rW1, rb1, rW2, rb2)
        router_enc = jnp.einsum('ebtd,bte->btd', router_out, gated)
        return shared_enc + router_enc + x

    def _L1_attn_ref(x, w_qkv, b_qkv, a_q, b_q, a_v, b_v, w_proj, b_proj):
        import jax, jax.numpy as jnp
        import numpy as np
        B, N, C = (2, 256, 128)
        H = 16
        HD = C // H
        R = 16
        LORA_SCALE = 32.0 / R
        ATTN_SCALE = HD ** (-0.5)
        Bb, Nn, Cc = x.shape
        qkv = (x @ w_qkv + b_qkv).reshape(Bb, Nn, 3, H, HD).transpose(2, 0, 3, 1, 4)
        q, k, v = (qkv[0], qkv[1], qkv[2])
        q = q + jnp.einsum('bhnr,rd->bhnd', jnp.einsum('bhnd,dr->bhnr', q, a_q), b_q) * LORA_SCALE
        v = v + jnp.einsum('bhnr,rd->bhnd', jnp.einsum('bhnd,dr->bhnr', v, a_v), b_v) * LORA_SCALE
        attn = jax.nn.softmax(jnp.einsum('bhnd,bhmd->bhnm', q, k) * ATTN_SCALE, axis=-1)
        out = jnp.einsum('bhnm,bhmd->bhnd', attn, v)
        out = out.transpose(0, 2, 1, 3).reshape(Bb, Nn, Cc)
        return out @ w_proj + b_proj

    def _L1_xattn_ref(k, v, q, Wk, Wv, bv, Wq, bq, Wo, bo):
        import jax, jax.numpy as jnp
        import numpy as np
        D_MODEL = 128
        B, S = (4, 256)
        kp = jnp.einsum('bsd,ed->bse', k, Wk)
        vp = jnp.einsum('bsd,ed->bse', v, Wv) + bv
        qp = jnp.einsum('bsd,ed->bse', q, Wq) + bq
        scale = 1.0 / jnp.sqrt(jnp.float32(kp.shape[-1]))
        scores = jnp.einsum('bqd,bkd->bqk', qp, kp) * scale
        probs = jax.nn.softmax(scores, axis=-1)
        ctx = jnp.einsum('bqk,bkd->bqd', probs, vp)
        return jnp.einsum('bqd,ed->bqe', ctx, Wo) + bo

    def _L1_ffn_ref(x, Wg, W1, b1, W2, b2, W3, b3):
        import jax, jax.numpy as jnp
        import numpy as np
        B, S, H, DFF, E, K = (2, 256, 128, 256, 8, 2)

        def _moe(x, Wg, W1, b1, W2, b2, W3, b3):
            Bm, Sm, Hm = x.shape
            xt = x.reshape(-1, Hm)
            gout = xt @ Wg.T
            topv, topi = jax.lax.top_k(gout, K)
            w = jax.nn.softmax(topv, axis=-1)
            comb = jnp.einsum('tke,tk->te', jax.nn.one_hot(topi, E, dtype=x.dtype), w)
            g = jnp.einsum('th,efh->etf', xt, W1) + b1[:, None, :]
            v = jnp.einsum('th,efh->etf', xt, W2) + b2[:, None, :]
            h = jax.nn.silu(g) * v
            eo = jnp.einsum('etf,ehf->eth', h, W3) + b3[:, None, :]
            out = jnp.einsum('eth,te->th', eo, comb)
            return out.reshape(Bm, Sm, Hm)
        return _moe(x, Wg, W1, b1, W2, b2, W3, b3)
    x = _layernorm(x + _L0_attn_ref(x, L0_attn_W_in, L0_attn_W_conv, L0_attn_W_xproj, L0_attn_W_dt, L0_attn_b_dt, L0_attn_A_log, L0_attn_D, L0_attn_W_out), axis=-1)
    x = _layernorm(x + _L0_xattn_ref(x, ctx_1024, ctx_1024, L0_xattn_w_q, L0_xattn_w_kv, L0_xattn_w_concat), axis=-1)
    x = _layernorm(x + _L0_ffn_ref(x, L0_ffn_sW1, L0_ffn_sb1, L0_ffn_sW2, L0_ffn_sb2, L0_ffn_rW1, L0_ffn_rb1, L0_ffn_rW2, L0_ffn_rb2, L0_ffn_gW, L0_ffn_gb), axis=-1)
    x = _layernorm(x + _L1_attn_ref(x, L1_attn_w_qkv, L1_attn_b_qkv, L1_attn_a_q, L1_attn_b_q, L1_attn_a_v, L1_attn_b_v, L1_attn_w_proj, L1_attn_b_proj), axis=-1)
    x = _layernorm(x + _L1_xattn_ref(ctx_1024, ctx_1024, x, L1_xattn_Wk, L1_xattn_Wv, L1_xattn_bv, L1_xattn_Wq, L1_xattn_bq, L1_xattn_Wo, L1_xattn_bo), axis=-1)
    x = _layernorm(x + _L1_ffn_ref(x, L1_ffn_Wg, L1_ffn_W1, L1_ffn_b1, L1_ffn_W2, L1_ffn_b2, L1_ffn_W3, L1_ffn_b3), axis=-1)
    return x

_drawn_inputs = setup_inputs


def setup_inputs(seed=0):
    import zlib

    import numpy as np

    out = dict(_drawn_inputs(seed))
    spreads = {'L0_attn_b_dt': (-0.8577413558959961, 0.56),
     'L0_attn_D': (1.0, 0.2),
     'L1_xattn_bv': (0.0, 0.1),
     'L1_xattn_bq': (0.0, 0.272),
     'L1_xattn_bo': (0.0, 0.1)}
    factors = {'L0_ffn_sb1': 4.828,
     'L0_ffn_sb2': 3.374,
     'L0_ffn_rW1': 2.732,
     'L0_ffn_rb1': 8.0,
     'L0_ffn_rb2': 8.0,
     'L0_ffn_gW': 2.72,
     'L0_ffn_gb': 8.0,
     'L1_attn_b_qkv': 2.94,
     'L1_attn_a_q': 4.084,
     'L1_attn_b_q': 3.427,
     'L1_attn_b_proj': 2.971,
     'L1_ffn_b1': 8.0,
     'L1_ffn_b2': 8.0}
    for name, (base, spread) in spreads.items():
        noise = np.random.default_rng([zlib.crc32(name.encode()), seed]).standard_normal(out[name].shape)
        drawn = base * np.exp(spread * noise) if base else spread * noise
        out[name] = jnp.asarray(drawn.astype(out[name].dtype))
    for name, factor in factors.items():
        out[name] = (out[name] * factor).astype(out[name].dtype)
    return out
```

```python
from contextlib import ExitStack

import concourse.bass as bass
from concourse import mybir

F32 = mybir.dt.float32
BF16 = mybir.dt.bfloat16
ALU = mybir.AluOpType
ACT = mybir.ActivationFunctionType
AX = mybir.AxisListType

P = 128
D = 128
T = 1024
NT = T // P
HALF = 512
H = 16
HD = D // H
CTX = 6404
NCH = -(-CTX // P)
TAIL = CTX - (NCH - 1) * P
EPS = 1e-5

AUG = P
SHIFT = 4 * HD
Q_PARTS = (0, 0, 0, 1, 1, 2, 1, 2, 2)
K_PARTS = (0, 1, 2, 0, 1, 0, 2, 1, 2)
USED = len(Q_PARTS) * HD + 3


def slot(s):
    return HD * s if s < 4 else HD * s + 3


class Chain:

    def __init__(self, eng, sem):
        self.eng, self.sem, self.n = eng, sem, 0

    def __call__(self, ins):
        self.n += 1
        ins.then_inc(self.sem, 1)
        self.eng.wait_ge(self.sem, self.n)


class Core:

    def __init__(self, nc, dram, ctx):
        self.nc, self.dram, self.ctx = nc, dram, ctx
        self.norms = 0


    def sb(self, name, shape, dt=F32, ctx=None):
        return (ctx or self.ctx).enter_context(self.nc.sbuf_tensor("sb_" + name, shape, dt))

    def ps(self, name, shape, ctx, dt=F32):
        return ctx.enter_context(self.nc.psum_tensor("ps_" + name, shape, dt))

    def sem(self, name):
        return self.ctx.enter_context(self.nc.semaphore(name))

    def chain(self, dve):
        self.steps.eng = dve
        return self.steps


def load_and_constants(k):
    nc, d = k.nc, k.dram
    k.x_tok = k.sb("x_tok", [P, NT, D])
    k.x_T = k.sb("x_T", [P, T])
    k.ident = k.sb("ident", [P, P])
    k.ident_b = k.sb("ident_b", [P, P], BF16)
    k.ones_b = k.sb("ones_b", [P, P], BF16)
    k.steps = Chain(None, k.sem("vector_step"))
    k.var_ready, k.sd_ready = k.sem("norm_var_ready"), k.sem("norm_sd_ready")
    k.tile_ready, k.turned_ready = k.sem("norm_tile_ready"), k.sem("norm_turned_ready")
    k.consts_ready = k.sem("consts_ready")
    k.ident_zeroed = k.sem("ident_zeroed")
    k.ident_ready = k.sem("ident_ready")

    with nc.Block() as block:
        @block.gpsimd
        def _(pool):
            nc.gpsimd.memset(k.ident[:], 0.0).then_inc(k.ident_zeroed, 1)
            pool.wait_ge(k.ident_zeroed, 1)
            nc.gpsimd.affine_select(out=k.ident[:], in_=k.ident[:], compare_op=ALU.not_equal, fill=1.0, base=0,
                                    pattern=[[-1, P]], channel_multiplier=1).then_inc(k.ident_ready, 1)

        @block.vector
        def _(dve):
            nc.vector.memset(k.ones_b[:], 1.0)
            dve.wait_ge(k.ident_ready, 1)
            nc.vector.tensor_copy(k.ident_b[:], k.ident[:]).then_inc(k.consts_ready, 1)


def residual_norm(k, tag, branch, bias=None, store=None):
    nc = k.nc
    with ExitStack() as tmp:
        res = k.sb(tag + "_res", [P, NT, D], F32, tmp)
        stats = k.sb(tag + "_stats", [P, NT, 6], F32, tmp)
        mv = k.sb(tag + "_mv", [P, NT, 2], F32, tmp)
        var = k.sb(tag + "_var", [P, NT], F32, tmp)
        sd = k.sb(tag + "_sd", [P, NT], F32, tmp)
        rstd = k.sb(tag + "_rstd", [P, NT], F32, tmp)
        turned = k.ps(tag + "_turned", [P, T], tmp)
        stored = k.sem("stored") if store is not None else None
        n = k.norms
        k.norms += 1

        with nc.Block() as block:
            @block.vector
            def _(dve):
                link = k.chain(dve)
                for h in range(0, NT, 4):
                    ins = nc.vector.tensor_tensor(res[:, h:h + 4, :], branch[:, h:h + 4, :], k.x_tok[:, h:h + 4, :],
                                                  ALU.add)
                    if bias is None:
                        link(ins)
                    else:
                        link(ins)
                        link(nc.vector.tensor_tensor(res[:, h:h + 4, :], res[:, h:h + 4, :],
                                                     bias[:].unsqueeze(1).to_broadcast([P, 4, D]), ALU.add))
                for t in range(NT):
                    ins = nc.vector.bn_stats(stats[:, t, :], res[:, t, :])
                link(ins)
                for t in range(NT):
                    ins = nc.vector.bn_aggr(mv[:, t, :], stats[:, t, :])
                link(ins)
                nc.vector.tensor_scalar(var[:], mv[:, :, 1], EPS, None, ALU.add).then_inc(k.var_ready, 1)
                dve.wait_ge(k.sd_ready, n + 1)
                link(nc.vector.reciprocal(rstd[:], sd[:]))
                for t in range(NT):
                    nc.vector.tensor_scalar(k.x_tok[:, t, :], res[:, t, :], mv[:, t, 0:1], rstd[:, t:t + 1],
                                            ALU.subtract, ALU.mult).then_inc(k.tile_ready, 1)

            @block.scalar
            def _(act):
                act.wait_ge(k.var_ready, n + 1)
                nc.scalar.activation(sd[:], var[:], ACT.Sqrt).then_inc(k.sd_ready, 1)
                if store is None:
                    for h in range(2):
                        act.wait_ge(k.turned_ready, 2 * n + h + 1)
                        nc.scalar.copy(k.x_T[:, h * HALF:(h + 1) * HALF], turned[:, h * HALF:(h + 1) * HALF])

            @block.tensor
            def _(pe):
                if store is None:
                    for t in range(NT):
                        pe.wait_ge(k.tile_ready, NT * n + t + 1)
                        ins = nc.tensor.transpose(turned[:, t * P:(t + 1) * P], k.x_tok[:, t, :], k.ident[:])
                        if t % 4 == 3:
                            ins.then_inc(k.turned_ready, 1)

            @block.sync
            def _(sp):
                if store is not None:
                    for h in range(2):
                        sp.wait_ge(k.tile_ready, NT * n + 4 * h + 4)
                        sp.dma_start(store[:, 4 * h:4 * h + 4, :], k.x_tok[:, 4 * h:4 * h + 4, :]).then_inc(stored, 16)
                    sp.wait_ge(stored, 32)


def context_projections(k):
    nc, d = k.nc, k.dram
    k.key1_T = k.sb("key1_T", [P, CTX])
    k.val1 = k.sb("val1", [P, NCH, D])
    k.wk1 = k.sb("wk1", [P, D])
    k.wv1 = k.sb("wv1", [P, D])
    k.layer0 = k.ctx.enter_context(ExitStack())
    k.ctx_T = k.sb("ctx_T", [P, CTX], F32, k.layer0)
    k.key_stack = k.sb("key_stack", [AUG, CTX], BF16, k.layer0)
    k.val_ones = k.sb("val_ones", [P, NCH, 32], F32, k.layer0)
    k.x_loaded, k.layer1_loaded = k.sem("x_loaded"), k.sem("layer1_loaded")

    ctx = ExitStack()
    with ctx:
        w_kv = k.sb("w_kv", [P, 2 * HD], F32, ctx)
        k_tok = k.sb("k_tok", [P, NCH, HD], F32, ctx)
        part = [k.sb(f"k_part{i}", [P, NCH, HD], BF16, ctx) for i in range(3)]
        rest = [k.sb(f"k_rest{i}", [P, NCH, HD], F32, ctx) for i in range(2)]
        stack_tok = k.sb("k_stack_tok", [P, NCH, AUG], BF16, ctx)
        kv_ps = k.ps("kv_ps", [P, 64, 2 * HD], ctx)
        turn_ps = k.ps("k_turn_ps", [P, 4, 2 * HALF], ctx, BF16)

        kv_loaded = k.sem("w_kv_loaded")
        ctx_loaded = [k.sem(f"ctx_loaded{i}") for i in range(2)]
        kv_ready, stack_zeroed, stack_ready = k.sem("kv_ready"), k.sem("k_stack_zeroed"), k.sem("k_stack_ready")
        turned, used_dve, used_act = k.sem("k_turned"), k.sem("k_turn_used_dve"), k.sem("k_turn_used_act")
        TURNS = -(-NCH // 8)
        CUT = 26 * P

        def copy_turned(eng, copy, g, used):
            cols = min(8 * P, CTX - g * 8 * P)
            eng.wait_ge(turned, g + 1)
            copy(k.key_stack[:, g * 8 * P:g * 8 * P + cols], turn_ps[0:AUG, g % 4, 0:cols]).then_inc(used, 1)

        with nc.Block() as block:
            @block.sync
            def _(sp):
                sp.dma_start(w_kv[:], d["L0_xattn_w_kv"]).then_inc(kv_loaded, 16)
                sp.dma_start(k.ctx_T[:, 0:CUT], d["ctx_T"][:, 0:CUT]).then_inc(ctx_loaded[0], 16)
                sp.dma_start(k.x_T[:], d["x_T"]).then_inc(k.x_loaded, 16)
                sp.dma_start(k.wv1[:], d["L1_xattn_Wv_T"]).then_inc(k.layer1_loaded, 16)

            @block.scalar
            def _(act):
                act.dma_start(k.ctx_T[:, CUT:CTX], d["ctx_T"][:, CUT:CTX]).then_inc(ctx_loaded[1], 16)
                act.dma_start(k.x_tok[:], d["x"].rearrange("b (t p) d -> p (b t) d", p=P)).then_inc(k.x_loaded, 16)
                act.dma_start(k.wk1[:], d["L1_xattn_Wk_T"]).then_inc(k.layer1_loaded, 16)
                for g in range(1, TURNS, 2):
                    copy_turned(act, nc.scalar.copy, g, used_act)

            @block.tensor
            def _(pe):
                pe.wait_ge(kv_loaded, 16)
                for c in range(NCH):
                    if c in (0, CUT // P):
                        pe.wait_ge(ctx_loaded[1 if c else 0], 16)
                    n = P if c < NCH - 1 else TAIL
                    ins = nc.tensor.matmul(kv_ps[0:n, c, :], k.ctx_T[:, c * P:c * P + n], w_kv[:], start=True, stop=True)
                ins.then_inc(kv_ready, 1)
                pe.wait_ge(stack_ready, 1)
                for c in range(NCH):
                    n = P if c < NCH - 1 else TAIL
                    g = c // 8
                    if c % 8 == 0 and g >= 4:
                        pe.wait_ge(used_act if g % 2 else used_dve, (g - 4) // 2 + 1)
                    ins = nc.tensor.transpose(turn_ps[0:AUG, g % 4, (c % 8) * P:(c % 8) * P + n],
                                              stack_tok[0:n, c, :], k.ident_b[0:n, 0:n])
                    if c % 8 == 7 or c == NCH - 1:
                        ins.then_inc(turned, 1)

            @block.gpsimd
            def _(pool):
                nc.gpsimd.memset(stack_tok[:, :, SHIFT:SHIFT + 3], 1.0)
                nc.gpsimd.memset(stack_tok[:, :, USED:AUG], 0.0).then_inc(stack_zeroed, 1)

            @block.vector
            def _(dve):
                link = k.chain(dve)
                full = NCH - 1
                nc.vector.memset(k_tok[:, full, :], 0.0)
                link(nc.vector.memset(k.val_ones[:], 0.0))
                nc.vector.memset(k.val_ones[:, 0:full, HD:HD + 1], 1.0)
                link(nc.vector.memset(k.val_ones[0:TAIL, full, HD:HD + 1], 1.0))
                dve.wait_ge(kv_ready, 1)
                nc.vector.tensor_copy(k_tok[:, 0:full, :], kv_ps[:, 0:full, 0:HD])
                link(nc.vector.tensor_copy(k_tok[0:TAIL, full, :], kv_ps[0:TAIL, full, 0:HD]))
                split(nc, link, k_tok[:], [p[:] for p in part], [r[:] for r in rest])
                dve.wait_ge(stack_zeroed, 1)
                for s, which in enumerate(K_PARTS):
                    ins = nc.vector.tensor_copy(stack_tok[:, :, slot(s):slot(s) + HD], part[which][:])
                ins.then_inc(stack_ready, 1)
                nc.vector.tensor_copy(k.val_ones[:, 0:full, 0:HD], kv_ps[:, 0:full, HD:2 * HD])
                nc.vector.tensor_copy(k.val_ones[0:TAIL, full, 0:HD], kv_ps[0:TAIL, full, HD:2 * HD])
                for g in range(0, TURNS, 2):
                    copy_turned(dve, nc.vector.tensor_copy, g, used_dve)


def split(nc, link, whole, part, rest):
    link(nc.vector.tensor_copy(part[0], whole))
    link(nc.vector.tensor_tensor(rest[0], whole, part[0], ALU.subtract))
    link(nc.vector.tensor_copy(part[1], rest[0]))
    link(nc.vector.tensor_tensor(rest[1], rest[0], part[1], ALU.subtract))
    link(nc.vector.tensor_copy(part[2], rest[1]))


def mamba(k):
    nc, d = k.nc, k.dram
    DI, NS, DR, KC = 2 * D, 16, D // 16, 4
    ROWS = DR + 2 * NS
    ctx = ExitStack()
    with ctx:
        w_in = k.sb("w_in_T", [P, 2 * DI], F32, ctx)
        w_conv = k.sb("w_conv", [P, 2, KC], F32, ctx)
        w_x = k.sb("w_xproj_T", [P, 2, ROWS], F32, ctx)
        w_dt = k.sb("w_dt_T", [DR, DI], F32, ctx)
        b_dt = k.sb("b_dt", [P, 2], F32, ctx)
        a_log = k.sb("a_log", [P, 2, NS], F32, ctx)
        a_neg = k.sb("a_neg", [P, 2, NS], F32, ctx)
        d_skip = k.sb("d_skip", [P, 2], F32, ctx)
        w_out = k.sb("w_out_T", [P, 2, D], F32, ctx)
        diag = k.sb("d_diag", [P, 2, P], F32, ctx)
        PAD = KC - 1
        xpad = k.sb("xpad", [P, 2, PAD + T], F32, ctx)
        zs = k.sb("z_silu", [P, 2, T], F32, ctx)
        conv = k.sb("conv", [P, 2, T], F32, ctx)
        xc = k.sb("xc", [P, 2, T], F32, ctx)
        delta = k.sb("delta", [P, 2, T], F32, ctx)
        u = k.sb("u", [P, 2, T], F32, ctx)
        dbc_all = k.sb("dbc", [P, T], F32, ctx)
        dbc = dbc_all[0:ROWS, :]
        bc_rows = k.sb("bc_rows", [P, NS, T], BF16, ctx)
        pick = k.sb("bc_pick", [P, 2, P], BF16, ctx)
        early = k.val1[:].rearrange("p c e -> p (c e)")
        decay = early[:, 0:2 * T].rearrange("p (s t) -> p s t", s=2)
        c_all = early[:, 2 * T:4 * T].rearrange("p (s t) -> p s t", s=2)
        state = k.sb("state", [P, 2, T], F32, ctx)
        dbc_part = [state[0:ROWS, i // 2, (i % 2) * HALF:(i % 2 + 1) * HALF].bitcast(BF16) for i in range(3)]
        dbc_rest = [decay[0:ROWS, i, :] for i in range(2)]
        read = xpad[:, :, 0:T]
        soft = drive = conv

        loaded = k.sem("mamba_loaded")
        xz_ready, xpad_ready, conv_ready = k.sem("xz_ready"), k.sem("xpad_ready"), k.sem("conv_ready")
        xc_ready, z_used, dbc_ready, dbc_copied = k.sem("xc_ready"), k.sem("z_used"), k.sem("dbc_ready"), k.sem("dbc_copied")
        dbc_split, dlt_ready, log_ready = k.sem("dbc_split"), k.sem("dlt_ready"), k.sem("log_ready")
        act_step, a_exp = k.sem("mamba_act_step"), k.sem("a_exp")
        rows_moved, pick_set, rows_zeroed = k.sem("rows_moved"), k.sem("pick_set"), k.sem("bc_rows_zeroed")
        b_ready, c_ready, b_used, c_copied = k.sem("b_ready"), k.sem("c_ready"), k.sem("b_used"), k.sem("c_copied")
        decay_ready, read_ready, y_added = k.sem("decay_ready"), k.sem("read_ready"), k.sem("y_added")
        scanned = k.sem("scanned")
        gated, out_ready = k.sem("y_gated"), k.sem("mamba_out_ready")

        with ExitStack() as front:
            xz = [k.ps(f"xz{c}", [P, T], front) for c in range(4)]
            with nc.Block() as block:
                @block.sync
                def _(sp):
                    sp.dma_start(w_in[:], d["L0_attn_W_in_T"]).then_inc(loaded, 16)
                    sp.dma_start(w_conv[:], d["L0_attn_W_conv"].rearrange("(s p) o k -> p s (o k)", p=P)).then_inc(loaded, 16)
                    sp.dma_start(w_x[:], d["L0_attn_W_xproj_T"].rearrange("(s p) r -> p s r", p=P)).then_inc(loaded, 16)
                    sp.dma_start(w_dt[:], d["L0_attn_W_dt_T"]).then_inc(loaded, 16)
                    sp.dma_start(w_out[:], d["L0_attn_W_out_T"].rearrange("(s p) m -> p s m", p=P)).then_inc(loaded, 16)
                    with nc.allow_non_contiguous_dma(reason="two floats to a partition"):
                        sp.dma_start(b_dt[:], d["L0_attn_b_dt"].rearrange("(s p) -> p s", p=P)).then_inc(loaded, 16)
                        sp.dma_start(d_skip[:], d["L0_attn_D"].rearrange("(s p) -> p s", p=P)).then_inc(loaded, 16)
                    sp.dma_start(a_log[:], d["L0_attn_A_log"].rearrange("(s p) n -> p s n", p=P)).then_inc(loaded, 16)
                    sp.wait_ge(dbc_split, 1)
                    sp.wait_ge(rows_zeroed, 1)
                    for i in range(3):
                        for base, first in ((0, DR), (3, DR + NS)):
                            sp.dma_start(bc_rows[base + i:base + i + 1, :, :],
                                         dbc_part[i][first:first + NS, :]).then_inc(rows_moved, 16)
                    sp.wait_ge(rows_moved, 16 * 6)

                @block.gpsimd
                def _(pool):
                    nc.gpsimd.memset(pick[:], 1.0).then_inc(pick_set, 1)
                    pool.wait_ge(pick_set, 1)
                    nc.gpsimd.affine_select(out=pick[:, 0, :], in_=pick[:, 0, :], compare_op=ALU.is_ge, fill=0.0, base=2,
                                            pattern=[[0, P]], channel_multiplier=-1)
                    nc.gpsimd.affine_select(out=pick[:, 1, :], in_=pick[:, 1, :], compare_op=ALU.is_ge, fill=0.0, base=-3,
                                            pattern=[[0, P]], channel_multiplier=1).then_inc(pick_set, 1)
                    pool.wait_ge(pick_set, 2)
                    nc.gpsimd.affine_select(out=pick[:, 1, :], in_=pick[:, 1, :], compare_op=ALU.is_ge, fill=0.0, base=5,
                                            pattern=[[0, P]], channel_multiplier=-1)
                    nc.gpsimd.memset(bc_rows[:], 0.0).then_inc(rows_zeroed, 1)

                @block.tensor
                def _(pe):
                    pe.wait_ge(loaded, 16 * 8)
                    pe.wait_ge(k.x_loaded, 32)
                    for c in range(4):
                        for h in range(2):
                            ins = nc.tensor.matmul(xz[c][:, h * HALF:(h + 1) * HALF], w_in[:, c * P:(c + 1) * P],
                                                   k.x_T[:, h * HALF:(h + 1) * HALF], start=True, stop=True)
                        ins.then_inc(xz_ready, 1)
                    pe.wait_ge(xpad_ready, 1)
                    pe.wait_ge(xc_ready, 2)
                    for h in range(2):
                        for s in range(2):
                            ins = nc.tensor.matmul(xz[0][0:ROWS, h * HALF:(h + 1) * HALF], w_x[:, s, :],
                                                   xc[:, s, h * HALF:(h + 1) * HALF], start=(s == 0), stop=(s == 1))
                    ins.then_inc(dbc_ready, 1)
                    pe.wait_ge(dbc_copied, 1)
                    pe.wait_ge(z_used, 2)
                    for s in range(2):
                        for h in range(2):
                            ins = nc.tensor.matmul(xz[2 + s][:, h * HALF:(h + 1) * HALF], w_dt[:, s * P:(s + 1) * P],
                                                   dbc[0:DR, h * HALF:(h + 1) * HALF], start=True, stop=True)
                        ins.then_inc(dlt_ready, 1)

                @block.scalar
                def _(act):
                    link = Chain(act, act_step)
                    for s in range(2):
                        act.wait_ge(xz_ready, s + 1)
                        nc.scalar.copy(xpad[:, s, PAD:PAD + T], xz[s][:]).then_inc(xpad_ready, 1)
                    for s in range(2):
                        act.wait_ge(xz_ready, 3 + s)
                        nc.scalar.activation(zs[:, s, :], xz[2 + s][:], ACT.Silu).then_inc(z_used, 1)
                    for s in range(2):
                        act.wait_ge(conv_ready, s + 1)
                        nc.scalar.activation(xc[:, s, :], conv[:, s, :], ACT.Silu).then_inc(xc_ready, 1)
                    act.wait_ge(loaded, 16 * 8)
                    nc.scalar.activation(a_neg[:], a_log[:], ACT.Exp).then_inc(a_exp, 1)
                    for s in range(2):
                        act.wait_ge(dlt_ready, s + 1)
                        link(nc.scalar.activation(soft[:, s, :], xz[2 + s][:], ACT.Abs, bias=b_dt[:, s:s + 1]))
                    for s in range(2):
                        link(nc.scalar.activation(soft[:, s, :], soft[:, s, :], ACT.Exp, scale=-1.0))
                    for s in range(2):
                        nc.scalar.activation(soft[:, s, :], soft[:, s, :], ACT.Ln, bias=1.0).then_inc(log_ready, 1)

                @block.vector
                def _(dve):
                    link = k.chain(dve)
                    link(nc.vector.memset(xpad[:, :, 0:PAD], 0.0))
                    dve.wait_ge(loaded, 16 * 8)
                    dve.wait_ge(k.consts_ready, 1)
                    for s in range(2):
                        nc.vector.tensor_scalar(diag[:, s, :], k.ident[:], d_skip[:, s:s + 1], None, ALU.mult)
                    for s in range(2):
                        dve.wait_ge(xpad_ready, s + 1)
                        link(nc.vector.tensor_scalar(conv[:, s, :], xpad[:, s, 0:T], w_conv[:, s, 0:1], None, ALU.mult))
                        for j in range(1, KC):
                            ins = nc.vector.scalar_tensor_tensor(
                                out=conv[:, s, :], in0=xpad[:, s, j:j + T], scalar=w_conv[:, s, j:j + 1],
                                in1=conv[:, s, :], op0=ALU.mult, op1=ALU.add)
                            if j < KC - 1:
                                link(ins)
                        ins.then_inc(conv_ready, 1)
                    dve.wait_ge(dbc_ready, 1)
                    nc.vector.tensor_copy(dbc[:], xz[0][0:ROWS, :]).then_inc(dbc_copied, 1)
                    dve.wait_ge(dbc_copied, 1)
                    split(nc, link, dbc, dbc_part, dbc_rest)
                    nc.vector.engine_nop().then_inc(dbc_split, 1)
                    dve.wait_ge(a_exp, 1)
                    link(nc.vector.tensor_scalar(a_neg[:], a_neg[:], -1.0, None, ALU.mult))
                    for s in range(2):
                        dve.wait_ge(log_ready, s + 1)
                        link(nc.vector.tensor_scalar(delta[:, s, :], xz[2 + s][:], b_dt[:, s:s + 1], 0.0, ALU.add, ALU.max))
                        link(nc.vector.tensor_tensor(delta[:, s, :], delta[:, s, :], soft[:, s, :], ALU.add))
                        nc.vector.tensor_tensor(u[:, s, :], delta[:, s, :], xc[:, s, :], ALU.mult)

        y = [k.ps(f"y{s}", [P, T], ctx) for s in range(2)]
        b_all = k.ps("b_all", [P, T], ctx)
        out_ps = b_all[:].rearrange("p (t e) -> p t e", t=NT)
        with ExitStack() as mid:
            c_ps = k.ps("c_all", [P, T], mid)

            def spread(pe, dst, which, n, ready):
                for h in range(2):
                    ins = nc.tensor.matmul(dst[:, h * HALF:(h + 1) * HALF], pick[:, which, :],
                                           bc_rows[:, n, h * HALF:(h + 1) * HALF], start=True, stop=True)
                ins.then_inc(ready, 1)

            def next_b(pe, n):
                pe.wait_ge(b_used, 2 * n)
                spread(pe, b_all, 0, n, b_ready)

            def next_c(pe, n):
                pe.wait_ge(c_copied, n)
                spread(pe, c_ps, 1, n, c_ready)

            def add_read(pe, n, s):
                pe.wait_ge(read_ready, 2 * n + s + 1)
                for h in range(2):
                    ins = nc.tensor.matmul(y[s][:, h * HALF:(h + 1) * HALF], k.ident[:],
                                           read[:, s, h * HALF:(h + 1) * HALF], start=False, stop=True,
                                           skip_group_check=True)
                ins.then_inc(y_added, 1)

            def decay_and_c(act, n, parity, first):
                for s in range(2):
                    if not first:
                        act.wait_ge(scanned, 2 * n + s - 1)
                    nc.scalar.activation(decay[:, s, :], delta[:, s, :], ACT.Exp,
                                         scale=a_neg[:, s, bass.ds(n, 1)]).then_inc(decay_ready, 1)
                act.wait_ge(c_ready, n + 1)
                if not (isinstance(n, int) and n < 2):
                    act.wait_ge(read_ready, 2 * n - 2)
                nc.scalar.copy(c_all[:, parity, :], c_ps[:]).then_inc(c_copied, 1)

            def scan(dve, n, first):
                dve.wait_ge(b_ready, n + 1)
                for s in range(2):
                    if not first:
                        dve.wait_ge(scanned, 2 * n + s - 1)
                    nc.vector.tensor_tensor(drive[:, s, :], b_all[:], u[:, s, :], ALU.mult).then_inc(b_used, 1)
                for s in range(2):
                    dve.wait_ge(b_used, 2 * n + s + 1)
                    dve.wait_ge(decay_ready, 2 * n + s + 1)
                    if not first:
                        dve.wait_ge(read_ready, 2 * n + s - 1)
                    nc.vector.tensor_tensor_scan(state[:, s, :], decay[:, s, :], drive[:, s, :], 0.0,
                                                 ALU.mult, ALU.add).then_inc(scanned, 1)

            def read_out(pool, n, parity, first):
                pool.wait_ge(c_copied, n + 1)
                for s in range(2):
                    pool.wait_ge(scanned, 2 * n + s + 1)
                    if not first:
                        pool.wait_ge(y_added, 2 * n + s - 1)
                    nc.gpsimd.tensor_tensor(read[:, s, :], state[:, s, :], c_all[:, parity, :], ALU.mult).then_inc(read_ready, 1)

            with nc.Block() as block:
                @block.tensor
                def _(pe):
                    spread(pe, b_all, 0, 0, b_ready)
                    spread(pe, c_ps, 1, 0, c_ready)
                    for s in range(2):
                        for h in range(2):
                            nc.tensor.matmul(y[s][:, h * HALF:(h + 1) * HALF], diag[:, s, :],
                                             xc[:, s, h * HALF:(h + 1) * HALF], start=True, stop=True,
                                             skip_group_check=True)
                    next_b(pe, 1)
                    next_c(pe, 1)
                    with nc.tensor.Fori(1, NS - 1) as n:
                        add_read(pe, n - 1, 0)
                        next_b(pe, n + 1)
                        add_read(pe, n - 1, 1)
                        next_c(pe, n + 1)
                    for n in (NS - 2, NS - 1):
                        for s in range(2):
                            add_read(pe, n, s)
                    pe.wait_ge(gated, 2)
                    for t in range(NT):
                        for s in range(2):
                            ins = nc.tensor.matmul(out_ps[:, t, :], state[:, s, t * P:(t + 1) * P], w_out[:, s, :],
                                                   start=(s == 0), stop=(s == 1))
                    ins.then_inc(out_ready, 1)

                @block.scalar
                def _(act):
                    nc.scalar.preload_act_table(ACT.Exp)
                    decay_and_c(act, 0, 0, True)
                    decay_and_c(act, 1, 1, False)
                    with nc.scalar.Fori(1, NS // 2) as p:
                        for parity in range(2):
                            decay_and_c(act, 2 * p + parity, parity, False)

                @block.vector
                def _(dve):
                    scan(dve, 0, True)
                    with nc.vector.Fori(1, NS) as n:
                        scan(dve, n, False)
                    for s in range(2):
                        dve.wait_ge(y_added, 2 * NS - 1 + s)
                        nc.vector.tensor_tensor(state[:, s, :], y[s][:], zs[:, s, :], ALU.mult).then_inc(gated, 1)

                @block.gpsimd
                def _(pool):
                    read_out(pool, 0, 0, True)
                    read_out(pool, 1, 1, False)
                    with nc.gpsimd.Fori(1, NS // 2) as p:
                        for parity in range(2):
                            read_out(pool, 2 * p + parity, parity, False)
        residual_norm(k, "norm0", out_ps)


def stack_queries(nc, link, whole, part, rest, stack, parts):
    split(nc, link, whole, part, rest)
    for s, which in enumerate(parts):
        ins = nc.vector.tensor_copy(stack[:, :, slot(s):slot(s) + HD], part[which])
    return ins


def negated_maximum(nc, link, partial, neg, rests, part3):
    link(nc.vector.tensor_reduce(neg, partial, AX.X, ALU.max, negate=True))
    link(nc.vector.tensor_copy(part3[:, :, 0], neg))
    link(nc.vector.tensor_tensor(rests[0], neg, part3[:, :, 0], ALU.subtract))
    link(nc.vector.tensor_copy(part3[:, :, 1], rests[0]))
    link(nc.vector.tensor_tensor(rests[1], rests[0], part3[:, :, 1], ALU.subtract))
    return nc.vector.tensor_copy(part3[:, :, 2], rests[1])


def context_attention(k):
    nc, d = k.nc, k.dram
    BLK = H * P
    JOBS = BLK // HALF
    WIDE = 2 * HALF
    RANGES = [(c0, min(WIDE, CTX - c0)) for c0 in range(0, CTX, WIDE)]
    NR = len(RANGES)
    UNITS = H * NR
    ctx = ExitStack()
    with ctx:
        stack_T = k.sb("q_stack_T", [AUG, NT, BLK], BF16, ctx)
        q_next = k.sb("q_next", [AUG, BLK], BF16, ctx)
        q_now = k.sb("q_now", [AUG, BLK], BF16, ctx)
        gathered = k.sb("gathered", [P, NT, HALF], F32, ctx)
        w_out = k.sb("w_concat", [P, D], F32, ctx)
        with ExitStack() as tmp:
            w_q = k.sb("w_q", [P, D], F32, tmp)
            early = k.val1[:].rearrange("p c e -> p (c e)")
            q_tok, *rest = [early[:, i * T:(i + 1) * T].rearrange("p (a b) -> p a b", b=HD) for i in range(3)]
            part = [k.sb(f"q_part{i}", [P, NT * H, HD], BF16, tmp) for i in range(3)]
            stack = k.sb("q_stack", [P, NT * H, AUG], BF16, tmp)
            q_ps = k.ps("q_ps", [P, NT * D], tmp)
            turn_ps = k.ps("q_turn_ps", [P, 4, 8 * P], tmp, BF16)
            loaded, q_ready = k.sem("wq_loaded"), k.sem("q_ready")
            stack_ready, turned, used_dve, used_act = (k.sem("q_stack_ready"), k.sem("q_turned"),
                                                       k.sem("q_turn_used_dve"), k.sem("q_turn_used_act"))
            with nc.Block() as block:
                @block.sync
                def _(sp):
                    sp.dma_start(w_q[:], d["L0_xattn_w_q"]).then_inc(loaded, 16)
                    sp.dma_start(w_out[:], d["L0_xattn_w_concat"]).then_inc(loaded, 16)

                @block.tensor
                def _(pe):
                    pe.wait_ge(loaded, 32)
                    for t in range(NT):
                        ins = nc.tensor.matmul(q_ps[:, t * D:(t + 1) * D], k.x_T[:, t * P:(t + 1) * P], w_q[:],
                                               start=True, stop=True)
                    ins.then_inc(q_ready, 1)
                    pe.wait_ge(stack_ready, 1)
                    for g in range(NT * H // 8):
                        if g >= 4:
                            pe.wait_ge(used_act if g % 2 else used_dve, (g - 4) // 2 + 1)
                        for j in range(8):
                            ins = nc.tensor.transpose(turn_ps[0:AUG, g % 4, j * P:(j + 1) * P],
                                                      stack[:, g * 8 + j, :], k.ident_b[:])
                        ins.then_inc(turned, 1)

                @block.vector
                def _(dve):
                    link = k.chain(dve)
                    nc.vector.memset(stack[:, :, USED:AUG], 0.0)
                    link(nc.vector.memset(stack[:, :, SHIFT:SHIFT + 3], 0.0))
                    dve.wait_ge(q_ready, 1)
                    link(nc.vector.tensor_scalar(q_tok.rearrange("p a b -> p (a b)"), q_ps[:], float(HD) ** -0.5,
                                                 None, ALU.mult))
                    stack_queries(nc, link, q_tok, [x[:] for x in part], rest, stack,
                                  Q_PARTS).then_inc(stack_ready, 1)
                    for g in range(0, NT * H // 8, 2):
                        dve.wait_ge(turned, g + 1)
                        nc.vector.tensor_copy(stack_T[:, g // 2, 0:8 * P], turn_ps[0:AUG, g % 4, :]).then_inc(used_dve, 1)

                @block.scalar
                def _(act):
                    for g in range(1, NT * H // 8, 2):
                        act.wait_ge(turned, g + 1)
                        nc.scalar.copy(stack_T[:, g // 2, 8 * P:16 * P], turn_ps[0:AUG, g % 4, :]).then_inc(used_act, 1)
                    nc.scalar.preload_act_table(ACT.Exp)

        with ExitStack() as tmp:
            probs = k.sb("probs", [P, 3, JOBS, HALF], F32, tmp)
            partial = k.sb("max_partial", [P, H, NR], F32, tmp)
            neg = k.sb("neg_max", [P, H], F32, tmp)
            rests = [k.sb(f"neg_rest{i}", [P, H], F32, tmp) for i in range(2)]
            part3 = k.sb("neg_part", [P, H, 3], BF16, tmp)
            score_ps = k.ps("score_ps", [P, 3, HALF], tmp)
            max_ps = k.ps("max_ps", [P, 2, WIDE], tmp)
            acc_ps = k.ps("acc_ps", [P, HALF], tmp)
            shift_ps = max_ps[:, 0, :].bitcast(BF16)
            steps_before = k.steps.n
            next_ready, now_ready, rows_ready = k.sem("q_next_ready"), k.sem("q_now_ready"), k.sem("shift_rows_ready")
            unit_ready, unit_used, parts_ready, shift_turned = (k.sem("max_ready"), k.sem("max_used"),
                                                                k.sem("neg_parts_ready"), k.sem("shift_turned"))
            score_ready, exp_done, pv_done, acc_used = (k.sem("score_ready"), k.sem("exp_done"), k.sem("pv_done"),
                                                        k.sem("acc_used"))
            job_ready, job_copied = k.sem("layer1_job_ready"), k.sem("layer1_job_copied")
            EXPS = NCH * JOBS
            LINKED = 5

            def max_unit(pe, blk, u, first):
                h, r = u // NR, u % NR
                if u >= 2 or not first:
                    pe.wait_ge(unit_used, blk * UNITS + u - 1)
                c0, cols = RANGES[r]
                for a in range(0, cols, HALF):
                    n = min(HALF, cols - a)
                    ins = nc.tensor.matmul(max_ps[:, u % 2, a:a + n], q_next[:, h * P:(h + 1) * P],
                                           k.key_stack[:, c0 + a:c0 + a + n], start=True, stop=True)
                ins.then_inc(unit_ready, 1)

            def turn_shift(pe, blk):
                pe.wait_ge(parts_ready, blk + 1)
                for h in range(H):
                    ins = nc.tensor.transpose(shift_ps[0:3, h * P:(h + 1) * P], part3[:, h, :], k.ident_b[:])
                ins.then_inc(shift_turned, 1)

            key_jobs = [(c0, min(HALF, CTX - c0)) for c0 in range(0, CTX, HALF)]
            val_jobs = [(c, min(4, NCH - 1 - c)) for c in range(0, NCH - 1, 4)] + [(NCH - 1, 1)]
            JOBS1 = len(key_jobs) + len(val_jobs)

            def layer1_job(pe, i):
                if i >= 3:
                    pe.wait_ge(job_copied, i - 2)
                bank = score_ps[:, i % 3, :]
                if i < len(key_jobs):
                    c0, cols = key_jobs[i]
                    ins = nc.tensor.matmul(bank[:, 0:cols], k.wk1[:], k.ctx_T[:, c0:c0 + cols], start=True, stop=True)
                else:
                    c, m = val_jobs[i - len(key_jobs)]
                    n = P if c < NCH - 1 else TAIL
                    for j in range(m):
                        ins = nc.tensor.matmul(bank[0:n, j * D:(j + 1) * D], k.ctx_T[:, (c + j) * P:(c + j) * P + n],
                                               k.wv1[:], start=True, stop=True)
                ins.then_inc(job_ready, 1)

            def copy_layer1_job(act, i):
                act.wait_ge(job_ready, i + 1)
                bank = score_ps[:, i % 3, :]
                if i < len(key_jobs):
                    c0, cols = key_jobs[i]
                    ins = nc.scalar.copy(k.key1_T[:, c0:c0 + cols], bank[:, 0:cols])
                else:
                    c, m = val_jobs[i - len(key_jobs)]
                    n = P if c < NCH - 1 else TAIL
                    ins = nc.scalar.copy(k.val1[0:n, c:c + m, :], bank[0:n, 0:m * D].rearrange("p (j e) -> p j e", j=m))
                ins.then_inc(job_copied, 1)

            def attend(pe, blk, with_max):
                pe.wait_ge(now_ready, blk + 1)
                if with_max:
                    pe.wait_ge(next_ready, blk + 2)
                last_max_chunk = NCH - 5
                u = 0
                for c in range(NCH + 1):
                    if c < NCH:
                        n = P if c < NCH - 1 else TAIL
                        for j in range(JOBS):
                            e = c * JOBS + j
                            pe.wait_ge(exp_done, blk * EXPS + max(0, e - 2))
                            nc.tensor.matmul(score_ps[0:n, e % 3, :], k.key_stack[:, c * P:c * P + n],
                                             q_now[:, j * HALF:(j + 1) * HALF], start=True, stop=True).then_inc(score_ready, 1)
                            due = min(UNITS, -(-UNITS * (e + 1) // (last_max_chunk * JOBS))) if with_max else 0
                            while u < due:
                                max_unit(pe, blk + 1, u, False)
                                u += 1
                    if with_max and c == NCH - 2:
                        turn_shift(pe, blk + 1)
                    if c >= 1:
                        v = c - 1
                        if v == 0:
                            pe.wait_ge(acc_used, blk)
                        pe.wait_ge(exp_done, blk * EXPS + JOBS * (v + 1))
                        for j in range(JOBS):
                            ins = nc.tensor.matmul(acc_ps[32 * j:32 * j + 32, :], k.val_ones[:, v, :],
                                                   probs[:, v % 3, j, :], start=(v == 0), stop=(v == NCH - 1))
                        ins.then_inc(pv_done, 1)

            def exponentiate(act, blk):
                for c in range(NCH):
                    n = P if c < NCH - 1 else TAIL
                    act.wait_ge(pv_done, blk * NCH + max(0, c - 2))
                    for j in range(JOBS):
                        e = c * JOBS + j
                        act.wait_ge(score_ready, blk * EXPS + e + 1)
                        nc.scalar.activation(probs[0:n, c % 3, j, :], score_ps[0:n, e % 3, :], ACT.Exp).then_inc(exp_done, 1)
                act.wait_ge(pv_done, (blk + 1) * NCH)
                nc.scalar.copy(gathered[:, at(blk), :], acc_ps[:]).then_inc(acc_used, 1)

            def maxima(dve, blk):
                nc.vector.tensor_copy(q_next[:], stack_T[:, at(blk), :]).then_inc(next_ready, 1)
                for u in range(UNITS):
                    h, r = u // NR, u % NR
                    dve.wait_ge(unit_ready, blk * UNITS + u + 1)
                    nc.vector.tensor_reduce(partial[:, h, r:r + 1], max_ps[:, u % 2, 0:RANGES[r][1]], AX.X,
                                            ALU.max).then_inc(unit_used, 1)
                dve.wait_ge(unit_used, (blk + 1) * UNITS)
                link = k.chain(dve)
                link.n = steps_before + blk * LINKED
                negated_maximum(nc, link, partial[:], neg[:], [x[:] for x in rests], part3[:]).then_inc(parts_ready, 1)
                dve.wait_ge(shift_turned, blk + 1)
                nc.vector.tensor_copy(q_next[SHIFT:SHIFT + 3, :], shift_ps[0:3, :]).then_inc(rows_ready, 1)
                dve.wait_ge(rows_ready, blk + 1)

            def take(dve, blk, first):
                if not first:
                    dve.wait_ge(score_ready, blk * EXPS)
                nc.vector.tensor_copy(q_now[:], q_next[:]).then_inc(now_ready, 1)
                dve.wait_ge(now_ready, blk + 1)

            def at(blk):
                return blk if isinstance(blk, int) else bass.ds(blk, 1)

            with nc.Block() as block:
                @block.tensor
                def _(pe):
                    pe.wait_ge(next_ready, 1)
                    pe.wait_ge(k.layer1_loaded, 32)
                    for u in range(UNITS):
                        max_unit(pe, 0, u, True)
                        for i in range(JOBS1 * u // UNITS, JOBS1 * (u + 1) // UNITS):
                            layer1_job(pe, i)
                    turn_shift(pe, 0)
                    pe.wait_ge(job_copied, JOBS1)
                    with nc.tensor.Fori(0, NT - 1) as i:
                        attend(pe, i, True)
                    attend(pe, NT - 1, False)

                @block.scalar
                def _(act):
                    for i in range(JOBS1):
                        copy_layer1_job(act, i)
                    with nc.scalar.Fori(0, NT) as i:
                        exponentiate(act, i)

                @block.vector
                def _(dve):
                    maxima(dve, 0)
                    take(dve, 0, True)
                    with nc.vector.Fori(0, NT - 1) as i:
                        maxima(dve, i + 1)
                        take(dve, i + 1, False)
                    k.steps.n = steps_before + NT * LINKED

        with ExitStack() as tmp:
            merged = k.sb("merged", [P, NT, D], F32, tmp)
            k.out_ps = k.ps("xattn0_out_ps", [P, NT, D], tmp)
            finish_heads(k, "xattn0", gathered, merged, w_out, k.out_ps, by_tile=True)
            residual_norm(k, "norm1", k.out_ps)
    k.layer0.close()


def finish_heads(k, tag, gathered, merged, w_out, out_ps, by_tile):
    nc = k.nc
    with ExitStack() as tmp:
        turn_ps = k.ps(tag + "_turn_ps", [P, 4, 4, P], tmp)
        recip = k.sb(tag + "_recip", [P, 4, 4, 4], F32, tmp)
        turned, used, recip_ready = k.sem(tag + "_turned"), k.sem(tag + "_turn_used"), k.sem(tag + "_recip")
        per_m = gathered.shape[2] // P
        M = gathered.shape[1]
        GROUPS = M * per_m // 4
        with nc.Block() as block:
            @block.tensor
            def _(pe):
                for g in range(GROUPS):
                    if g >= 4:
                        pe.wait_ge(used, g - 3)
                    for i in range(4):
                        w = g * 4 + i
                        m, s = w // per_m, w % per_m
                        ins = nc.tensor.transpose(turn_ps[:, g % 4, i, :], gathered[:, m, s * P:(s + 1) * P], k.ident[:])
                    ins.then_inc(turned, 1)
            @block.vector
            def _(dve):
                for g in range(GROUPS):
                    dve.wait_ge(turned, g + 1)
                    rows = turn_ps[:, g % 4, :, :].rearrange("p i (q r) -> p i q r", q=4)
                    nc.vector.reciprocal(recip[:, g % 4, :, :], rows[:, :, :, HD]).then_inc(recip_ready, 1)
                    dve.wait_ge(recip_ready, g + 1)
                    for i in range(4):
                        src = turn_ps[:, g % 4, i, :].rearrange("p (q r) -> p q r", q=4)[:, :, 0:HD]
                        w = g * 4 + i
                        m, s = w // per_m, w % per_m
                        if by_tile:
                            dst = merged[:, m, :].rearrange("p (q s e) -> p s q e", q=4, s=4)[:, s, :, :]
                        else:
                            dst = merged[:].rearrange("p (q s) (h e) -> p s h q e", s=2, h=H)[:, s, m, :, :]
                        ins = nc.vector.tensor_tensor(dst, src, recip[:, g % 4, i, :].unsqueeze(2).to_broadcast([P, 4, HD]),
                                                      ALU.mult)
                    ins.then_inc(used, 1)
    project(k, tag, merged, w_out, out_ps)


def project(k, tag, merged, w_out, out_ps):
    nc = k.nc
    with ExitStack() as tmp:
        back_ps = k.ps(tag + "_back_ps", [P, T], tmp)
        merged_T = k.sb(tag + "_merged_T", [P, T], F32, tmp)
        back, back_copied = k.sem(tag + "_back"), k.sem(tag + "_back_copied")
        with nc.Block() as block:
            @block.tensor
            def _(pe):
                for t in range(NT):
                    ins = nc.tensor.transpose(back_ps[:, t * P:(t + 1) * P], merged[:, t, :], k.ident[:])
                    if t % 4 == 3:
                        ins.then_inc(back, 1)
                for t in range(NT):
                    if t % 4 == 0:
                        pe.wait_ge(back_copied, t // 4 + 1)
                    nc.tensor.matmul(out_ps[:, t, :], merged_T[:, t * P:(t + 1) * P], w_out[:], start=True, stop=True)

            @block.scalar
            def _(act):
                for h in range(2):
                    act.wait_ge(back, h + 1)
                    nc.scalar.copy(merged_T[:, h * HALF:(h + 1) * HALF],
                                   back_ps[:, h * HALF:(h + 1) * HALF]).then_inc(back_copied, 1)


def choose(nc, link, values, width, pads, n_top, lowest, top8, wanted, left, chosen):
    mark = 2.0 * lowest
    for t in range(NT):
        ins = nc.vector.max(top8[:, t, :], values[:, t, :])
    link(ins)
    link(nc.vector.tensor_copy(wanted[:, :, 0:n_top], top8[:, :, 0:n_top]))
    for t in range(NT):
        ins = nc.vector.match_replace(left[:, t, :], wanted[:, t, :], values[:, t, :], mark)
    link(ins)
    link(nc.vector.tensor_scalar(chosen, left[:, :, 0:width], mark, None, ALU.is_equal))


def experts0(k):
    nc, d = k.nc, k.dram
    E, F, TOP = 15, 2 * P, 3
    STEPS = E + 2
    PADS = 8 - TOP
    LOWEST = -1.0
    ctx = ExitStack()
    with ctx:
        w1 = k.sb("e0_w1", [P, 2, F], F32, ctx)
        w2 = k.sb("e0_w2", [P, 2, 2, D], F32, ctx)
        b1 = k.sb("e0_b1", [P, STEPS * 2], F32, ctx)
        b2 = k.sb("e0_b2", [E + 1, D], F32, ctx)
        gw = k.sb("e0_gw", [P, E], F32, ctx)
        gb = k.sb("e0_gb", [P, E], F32, ctx)
        acc = k.sb("e0_acc", [P, NT, D], F32, ctx)
        gates = k.sb("e0_gates", [P, NT, STEPS], F32, ctx)
        hidden = k.sb("e0_hidden", [P, 2, 2, T], F32, ctx)
        gates_loaded, late_loaded = k.sem("e0_gates_loaded"), k.sem("e0_late_loaded")
        slot_loaded = [k.sem(f"e0_slot{i}_loaded") for i in range(2)]
        out_done, added = k.sem("e0_out_done"), k.sem("e0_added")

        def load(sp, step, w1_src, w2_src):
            s = step % 2 if isinstance(step, int) else None
            sp.dma_start(w1[:, s, :], w1_src).then_inc(slot_loaded[s], 16)
            sp.dma_start(w2[:, s, :, :], w2_src.rearrange("(f p) m -> p f m", p=P)).then_inc(slot_loaded[s], 16)

        with ExitStack() as tmp:
            logits = k.sb("e0_logits", [P, NT, E], F32, tmp)
            top = k.sb("e0_top", [P, NT], F32, tmp)
            weights = k.sb("e0_weights", [P, NT, E + PADS], F32, tmp)
            total = k.sb("e0_total", [P, NT], F32, tmp)
            top8 = k.sb("e0_top8", [P, NT, 8], F32, tmp)
            wanted = k.sb("e0_wanted", [P, NT, 8], F32, tmp)
            left = k.sb("e0_left", [P, NT, E + PADS], F32, tmp)
            chosen = k.sb("e0_chosen", [P, NT, E], F32, tmp)
            gates_T = k.sb("e0_gates_T", [E + 1, T], F32, tmp)
            logit_ps = k.ps("e0_logit_ps", [P, NT, 16], tmp)
            turn_ps = k.ps("e0_turn_ps", [E + 1, T], tmp)
            b2_ps = k.ps("e0_b2_ps", [P, NT, D], tmp)
            logits_ready, shifted, exp_ready = (k.sem("e0_logits_ready"), k.sem("e0_shifted"),
                                                       k.sem("e0_exp_ready"))
            gates_ready, turned, turn_copied, b2_ready = (k.sem("e0_gates_ready"), k.sem("e0_turned"),
                                                          k.sem("e0_turn_copied"), k.sem("e0_b2_ready"))
            with nc.Block() as block:
                @block.sync
                def _(sp):
                    sp.dma_start(gw[:], d["L0_ffn_gW"]).then_inc(gates_loaded, 16)
                    sp.dma_start(gb[:], d["L0_ffn_gb"].unsqueeze(0).to_broadcast([P, E])).then_inc(gates_loaded, 16)
                    sp.dma_start(b2[0:1, :], d["L0_ffn_sb2"]).then_inc(late_loaded, 16)
                    sp.dma_start(b2[1:E + 1, :], d["L0_ffn_rb2"]).then_inc(late_loaded, 16)
                    sp.dma_start(b1[:, 0:4], d["L0_ffn_sb1_p"]).then_inc(late_loaded, 16)
                    sp.dma_start(b1[:, 4:], d["L0_ffn_rb1_p"]).then_inc(late_loaded, 16)
                    for s in range(2):
                        load(sp, s, d["L0_ffn_sW1"][0][:, s * F:(s + 1) * F], d["L0_ffn_sW2"][0][s * F:(s + 1) * F, :])
                    sp.wait_ge(late_loaded, 64)

                @block.tensor
                def _(pe):
                    pe.wait_ge(gates_loaded, 32)
                    for t in range(NT):
                        ins = nc.tensor.matmul(logit_ps[:, t, 0:E], k.x_T[:, t * P:(t + 1) * P], gw[:], start=True, stop=True)
                    ins.then_inc(logits_ready, 1)
                    pe.wait_ge(gates_ready, 1)
                    for t in range(NT):
                        ins = nc.tensor.transpose(turn_ps[:, t * P:(t + 1) * P], gates[:, t, 1:STEPS], k.ident[:])
                    ins.then_inc(turned, 1)
                    pe.wait_ge(turn_copied, 1)
                    pe.wait_ge(late_loaded, 64)
                    for t in range(NT):
                        ins = nc.tensor.matmul(b2_ps[:, t, :], gates_T[:, t * P:(t + 1) * P], b2[:], start=True, stop=True)
                    ins.then_inc(b2_ready, 1)

                @block.scalar
                def _(act):
                    act.wait_ge(shifted, 1)
                    nc.scalar.activation(weights[:, :, 0:E], logits[:], ACT.Exp).then_inc(exp_ready, 1)
                    act.wait_ge(turned, 1)
                    nc.scalar.copy(gates_T[:], turn_ps[:]).then_inc(turn_copied, 1)
                    nc.scalar.preload_act_table(ACT.Gelu)

                @block.vector
                def _(dve):
                    link = k.chain(dve)

                    def spread(x, n):
                        return x[:].unsqueeze(2).to_broadcast([P, NT, n])
                    nc.vector.memset(weights[:, :, E:E + PADS], LOWEST)
                    nc.vector.memset(wanted[:], LOWEST)
                    nc.vector.memset(gates[:, :, 0:2], 1.0)
                    dve.wait_ge(gates_loaded, 32)
                    dve.wait_ge(logits_ready, 1)
                    link(nc.vector.tensor_tensor(logits[:], logit_ps[:, :, 0:E], gb[:].unsqueeze(1).to_broadcast([P, NT, E]),
                                                 ALU.add))
                    link(nc.vector.tensor_reduce(top[:], logits[:], AX.X, ALU.max))
                    nc.vector.tensor_tensor(logits[:], logits[:], spread(top, E), ALU.subtract).then_inc(shifted, 1)
                    dve.wait_ge(exp_ready, 1)
                    link(nc.vector.tensor_reduce(total[:], weights[:, :, 0:E], AX.X, ALU.add))
                    link(nc.vector.reciprocal(total[:], total[:]))
                    link(nc.vector.tensor_tensor(weights[:, :, 0:E], weights[:, :, 0:E], spread(total, E), ALU.mult))
                    choose(nc, link, weights, E, PADS, TOP, LOWEST, top8, wanted, left, chosen[:])
                    nc.vector.tensor_tensor(gates[:, :, 2:STEPS], weights[:, :, 0:E], chosen[:], ALU.mult).then_inc(gates_ready, 1)
                    dve.wait_ge(b2_ready, 1)
                    nc.vector.tensor_tensor(acc[:], b2_ps[:], k.x_tok[:], ALU.add)

        with ExitStack() as tmp:
            hid_ps = k.ps("e0_hid_ps", [P, 2, T], tmp)
            out_ps = k.ps("e0_out_ps", [P, 2, NT, D], tmp)
            hid_ready, gelu_done = k.sem("e0_hid_ready"), k.sem("e0_gelu_done")

            def hid(pe, step, s):
                pe.wait_ge(slot_loaded[s], 32 * half(step, s) + 32)
                for f in range(2):
                    if not isinstance(step, int) or step > 0:
                        pe.wait_ge(gelu_done, 2 * step - 1 + f)
                    for h in range(2):
                        ins = nc.tensor.matmul(hid_ps[:, f, h * HALF:(h + 1) * HALF], w1[:, s, f * P:(f + 1) * P],
                                               k.x_T[:, h * HALF:(h + 1) * HALF], start=True, stop=True)
                    ins.then_inc(hid_ready, 1)

            def out(pe, step, s):
                pe.wait_ge(gelu_done, 2 * step + 2)
                pe.wait_ge(added, half(step, s))
                if s == 1:
                    pe.wait_ge(added_odd, half(step, s))
                for t in range(NT):
                    for f in range(2):
                        ins = nc.tensor.matmul(out_ps[:, s, t, :], hidden[:, s, f, t * P:(t + 1) * P], w2[:, s, f, :],
                                               start=(f == 0), stop=(f == 1))
                ins.then_inc(out_done, 1)

            def half(step, s):
                if isinstance(step, int):
                    return step // 2
                return pair_of[0] + (step_offset[0] - s) // 2

            pair_of, step_offset, added_odd = [None], [0], k.sem("e0_added_odd")

            with nc.Block() as block:
                @block.sync
                def _(sp):
                    with nc.sync.Fori(0, (E - 1) // 2) as p:
                        for s in range(2):
                            sp.wait_ge(out_done, 2 * p + s + 1)
                            e = 2 * p + s
                            sp.dma_start(w1[:, s, :], one(d["L0_ffn_rW1"], e)).then_inc(slot_loaded[s], 16)
                            sp.dma_start(w2[:, s, :, :], one(d["L0_ffn_rW2"], e).rearrange("(f p) m -> p f m", p=P)).then_inc(
                                slot_loaded[s], 16)
                    sp.wait_ge(out_done, STEPS - 2)
                    load(sp, STEPS - 1, d["L0_ffn_rW1"][E - 1], d["L0_ffn_rW2"][E - 1])

                @block.tensor
                def _(pe):
                    hid(pe, 0, 0)
                    with nc.tensor.Fori(0, (STEPS - 1) // 2) as p:
                        pair_of[0] = p
                        for s in range(2):
                            step_offset[0] = s + 1
                            hid(pe, 2 * p + s + 1, 1 - s)
                            step_offset[0] = s
                            out(pe, 2 * p + s, s)
                    out(pe, STEPS - 1, 0)

                def gelu(act, step, s):
                    act.wait_ge(out_done, step_less(step))
                    for f in range(2):
                        act.wait_ge(hid_ready, 2 * step + f + 1)
                        nc.scalar.activation(hidden[:, s, f, :], hid_ps[:, f, :], ACT.Gelu,
                                             bias=b1[:, bass.ds(2 * step + f, 1)]).then_inc(gelu_done, 1)

                def step_less(step):
                    return max(0, step - 1) if isinstance(step, int) else step - 1

                @block.scalar
                def _(act):
                    gelu(act, 0, 0)
                    gelu(act, 1, 1)
                    with nc.scalar.Fori(1, (STEPS - 1) // 2) as p:
                        for s in range(2):
                            gelu(act, 2 * p + s, s)
                    gelu(act, STEPS - 1, 0)

                def add_up(dve, step, s, nth):
                    dve.wait_ge(out_done, step + 1)
                    for t in range(NT):
                        if t == 0:
                            dve.wait_ge(added if s == 1 else added_odd, nth + (1 if s == 1 else 0))
                        ins = nc.vector.scalar_tensor_tensor(out=acc[:, t, :], in0=out_ps[:, s, t, :],
                                                             scalar=gates[:, t, bass.ds(step, 1)], in1=acc[:, t, :],
                                                             op0=ALU.mult, op1=ALU.add)
                    ins.then_inc(added_odd if s else added, 1)

                @block.vector
                def _(dve):
                    with nc.vector.Fori(0, (STEPS - 1) // 2) as p:
                        for s in range(2):
                            add_up(dve, 2 * p + s, s, p)
                    add_up(dve, STEPS - 1, 0, (STEPS - 1) // 2)
        residual_norm(k, "norm2", acc)


def one(ap, e):
    return ap[bass.ds(e, 1)].rearrange("o a b -> (o a) b")


def turn_stack(k, tag, stack, stack_T, turn_ps, stack_ready, used_dve, used_act, turned, base=0):
    nc = k.nc
    G = NT * H // 8

    def on_pe(pe):
        pe.wait_ge(stack_ready, base + 1)
        for g in range(G):
            if g >= 4 or base:
                pe.wait_ge(used_act if g % 2 else used_dve, base * G // 2 + (g - 4) // 2 + 1)
            for j in range(8):
                ins = nc.tensor.transpose(turn_ps[:, g % 4, j * P:(j + 1) * P], stack[:, g * 8 + j, :], k.ident_b[:])
            ins.then_inc(turned, 1)

    def on_dve(dve):
        for g in range(0, G, 2):
            dve.wait_ge(turned, base * G + g + 1)
            nc.vector.tensor_copy(stack_T[:, g // 2, 0:8 * P], turn_ps[:, g % 4, :]).then_inc(used_dve, 1)

    def on_act(act):
        for g in range(1, G, 2):
            act.wait_ge(turned, base * G + g + 1)
            nc.scalar.copy(stack_T[:, g // 2, 8 * P:16 * P], turn_ps[:, g % 4, :]).then_inc(used_act, 1)

    return on_pe, on_dve, on_act


def self_attention(k):
    nc, d = k.nc, k.dram
    R = 16
    LORA = 32.0 / R
    ctx = ExitStack()
    with ctx:
        q_T = k.sb("s_q_stack_T", [P, NT, H * P], BF16, ctx)
        k_T = k.sb("s_k_stack_T", [P, NT, H * P], BF16, ctx)
        val = k.sb("s_val_ones", [P, NT, H, 32], F32, ctx)
        w_proj = k.sb("s_w_proj", [P, D], F32, ctx)
        b_proj = k.sb("s_b_proj", [P, D], F32, ctx)
        with ExitStack() as tmp:
            w = k.sb("s_w_qkv", [P, 3 * D], F32, tmp)
            b_feat = k.sb("s_b_feat", [P, 3], F32, tmp)
            b_k = k.sb("s_b_k", [P, D], F32, tmp)
            lora_a = k.sb("s_lora_a", [R, 2, H, HD], F32, tmp)
            lora_b = k.sb("s_lora_b", [R, 2, H, HD], F32, tmp)
            mask = k.sb("s_mask", [P, H, HD], F32, tmp)
            mix = k.sb("s_mix", [P, 2, D], F32, tmp)
            before = k.sb("s_before", [P, 2, T], F32, tmp)
            tok = k.sb("s_tok", [P, NT * H, HD], F32, tmp)
            part = [k.sb(f"s_part{i}", [P, NT * H, HD], BF16, tmp) for i in range(3)]
            rest = [before[:, i, :].rearrange("p (a b) -> p a b", b=HD) for i in range(2)]
            stack = k.sb("s_stack", [P, NT * H, AUG], BF16, tmp)
            proj_ps = k.ps("s_proj_ps", [P, 2, T], tmp)
            turn_ps = k.ps("s_turn_ps", [P, 4, 8 * P], tmp, BF16)
            loaded = k.sem("s_loaded")
            masked0, masked1, masked2 = k.sem("s_masked0"), k.sem("s_masked1"), k.sem("s_masked2")
            mix_raw, mix_ready, raw_ready, biased = (k.sem("s_mix_raw"), k.sem("s_mix_ready"), k.sem("s_raw_ready"),
                                                     k.sem("s_biased"))
            tok_ready, tok_taken, stack_ready = k.sem("s_tok_ready"), k.sem("s_tok_taken"), k.sem("s_stack_ready")
            turned, used_dve, used_act = k.sem("s_turned"), k.sem("s_turn_used_dve"), k.sem("s_turn_used_act")
            turns = [turn_stack(k, "s", stack, x, turn_ps, stack_ready, used_dve, used_act, turned, base=i)
                     for i, x in enumerate((q_T, k_T))]
            with nc.Block() as block:
                @block.sync
                def _(sp):
                    sp.dma_start(w[:], d["L1_attn_w_qkv"]).then_inc(loaded, 16)
                    with nc.allow_non_contiguous_dma(reason="three floats to a partition; 256 of a LoRA matrix"):
                        sp.dma_start(b_feat[:], d["L1_attn_b_qkv"].rearrange("(s p) -> p s", p=P)).then_inc(loaded, 16)
                        for i, n in enumerate("qv"):
                            sp.dma_start(lora_a[:, i], d[f"L1_attn_a_{n}_T"].unsqueeze(1).to_broadcast([R, H, HD])).then_inc(loaded, 16)
                            sp.dma_start(lora_b[:, i], d[f"L1_attn_b_{n}"].unsqueeze(1).to_broadcast([R, H, HD])).then_inc(loaded, 16)
                    sp.dma_start(b_k[:], d["L1_attn_b_qkv"][D:2 * D].unsqueeze(0).to_broadcast([P, D])).then_inc(loaded, 16)
                    sp.dma_start(w_proj[:], d["L1_attn_w_proj"]).then_inc(loaded, 16)
                    sp.dma_start(b_proj[:], d["L1_attn_b_proj"].unsqueeze(0).to_broadcast([P, D])).then_inc(loaded, 16)

                @block.gpsimd
                def _(pool):
                    nc.gpsimd.memset(mask[:], LORA).then_inc(masked0, 1)
                    pool.wait_ge(masked0, 1)
                    nc.gpsimd.affine_select(out=mask[:], in_=mask[:], compare_op=ALU.is_ge, fill=0.0, base=0,
                                            pattern=[[-HD, H], [0, HD]], channel_multiplier=1).then_inc(masked1, 1)
                    pool.wait_ge(masked1, 1)
                    nc.gpsimd.affine_select(out=mask[:], in_=mask[:], compare_op=ALU.is_ge, fill=0.0, base=HD - 1,
                                            pattern=[[HD, H], [0, HD]], channel_multiplier=-1).then_inc(masked2, 1)

                @block.tensor
                def _(pe):
                    pe.wait_ge(loaded, 16 * 9)
                    for i in range(2):
                        ins = nc.tensor.matmul(proj_ps[:, i, 0:D], lora_a[:, i].rearrange("r h e -> r (h e)"),
                                               lora_b[:, i].rearrange("r h e -> r (h e)"), start=True, stop=True)
                    ins.then_inc(mix_raw, 1)
                    pe.wait_ge(mix_ready, 1)
                    for i, col in enumerate((0, 2 * D)):
                        for h in range(2):
                            ins = nc.tensor.matmul(proj_ps[:, i, h * HALF:(h + 1) * HALF], w[:, col:col + D],
                                                   k.x_T[:, h * HALF:(h + 1) * HALF], start=True, stop=True)
                        ins.then_inc(raw_ready, 1)
                    for i in range(2):
                        pe.wait_ge(biased, i + 1)
                        for t in range(NT):
                            ins = nc.tensor.matmul(proj_ps[:, i, t * P:(t + 1) * P], before[:, i, t * P:(t + 1) * P],
                                                   mix[:, i, :], start=True, stop=True)
                        ins.then_inc(tok_ready, 1)
                    pe.wait_ge(tok_taken, 1)
                    for t in range(NT):
                        ins = nc.tensor.matmul(proj_ps[:, 0, t * P:(t + 1) * P], k.x_T[:, t * P:(t + 1) * P],
                                               w[:, D:2 * D], start=True, stop=True)
                    ins.then_inc(tok_ready, 1)
                    for on_pe, _, _ in turns:
                        on_pe(pe)

                @block.scalar
                def _(act):
                    for i, col in enumerate((0, 2)):
                        act.wait_ge(raw_ready, i + 1)
                        nc.scalar.activation(before[:, i, :], proj_ps[:, i, :], ACT.Identity,
                                             bias=b_feat[:, col:col + 1]).then_inc(biased, 1)
                    for _, _, on_act in turns:
                        on_act(act)
                    nc.scalar.preload_act_table(ACT.Exp)

                @block.vector
                def _(dve):
                    link = k.chain(dve)
                    flat = tok[:].rearrange("p a b -> p (a b)")
                    nc.vector.memset(val[:], 0.0)
                    nc.vector.memset(stack[:, :, USED:AUG], 0.0)
                    link(nc.vector.memset(stack[:, :, SHIFT:SHIFT + 3], 0.0))
                    link(nc.vector.memset(val[:, :, :, HD:HD + 1], 1.0))
                    dve.wait_ge(mix_raw, 1)
                    dve.wait_ge(masked2, 1)
                    for i in range(2):
                        link(nc.vector.tensor_tensor(mix[:, i, :], proj_ps[:, i, 0:D], mask[:].rearrange("p h e -> p (h e)"),
                                                     ALU.mult))
                    link(nc.vector.tensor_tensor(mix[:, 0, :], mix[:, 0, :], k.ident[:], ALU.add))
                    nc.vector.tensor_tensor(mix[:, 1, :], mix[:, 1, :], k.ident[:], ALU.add).then_inc(mix_ready, 1)
                    dve.wait_ge(tok_ready, 1)
                    dve.wait_ge(tok_ready, 2)
                    nc.vector.tensor_scalar(flat, proj_ps[:, 0, :], float(HD) ** -0.5, None, ALU.mult).then_inc(tok_taken, 1)
                    dve.wait_ge(tok_taken, 1)
                    nc.vector.tensor_copy(val[:, :, :, 0:HD], proj_ps[:, 1, :].rearrange("p (t h e) -> p t h e", t=NT, h=H))
                    stack_queries(nc, link, tok[:], [x[:] for x in part], rest, stack, Q_PARTS).then_inc(stack_ready, 1)
                    turns[0][1](dve)
                    dve.wait_ge(tok_ready, 3)
                    dve.wait_ge(turned, NT * H // 8)
                    nc.vector.memset(stack[:, :, SHIFT:SHIFT + 3], 1.0)
                    link(nc.vector.tensor_tensor(tok[:].rearrange("p (t h) e -> p t (h e)", t=NT),
                                                 proj_ps[:, 0, :].rearrange("p (t f) -> p t f", t=NT),
                                                 b_k[:].unsqueeze(1).to_broadcast([P, NT, D]), ALU.add))
                    stack_queries(nc, link, tok[:], [x[:] for x in part], rest, stack, K_PARTS).then_inc(stack_ready, 1)
                    turns[1][1](dve)

        gathered = k.sb("s_gathered", [P, H, 2 * P], F32, ctx)
        with ExitStack() as tmp:
            q_buf = k.sb("s_q_buf", [P, 2, T], BF16, tmp)
            k_buf = k.sb("s_k_buf", [P, 2, T], BF16, tmp)
            v_buf = k.sb("s_v_buf", [P, 2, NT, 32], F32, tmp)
            probs = k.sb("s_probs", [P, 2, T], F32, tmp)
            partial = k.sb("s_max_partial", [P, NT, 2], F32, tmp)
            neg = k.sb("s_neg_max", [P, NT], F32, tmp)
            rests = [k.sb(f"s_neg_rest{i}", [P, NT], F32, tmp) for i in range(2)]
            part3 = k.sb("s_neg_part", [P, NT, 3], BF16, tmp)
            score_ps = k.ps("s_score_ps", [P, 2, T], tmp)
            max_ps = k.ps("s_max_ps", [P, 2, HALF], tmp)
            acc_ps = k.ps("s_acc_ps", [P, 2, HALF], tmp)
            shift_ps = max_ps[:, 0, :].bitcast(BF16)
            steps_before = k.steps.n
            LINKED = 5
            buf_ready, q_ready, val_ready = k.sem("s_buf_ready"), k.sem("s_q_ready"), k.sem("s_val_ready")
            unit_ready, unit_used, parts_ready, shift_turned = (k.sem("s_max_ready"), k.sem("s_max_used"),
                                                                k.sem("s_neg_parts_ready"), k.sem("s_shift_turned"))
            score_ready, exp_done, pv_done, acc_used = (k.sem("s_score_ready"), k.sem("s_exp_done"), k.sem("s_pv_done"),
                                                        k.sem("s_acc_used"))
            UNITS = 2 * NT
            QUART = T // 4

            def max_unit(pe, h, s, u, first=False):
                t, half = u // 2, u % 2
                if u >= 2 or not first:
                    pe.wait_ge(unit_used, h * UNITS + u - 1)
                nc.tensor.matmul(max_ps[:, u % 2, :], q_buf[:, s, t * P:(t + 1) * P],
                                 k_buf[:, s, half * HALF:(half + 1) * HALF], start=True, stop=True).then_inc(unit_ready, 1)

            def turn_shift(pe, h):
                pe.wait_ge(parts_ready, h + 1)
                for t in range(NT):
                    ins = nc.tensor.transpose(shift_ps[0:3, t * P:(t + 1) * P], part3[:, t, :], k.ident_b[:])
                ins.then_inc(shift_turned, 1)

            def attend(pe, h, s, with_max):
                pe.wait_ge(q_ready, h + 1)
                if with_max:
                    pe.wait_ge(buf_ready, h + 2)
                for c in range(NT + 1):
                    if c < NT:
                        pe.wait_ge(exp_done, h * NT + max(0, c - 1))
                        for half in range(2):
                            ins = nc.tensor.matmul(score_ps[:, c % 2, half * HALF:(half + 1) * HALF],
                                                   k_buf[:, s, c * P:(c + 1) * P],
                                                   q_buf[:, s, half * HALF:(half + 1) * HALF], start=True, stop=True)
                        ins.then_inc(score_ready, 1)
                        if with_max and c < NT - 1:
                            for u in range(UNITS * c // (NT - 1), UNITS * (c + 1) // (NT - 1)):
                                max_unit(pe, h + 1, 1 - s, u)
                    if c == NT and with_max:
                        turn_shift(pe, h + 1)
                    if c >= 1:
                        v = c - 1
                        if v == 0:
                            pe.wait_ge(acc_used, at_least(h, 1))
                            pe.wait_ge(val_ready, h + 1)
                        pe.wait_ge(exp_done, h * NT + v + 1)
                        for j in range(4):
                            ins = nc.tensor.matmul(acc_ps[32 * j:32 * j + 32, s, 0:QUART], v_buf[:, s, v, :],
                                                   probs[:, v % 2, j * QUART:(j + 1) * QUART],
                                                   start=(v == 0), stop=(v == NT - 1))
                        ins.then_inc(pv_done, 1)

            def at_least(h, n):
                return max(0, h - n) if isinstance(h, int) else h - n

            def exponentiate(act, h, s):
                for c in range(NT):
                    act.wait_ge(score_ready, h * NT + c + 1)
                    act.wait_ge(pv_done, h * NT + max(0, c - 1))
                    nc.scalar.activation(probs[:, c % 2, :], score_ps[:, c % 2, :], ACT.Exp).then_inc(exp_done, 1)
                act.wait_ge(pv_done, (h + 1) * NT)
                nc.scalar.copy(gathered[:, at(h), :], acc_ps[:, s, 0:QUART]).then_inc(acc_used, 1)

            def at(h):
                return h if isinstance(h, int) else bass.ds(h, 1)

            def head(ap, h):
                return ap[:].rearrange("p t (h c) -> p t h c", h=H)[:, :, at(h), :]

            def maxima(dve, h, s):
                def view(buf):
                    x = buf[:, s, :].rearrange("p (t c) -> p t c", t=NT)
                    return x if isinstance(h, int) else x.unsqueeze(2)
                nc.vector.tensor_copy(view(k_buf), head(k_T, h))
                nc.vector.tensor_copy(view(q_buf), head(q_T, h)).then_inc(buf_ready, 1)
                for u in range(UNITS):
                    dve.wait_ge(unit_ready, h * UNITS + u + 1)
                    nc.vector.tensor_reduce(partial[:, u // 2, u % 2:u % 2 + 1], max_ps[:, u % 2, :], AX.X,
                                            ALU.max).then_inc(unit_used, 1)
                dve.wait_ge(unit_used, (h + 1) * UNITS)
                link = k.chain(dve)
                link.n = steps_before + h * LINKED
                negated_maximum(nc, link, partial[:], neg[:], [x[:] for x in rests], part3[:]).then_inc(parts_ready, 1)
                dve.wait_ge(shift_turned, h + 1)
                nc.vector.tensor_copy(q_buf[SHIFT:SHIFT + 3, s, :], shift_ps[0:3, :]).then_inc(q_ready, 1)
                dve.wait_ge(q_ready, h + 1)

            def values(pool, h, s):
                out = v_buf[:, s, :, :] if isinstance(h, int) else v_buf[:, s, :, :].unsqueeze(2)
                nc.gpsimd.tensor_copy(out, val[:, :, at(h), :]).then_inc(val_ready, 1)

            with nc.Block() as block:
                @block.tensor
                def _(pe):
                    pe.wait_ge(buf_ready, 1)
                    for u in range(UNITS):
                        max_unit(pe, 0, 0, u, True)
                    turn_shift(pe, 0)
                    attend(pe, 0, 0, True)
                    with nc.tensor.Fori(0, H // 2 - 1) as p:
                        for s in (1, 0):
                            attend(pe, 2 * p + (1 if s else 2), s, True)
                    attend(pe, H - 1, 1, False)

                @block.scalar
                def _(act):
                    with nc.scalar.Fori(0, H // 2) as p:
                        for s in range(2):
                            exponentiate(act, 2 * p + s, s)

                @block.gpsimd
                def _(pool):
                    for h in range(2):
                        values(pool, h, h)
                    with nc.gpsimd.Fori(1, H // 2) as p:
                        for s in range(2):
                            pool.wait_ge(pv_done, (2 * p + s - 1) * NT)
                            values(pool, 2 * p + s, s)

                @block.vector
                def _(dve):
                    maxima(dve, 0, 0)
                    maxima(dve, 1, 1)
                    with nc.vector.Fori(1, H // 2) as p:
                        for s in range(2):
                            dve.wait_ge(score_ready, (2 * p + s - 1) * NT)
                            maxima(dve, 2 * p + s, s)
                    k.steps.n = steps_before + H * LINKED

        with ExitStack() as tmp:
            merged = k.sb("s_merged", [P, NT, D], F32, tmp)
            out_ps = k.ps("s_out_ps", [P, NT, D], tmp)
            finish_heads(k, "self", gathered, merged, w_proj, out_ps, by_tile=False)
            residual_norm(k, "norm3", out_ps, bias=b_proj)


def context_attention1(k):
    nc, d = k.nc, k.dram
    WIDE = 2 * HALF
    RANGES = [(c0, min(WIDE, CTX - c0)) for c0 in range(0, CTX, WIDE)]
    NR = len(RANGES)
    GROUPS = [(c, min(4, NCH - c)) for c in range(0, NCH, 4)]
    NG = len(GROUPS)
    SCALE = float(D) ** -0.5
    ctx = ExitStack()
    with ctx:
        q_T = k.sb("x1_q_T", [P, T], F32, ctx)
        merged = k.sb("x1_merged", [P, NT, D], F32, ctx)
        w_out = k.sb("x1_w_out", [P, D], F32, ctx)
        b_out = k.sb("x1_b_out", [P, D], F32, ctx)
        b_v = k.sb("x1_b_v", [P, D], F32, ctx)
        with ExitStack() as tmp:
            w_q = k.sb("x1_w_q", [P, D], F32, tmp)
            b_q = k.sb("x1_b_q", [P, 1], F32, tmp)
            b_scaled = k.sb("x1_b_scaled", [P, 1], F32, tmp)
            q_ps = k.ps("x1_q_ps", [P, T], tmp)
            loaded, q_ready, scaled = k.sem("x1_loaded"), k.sem("x1_q_ready"), k.sem("x1_scaled")
            with nc.Block() as block:
                @block.sync
                def _(sp):
                    sp.dma_start(w_q[:], d["L1_xattn_Wq_T"]).then_inc(loaded, 16)
                    with nc.allow_non_contiguous_dma(reason="a float to a partition"):
                        sp.dma_start(b_q[:], d["L1_xattn_bq"].unsqueeze(1)).then_inc(loaded, 16)
                    sp.dma_start(w_out[:], d["L1_xattn_Wo_T"]).then_inc(loaded, 16)
                    sp.dma_start(b_v[:], d["L1_xattn_bv"].unsqueeze(0).to_broadcast([P, D])).then_inc(loaded, 16)
                    sp.dma_start(b_out[:], d["L1_xattn_bo"].unsqueeze(0).to_broadcast([P, D])).then_inc(loaded, 16)

                @block.tensor
                def _(pe):
                    pe.wait_ge(loaded, 80)
                    for h in range(2):
                        nc.tensor.matmul(q_ps[:, h * HALF:(h + 1) * HALF], w_q[:], k.x_T[:, h * HALF:(h + 1) * HALF],
                                         start=True, stop=True).then_inc(q_ready, 1)

                @block.vector
                def _(dve):
                    dve.wait_ge(loaded, 80)
                    nc.vector.tensor_scalar(b_scaled[:], b_q[:], SCALE, None, ALU.mult).then_inc(scaled, 1)

                @block.scalar
                def _(act):
                    act.wait_ge(scaled, 1)
                    for h in range(2):
                        act.wait_ge(q_ready, h + 1)
                        nc.scalar.activation(q_T[:, h * HALF:(h + 1) * HALF], q_ps[:, h * HALF:(h + 1) * HALF],
                                             ACT.Identity, bias=b_scaled[:], scale=SCALE)
                    nc.scalar.preload_act_table(ACT.Exp)

        with ExitStack() as tmp:
            q_buf = k.sb("x1_q_buf", [P, 2, P], F32, tmp)
            scores = k.sb("x1_scores", [P, 2, CTX], F32, tmp)
            turned = k.sb("x1_turned", [P, 2, HALF], F32, tmp)
            top = k.sb("x1_top", [P, 2, NR], F32, tmp)
            neg = k.sb("x1_neg", [P, 2], F32, tmp)
            sums = k.sb("x1_sums", [P, 2, NR], F32, tmp)
            total = k.sb("x1_total", [P, 2], F32, tmp)
            recip = k.sb("x1_recip", [P, 2], F32, tmp)
            score_ps = k.ps("x1_score_ps", [P, 2, WIDE], tmp)
            turn_ps = k.ps("x1_turn_ps", [P, 2, HALF], tmp)
            acc_ps = k.ps("x1_acc_ps", [P, 2, HALF], tmp)
            q_ready, range_ready, taken = k.sem("x1_q_buf_ready"), k.sem("x1_range_ready"), k.sem("x1_taken")
            neg_ready, exp_done, group_turned = k.sem("x1_neg_ready"), k.sem("x1_exp_done"), k.sem("x1_group_turned")
            copied = [k.sem("x1_copied_even"), k.sem("x1_copied_odd")]
            pv_done, summed, recip_ready, merged_ready = (k.sem("x1_pv_done"), k.sem("x1_summed"), k.sem("x1_recip_ready"),
                                                          k.sem("x1_merged_ready"))

            def tile_of(p, s):
                return 2 * p + s

            def score_step(pe, p, s, g):
                t = tile_of(p, s)
                r, n = g // 2, min(HALF, CTX - g * HALF)
                local = NR * s + r
                if g == 0:
                    pe.wait_ge(q_ready, t + 1)
                if g % 2 == 0 and not (isinstance(p, int) and p == 0 and local < 2):
                    pe.wait_ge(taken, 2 * NR * p + local - 1)
                ins = nc.tensor.matmul(score_ps[:, local % 2, (g % 2) * HALF:(g % 2) * HALF + n], q_buf[:, s, :],
                                       k.key1_T[:, g * HALF:g * HALF + n], start=True, stop=True)
                if g % 2 == 1 or g == NG - 1:
                    ins.then_inc(range_ready, 1)

            def weigh_turn(pe, p, s, g):
                t, local = tile_of(p, s), NG * s + g
                c0, m = GROUPS[g]
                last_key = min(CTX, (c0 + m) * P)
                pe.wait_ge(exp_done, NR * t + (last_key - 1) // WIDE + 1)
                pe.wait_ge(copied[local % 2], NG * p + local // 2)
                for j in range(m):
                    keys = min(P, CTX - (c0 + j) * P)
                    ins = nc.tensor.transpose(turn_ps[0:keys, local % 2, j * P:(j + 1) * P],
                                              scores[:, s, (c0 + j) * P:(c0 + j) * P + keys], k.ident[:])
                ins.then_inc(group_turned, 1)

            def weigh_add(pe, p, s, g):
                t, local = tile_of(p, s), NG * s + g
                c0, m = GROUPS[g]
                pe.wait_ge(copied[local % 2], NG * p + local // 2 + 1)
                if g == 0:
                    pe.wait_ge(merged_ready, 2 * p + max(0, s - 1))
                for j in range(m):
                    keys = min(P, CTX - (c0 + j) * P)
                    ins = nc.tensor.matmul(acc_ps[:, s, 0:D], turned[0:keys, local % 2, j * P:(j + 1) * P],
                                           k.val1[0:keys, c0 + j, :], start=(c0 + j == 0), stop=(c0 + j == NCH - 1))
                ins.then_inc(pv_done, 1)

            def copy_group(eng, copy, p, s, g):
                local = NG * s + g
                c0, m = GROUPS[g]
                eng.wait_ge(group_turned, 2 * NG * p + local + 1)
                eng.wait_ge(pv_done, 2 * NG * p + max(0, local - 1))
                full = min(m, NCH - 1 - c0)
                ins = copy(turned[:, local % 2, 0:full * P], turn_ps[:, local % 2, 0:full * P])
                if full < m:
                    ins = copy(turned[0:TAIL, local % 2, full * P:m * P], turn_ps[0:TAIL, local % 2, full * P:m * P])
                ins.then_inc(copied[local % 2], 1)

            def tile_on_pe(pe, p, s, nxt):
                for g in range(NG + 1):
                    if g < NG:
                        if nxt:
                            score_step(pe, *nxt, g)
                        weigh_turn(pe, p, s, g)
                    if g >= 1:
                        weigh_add(pe, p, s, g - 1)

            def take_range(dve, p, s, r):
                t, local = tile_of(p, s), NR * s + r
                c0, cols = RANGES[r]
                dve.wait_ge(range_ready, 2 * NR * p + local + 1)
                nc.vector.tensor_scalar(scores[:, s, c0:c0 + cols], score_ps[:, local % 2, 0:cols], 1.0, None, ALU.mult,
                                        ALU.max, accum_out=top[:, s, r:r + 1]).then_inc(taken, 1)
                if r == NR - 1:
                    dve.wait_ge(taken, NR * (t + 1))
                    nc.vector.tensor_reduce(neg[:, s:s + 1], top[:, s, :], AX.X, ALU.max, negate=True).then_inc(neg_ready, 1)

            def fetch_query(dve, p, s):
                t = tile_of(p, s)
                src = q_T[:, t * P:(t + 1) * P] if isinstance(p, int) else q_T[:, bass.ds(t * P, P)]
                nc.vector.tensor_copy(q_buf[:, s, :], src).then_inc(q_ready, 1)

            def tile_on_dve(dve, p, s, nxt):
                if nxt:
                    fetch_query(dve, *nxt)
                for g in range(NG):
                    if nxt and (g % 2 == 1 or g == NG - 1):
                        take_range(dve, *nxt, g // 2)
                    if (NG * s + g) % 2 == 0:
                        copy_group(dve, nc.vector.tensor_copy, p, s, g)
                t = tile_of(p, s)
                dve.wait_ge(exp_done, NR * (t + 1))
                nc.vector.tensor_reduce(total[:, s:s + 1], sums[:, s, :], AX.X, ALU.add).then_inc(summed, 1)
                dve.wait_ge(summed, t + 1)
                nc.vector.reciprocal(recip[:, s:s + 1], total[:, s:s + 1]).then_inc(recip_ready, 1)
                dve.wait_ge(recip_ready, t + 1)
                dve.wait_ge(pv_done, NG * (t + 1))
                out = merged[:, t, :] if isinstance(p, int) else merged[:, bass.ds(t, 1), :].rearrange("p o e -> p (o e)")
                nc.vector.scalar_tensor_tensor(out=out, in0=acc_ps[:, s, 0:D], scalar=recip[:, s:s + 1], in1=b_v[:],
                                               op0=ALU.mult, op1=ALU.add).then_inc(merged_ready, 1)

            def exponentiate(act, p, s):
                t = tile_of(p, s)
                act.wait_ge(neg_ready, t + 1)
                act.wait_ge(summed, 2 * p + max(0, s - 1))
                for r, (c0, cols) in enumerate(RANGES):
                    nc.scalar.activation(scores[:, s, c0:c0 + cols], scores[:, s, c0:c0 + cols], ACT.Exp,
                                         bias=neg[:, s:s + 1], accum_out=sums[:, s, r:r + 1]).then_inc(exp_done, 1)

            def tile_on_act(act, p, s):
                exponentiate(act, p, s)
                for g in range(NG):
                    if (NG * s + g) % 2 == 1:
                        copy_group(act, nc.scalar.copy, p, s, g)

            LAST = NT // 2 - 1
            with nc.Block() as block:
                @block.tensor
                def _(pe):
                    for g in range(NG):
                        score_step(pe, 0, 0, g)
                    with nc.tensor.Fori(0, LAST) as p:
                        tile_on_pe(pe, p, 0, (p, 1))
                        tile_on_pe(pe, p, 1, (p + 1, 0))
                    tile_on_pe(pe, LAST, 0, (LAST, 1))
                    tile_on_pe(pe, LAST, 1, None)

                @block.vector
                def _(dve):
                    fetch_query(dve, 0, 0)
                    for r in range(NR):
                        take_range(dve, 0, 0, r)
                    with nc.vector.Fori(0, LAST) as p:
                        tile_on_dve(dve, p, 0, (p, 1))
                        tile_on_dve(dve, p, 1, (p + 1, 0))
                    tile_on_dve(dve, LAST, 0, (LAST, 1))
                    tile_on_dve(dve, LAST, 1, None)

                @block.scalar
                def _(act):
                    with nc.scalar.Fori(0, NT // 2) as p:
                        for s in range(2):
                            tile_on_act(act, p, s)

        with ExitStack() as tmp:
            out_ps = k.ps("x1_out_ps", [P, NT, D], tmp)
            project(k, "x1", merged, w_out, out_ps)
            residual_norm(k, "norm4", out_ps, bias=b_out)


def experts1(k, store=None):
    nc, d = k.nc, k.dram
    E, F, TOP = 8, 2 * P, 2
    PADS = 8 - TOP
    LOWEST = -1e38
    ctx = ExitStack()
    with ctx:
        w1 = k.sb("e1_w1", [P, 2, F], F32, ctx)
        w2 = k.sb("e1_w2", [P, 2, F], F32, ctx)
        w3 = k.sb("e1_w3", [P, 2, 2, D], F32, ctx)
        b1 = k.sb("e1_b1", [P, E * 2], F32, ctx)
        b2 = k.sb("e1_b2", [P, E * 2], F32, ctx)
        b3 = k.sb("e1_b3", [E, D], F32, ctx)
        wg = k.sb("e1_wg", [P, E], F32, ctx)
        acc = k.sb("e1_acc", [P, NT, D], F32, ctx)
        gates = k.sb("e1_gates", [P, NT, E], F32, ctx)
        gate_act = k.sb("e1_silu", [P, 2, T], F32, ctx)
        hidden = k.sb("e1_hidden", [P, 2, 2, T], F32, ctx)
        early_loaded, late_loaded = k.sem("e1_early_loaded"), k.sem("e1_late_loaded")
        slot_loaded = [k.sem(f"e1_slot{i}_loaded") for i in range(2)]
        out_done, added = k.sem("e1_out_done"), [k.sem("e1_added_even"), k.sem("e1_added_odd")]

        def load(sp, e, s):
            for buf, n in ((w1, "W1"), (w2, "W2")):
                sp.dma_start(buf[:, s, :], one(d[f"L1_ffn_{n}_T"], e)).then_inc(slot_loaded[s], 16)
            sp.dma_start(w3[:, s, :, :], one(d["L1_ffn_W3_T"], e).rearrange("(f p) m -> p f m", p=P)).then_inc(
                slot_loaded[s], 16)

        with ExitStack() as tmp:
            scores = k.sb("e1_scores", [P, NT, E + PADS], F32, tmp)
            top8 = k.sb("e1_top8", [P, NT, 8], F32, tmp)
            wanted = k.sb("e1_wanted", [P, NT, 8], F32, tmp)
            left = k.sb("e1_left", [P, NT, E + PADS], F32, tmp)
            chosen = k.sb("e1_chosen", [P, NT, E], F32, tmp)
            raised = k.sb("e1_raised", [P, NT, E], F32, tmp)
            total = k.sb("e1_total", [P, NT], F32, tmp)
            gates_T = k.sb("e1_gates_T", [E, T], F32, tmp)
            score_ps = k.ps("e1_score_ps", [P, NT, E], tmp)
            turn_ps = k.ps("e1_turn_ps", [E, T], tmp)
            b3_ps = k.ps("e1_b3_ps", [P, NT, D], tmp)
            scores_ready, shifted, exp_ready = (k.sem("e1_scores_ready"), k.sem("e1_shifted"),
                                                      k.sem("e1_exp_ready"))
            gates_ready, turned, turn_copied, b3_ready = (k.sem("e1_gates_ready"), k.sem("e1_turned"),
                                                          k.sem("e1_turn_copied"), k.sem("e1_b3_ready"))
            with nc.Block() as block:
                @block.sync
                def _(sp):
                    sp.dma_start(wg[:], d["L1_ffn_Wg_T"]).then_inc(early_loaded, 16)
                    sp.dma_start(b3[:], d["L1_ffn_b3"]).then_inc(late_loaded, 16)
                    sp.dma_start(b1[:], d["L1_ffn_b1_p"]).then_inc(late_loaded, 16)
                    sp.dma_start(b2[:], d["L1_ffn_b2_p"]).then_inc(late_loaded, 16)
                    for s in range(2):
                        load(sp, s, s)
                    sp.wait_ge(late_loaded, 48)

                @block.tensor
                def _(pe):
                    pe.wait_ge(early_loaded, 16)
                    for t in range(NT):
                        ins = nc.tensor.matmul(score_ps[:, t, :], k.x_T[:, t * P:(t + 1) * P], wg[:], start=True, stop=True)
                    ins.then_inc(scores_ready, 1)
                    pe.wait_ge(gates_ready, 1)
                    for t in range(NT):
                        ins = nc.tensor.transpose(turn_ps[:, t * P:(t + 1) * P], gates[:, t, :], k.ident[:])
                    ins.then_inc(turned, 1)
                    pe.wait_ge(turn_copied, 1)
                    pe.wait_ge(late_loaded, 48)
                    for t in range(NT):
                        ins = nc.tensor.matmul(b3_ps[:, t, :], gates_T[:, t * P:(t + 1) * P], b3[:], start=True, stop=True)
                    ins.then_inc(b3_ready, 1)

                @block.scalar
                def _(act):
                    act.wait_ge(shifted, 1)
                    nc.scalar.activation(raised[:], raised[:], ACT.Exp).then_inc(exp_ready, 1)
                    act.wait_ge(turned, 1)
                    nc.scalar.copy(gates_T[:], turn_ps[:]).then_inc(turn_copied, 1)
                    nc.scalar.preload_act_table(ACT.Silu)

                @block.vector
                def _(dve):
                    link = k.chain(dve)
                    nc.vector.memset(scores[:, :, E:E + PADS], LOWEST)
                    nc.vector.memset(wanted[:], LOWEST)
                    dve.wait_ge(scores_ready, 1)
                    link(nc.vector.tensor_copy(scores[:, :, 0:E], score_ps[:]))
                    choose(nc, link, scores, E, PADS, TOP, LOWEST, top8, wanted, left, chosen[:])
                    nc.vector.tensor_tensor(raised[:], scores[:, :, 0:E], top8[:, :, 0:1].to_broadcast([P, NT, E]),
                                            ALU.subtract).then_inc(shifted, 1)
                    dve.wait_ge(exp_ready, 1)
                    link(nc.vector.tensor_tensor(raised[:], raised[:], chosen[:], ALU.mult))
                    link(nc.vector.tensor_reduce(total[:], raised[:], AX.X, ALU.add))
                    link(nc.vector.reciprocal(total[:], total[:]))
                    nc.vector.tensor_tensor(gates[:], raised[:], total[:].unsqueeze(2).to_broadcast([P, NT, E]),
                                            ALU.mult).then_inc(gates_ready, 1)
                    dve.wait_ge(b3_ready, 1)
                    nc.vector.tensor_copy(acc[:], b3_ps[:])

        with ExitStack() as tmp:
            a_ps = k.ps("e1_a_ps", [P, T], tmp)
            b_ps = k.ps("e1_b_ps", [P, T], tmp)
            out_ps = k.ps("e1_out_ps", [P, 2, NT, D], tmp)
            a_ready, b_ready, silu_done, hidden_done = (k.sem("e1_a_ready"), k.sem("e1_b_ready"), k.sem("e1_silu_done"),
                                                        k.sem("e1_hidden_done"))

            def up(pe, e, s, f, uses):
                pe.wait_ge(slot_loaded[s], 48 * (uses + 1))
                first = isinstance(e, int) and e == 0 and f == 0
                for w, ps, ready, used in ((w1, a_ps, a_ready, silu_done), (w2, b_ps, b_ready, hidden_done)):
                    if not first:
                        pe.wait_ge(used, 2 * e + f)
                    for h in range(2):
                        ins = nc.tensor.matmul(ps[:, h * HALF:(h + 1) * HALF], w[:, s, f * P:(f + 1) * P],
                                               k.x_T[:, h * HALF:(h + 1) * HALF], start=True, stop=True)
                    ins.then_inc(ready, 1)

            def down(pe, e, s, uses, part):
                if part == 0:
                    pe.wait_ge(hidden_done, 2 * e + 2)
                    pe.wait_ge(added[s], uses)
                for t in range(part * NT // 2, (part + 1) * NT // 2):
                    for f in range(2):
                        ins = nc.tensor.matmul(out_ps[:, s, t, :], hidden[:, s, f, t * P:(t + 1) * P], w3[:, s, f, :],
                                               start=(f == 0), stop=(f == 1))
                if part:
                    ins.then_inc(out_done, 1)

            def activate(act, e, s, f):
                act.wait_ge(a_ready, 2 * e + f + 1)
                act.wait_ge(hidden_done, 2 * e + f if isinstance(e, int) and e == 0 and f == 0 else 2 * e + f - 1)
                nc.scalar.activation(gate_act[:, f, :], a_ps[:], ACT.Silu,
                                     bias=b1[:, bass.ds(2 * e + f, 1)]).then_inc(silu_done, 1)

            def combine(dve, e, s, f):
                dve.wait_ge(b_ready, 2 * e + f + 1)
                dve.wait_ge(silu_done, 2 * e + f + 1)
                nc.vector.scalar_tensor_tensor(out=hidden[:, s, f, :], in0=b_ps[:], scalar=b2[:, bass.ds(2 * e + f, 1)],
                                               in1=gate_act[:, f, :], op0=ALU.add, op1=ALU.mult).then_inc(hidden_done, 1)

            def add_up(dve, e, s, uses):
                dve.wait_ge(out_done, e + 1)
                dve.wait_ge(added[1 - s], uses + s)
                for t in range(NT):
                    ins = nc.vector.scalar_tensor_tensor(out=acc[:, t, :], in0=out_ps[:, s, t, :],
                                                         scalar=gates[:, t, bass.ds(e, 1)], in1=acc[:, t, :],
                                                         op0=ALU.mult, op1=ALU.add)
                ins.then_inc(added[s], 1)

            with nc.Block() as block:
                @block.sync
                def _(sp):
                    with nc.sync.Fori(1, E // 2) as p:
                        for s in range(2):
                            sp.wait_ge(out_done, 2 * p + s - 1)
                            load(sp, 2 * p + s, s)

                def pe_step(pe, e, s, uses, prev_uses):
                    up(pe, e, s, 0, uses)
                    down(pe, e - 1, 1 - s, prev_uses, 0)
                    up(pe, e, s, 1, uses)
                    down(pe, e - 1, 1 - s, prev_uses, 1)

                @block.tensor
                def _(pe):
                    for f in range(2):
                        up(pe, 0, 0, f, 0)
                    pe_step(pe, 1, 1, 0, 0)
                    with nc.tensor.Fori(1, E // 2) as p:
                        pe_step(pe, 2 * p, 0, p, p - 1)
                        pe_step(pe, 2 * p + 1, 1, p, p)
                    for part in range(2):
                        down(pe, E - 1, 1, E // 2 - 1, part)

                @block.scalar
                def _(act):
                    activate(act, 0, 0, 0)
                    activate(act, 0, 0, 1)
                    activate(act, 1, 1, 0)
                    activate(act, 1, 1, 1)
                    with nc.scalar.Fori(1, E // 2) as p:
                        for s in range(2):
                            for f in range(2):
                                activate(act, 2 * p + s, s, f)

                @block.vector
                def _(dve):
                    for f in range(2):
                        combine(dve, 0, 0, f)
                    for f in range(2):
                        combine(dve, 1, 1, f)
                    add_up(dve, 0, 0, 0)
                    with nc.vector.Fori(1, E // 2) as p:
                        for f in range(2):
                            combine(dve, 2 * p, 0, f)
                        add_up(dve, 2 * p - 1, 1, p - 1)
                        for f in range(2):
                            combine(dve, 2 * p + 1, 1, f)
                        add_up(dve, 2 * p, 0, p)
                    add_up(dve, E - 1, 1, E // 2 - 1)
        residual_norm(k, "norm5", acc, store=store)


def decoder(nc, dram, out):
    with ExitStack() as ctx:
        k = Core(nc, dram, ctx)
        load_and_constants(k)
        context_projections(k)
        mamba(k)
        context_attention(k)
        experts0(k)
        self_attention(k)
        context_attention1(k)
        experts1(k, store=out.rearrange("b (t p) d -> p (b t) d", p=P))


TRANSPOSED = ["L0_attn_W_in", "L0_attn_W_xproj", "L0_attn_W_dt", "L0_attn_W_out", "L1_xattn_Wk", "L1_xattn_Wv",
              "L1_xattn_Wq", "L1_xattn_Wo", "L1_ffn_Wg",
              "L1_attn_a_q", "L1_attn_a_v"]
PER_FEATURE = ["L0_ffn_sb1", "L0_ffn_rb1", "L1_ffn_b1", "L1_ffn_b2"]


def kernel(**inputs):
    import numpy as _np
    import concourse.bacc as _bacc
    from concourse import mybir as _mybir
    from concourse.bass_utils import run_bass_kernel_spmd as _run

    laid = {n: _np.asarray(a) for n, a in inputs.items()}
    laid["x_T"] = laid["x"][0].T
    laid["ctx_T"] = laid.pop("ctx_1024")[0].T
    for n in TRANSPOSED:
        laid[n + "_T"] = laid.pop(n).T
    for n in ("L1_ffn_W1", "L1_ffn_W2", "L1_ffn_W3"):
        laid[n + "_T"] = laid.pop(n).transpose(0, 2, 1)
    for n in PER_FEATURE:
        laid[n + "_p"] = laid.pop(n).reshape(-1, 2, P).transpose(2, 0, 1).reshape(P, -1)
    nc = _bacc.Bacc("TRN2", target_bir_lowering=False, num_devices=1)
    arrays, dram = {}, {}
    for name, a in laid.items():
        a = _np.ascontiguousarray(a)
        arrays[name] = a
        dram[name] = nc.dram_tensor(name, a.shape, _mybir.dt.from_np(a.dtype), kind="ExternalInput").ap()
    out = nc.dram_tensor("out", (1, T, D), F32, kind="ExternalOutput").ap()
    decoder(nc, dram, out)
    r = _run(nc, [arrays], core_ids=[0])
    return r.results[0]["out"]
```

```python
from contextlib import ExitStack

import concourse.bass as bass
from concourse import mybir

F32 = mybir.dt.float32
BF16 = mybir.dt.bfloat16
ALU = mybir.AluOpType
ACT = mybir.ActivationFunctionType
AX = mybir.AxisListType

P = 128
D = 128
T = 1024
NT = T // P
HALF = 512
H = 16
HD = D // H
CTX = 6404
NCH = -(-CTX // P)
TAIL = CTX - (NCH - 1) * P
EPS = 1e-5

AUG = P
SHIFT = 4 * HD
Q_PARTS = (0, 0, 0, 1, 1, 2, 1, 2, 2)
K_PARTS = (0, 1, 2, 0, 1, 0, 2, 1, 2)
USED = len(Q_PARTS) * HD + 3


def slot(s):
    return HD * s if s < 4 else HD * s + 3


class Chain:

    def __init__(self, eng, sem):
        self.eng, self.sem, self.n = eng, sem, 0

    def __call__(self, ins):
        self.n += 1
        ins.then_inc(self.sem, 1)
        self.eng.wait_ge(self.sem, self.n)


class Core:

    def __init__(self, nc, dram, ctx):
        self.nc, self.dram, self.ctx = nc, dram, ctx
        self.norms = 0


    def sb(self, name, shape, dt=F32, ctx=None):
        return (ctx or self.ctx).enter_context(self.nc.sbuf_tensor("sb_" + name, shape, dt))

    def ps(self, name, shape, ctx, dt=F32):
        return ctx.enter_context(self.nc.psum_tensor("ps_" + name, shape, dt))

    def sem(self, name):
        return self.ctx.enter_context(self.nc.semaphore(name))

    def chain(self, dve):
        self.steps.eng = dve
        return self.steps


def load_and_constants(k):
    nc, d = k.nc, k.dram
    k.x_tok = k.sb("x_tok", [P, NT, D])
    k.x_T = k.sb("x_T", [P, T])
    k.ident = k.sb("ident", [P, P])
    k.ident_b = k.sb("ident_b", [P, P], BF16)
    k.ones_b = k.sb("ones_b", [P, P], BF16)
    k.steps = Chain(None, k.sem("vector_step"))
    k.var_ready, k.sd_ready = k.sem("norm_var_ready"), k.sem("norm_sd_ready")
    k.tile_ready, k.turned_ready = k.sem("norm_tile_ready"), k.sem("norm_turned_ready")
    k.consts_ready = k.sem("consts_ready")
    k.ident_zeroed = k.sem("ident_zeroed")
    k.ident_ready = k.sem("ident_ready")

    with nc.Block() as block:
        @block.gpsimd
        def _(pool):
            nc.gpsimd.memset(k.ident[:], 0.0).then_inc(k.ident_zeroed, 1)
            pool.wait_ge(k.ident_zeroed, 1)
            nc.gpsimd.affine_select(out=k.ident[:], in_=k.ident[:], compare_op=ALU.not_equal, fill=1.0, base=0,
                                    pattern=[[-1, P]], channel_multiplier=1).then_inc(k.ident_ready, 1)

        @block.vector
        def _(dve):
            nc.vector.memset(k.ones_b[:], 1.0)
            dve.wait_ge(k.ident_ready, 1)
            nc.vector.tensor_copy(k.ident_b[:], k.ident[:]).then_inc(k.consts_ready, 1)


def residual_norm(k, tag, branch, bias=None, store=None):
    nc = k.nc
    with ExitStack() as tmp:
        res = k.sb(tag + "_res", [P, NT, D], F32, tmp)
        stats = k.sb(tag + "_stats", [P, NT, 6], F32, tmp)
        mv = k.sb(tag + "_mv", [P, NT, 2], F32, tmp)
        var = k.sb(tag + "_var", [P, NT], F32, tmp)
        sd = k.sb(tag + "_sd", [P, NT], F32, tmp)
        rstd = k.sb(tag + "_rstd", [P, NT], F32, tmp)
        turned = k.ps(tag + "_turned", [P, T], tmp)
        stored = k.sem("stored") if store is not None else None
        n = k.norms
        k.norms += 1

        with nc.Block() as block:
            @block.vector
            def _(dve):
                link = k.chain(dve)
                for h in range(0, NT, 4):
                    ins = nc.vector.tensor_tensor(res[:, h:h + 4, :], branch[:, h:h + 4, :], k.x_tok[:, h:h + 4, :],
                                                  ALU.add)
                    if bias is None:
                        link(ins)
                    else:
                        link(ins)
                        link(nc.vector.tensor_tensor(res[:, h:h + 4, :], res[:, h:h + 4, :],
                                                     bias[:].unsqueeze(1).to_broadcast([P, 4, D]), ALU.add))
                for t in range(NT):
                    ins = nc.vector.bn_stats(stats[:, t, :], res[:, t, :])
                link(ins)
                for t in range(NT):
                    ins = nc.vector.bn_aggr(mv[:, t, :], stats[:, t, :])
                link(ins)
                nc.vector.tensor_scalar(var[:], mv[:, :, 1], EPS, None, ALU.add).then_inc(k.var_ready, 1)
                dve.wait_ge(k.sd_ready, n + 1)
                link(nc.vector.reciprocal(rstd[:], sd[:]))
                for t in range(NT):
                    nc.vector.tensor_scalar(k.x_tok[:, t, :], res[:, t, :], mv[:, t, 0:1], rstd[:, t:t + 1],
                                            ALU.subtract, ALU.mult).then_inc(k.tile_ready, 1)

            @block.scalar
            def _(act):
                act.wait_ge(k.var_ready, n + 1)
                nc.scalar.activation(sd[:], var[:], ACT.Sqrt).then_inc(k.sd_ready, 1)
                if store is None:
                    for h in range(2):
                        act.wait_ge(k.turned_ready, 2 * n + h + 1)
                        nc.scalar.copy(k.x_T[:, h * HALF:(h + 1) * HALF], turned[:, h * HALF:(h + 1) * HALF])

            @block.tensor
            def _(pe):
                if store is None:
                    for t in range(NT):
                        pe.wait_ge(k.tile_ready, NT * n + t + 1)
                        ins = nc.tensor.transpose(turned[:, t * P:(t + 1) * P], k.x_tok[:, t, :], k.ident[:])
                        if t % 4 == 3:
                            ins.then_inc(k.turned_ready, 1)

            @block.sync
            def _(sp):
                if store is not None:
                    for h in range(2):
                        sp.wait_ge(k.tile_ready, NT * n + 4 * h + 4)
                        sp.dma_start(store[:, 4 * h:4 * h + 4, :], k.x_tok[:, 4 * h:4 * h + 4, :]).then_inc(stored, 16)
                    sp.wait_ge(stored, 32)


def context_projections(k):
    nc, d = k.nc, k.dram
    k.key1_T = k.sb("key1_T", [P, CTX])
    k.val1 = k.sb("val1", [P, NCH, D])
    k.wk1 = k.sb("wk1", [P, D])
    k.wv1 = k.sb("wv1", [P, D])
    k.layer0 = k.ctx.enter_context(ExitStack())
    k.ctx_T = k.sb("ctx_T", [P, CTX], F32, k.layer0)
    k.key_stack = k.sb("key_stack", [AUG, NCH * P], BF16, k.layer0)
    k.val_ones = k.sb("val_ones", [P, NCH, 32], F32, k.layer0)
    k.x_loaded, k.layer1_loaded = k.sem("x_loaded"), k.sem("layer1_loaded")

    ctx = ExitStack()
    with ctx:
        w_kv = k.sb("w_kv", [P, 2 * HD], F32, ctx)
        k_tok = k.sb("k_tok", [P, NCH, HD], F32, ctx)
        part = [k.sb(f"k_part{i}", [P, NCH, HD], BF16, ctx) for i in range(3)]
        rest = [k.sb(f"k_rest{i}", [P, NCH, HD], F32, ctx) for i in range(2)]
        stack_tok = k.sb("k_stack_tok", [P, NCH, AUG], BF16, ctx)
        kv_ps = k.ps("kv_ps", [P, 64, 2 * HD], ctx)
        turn_ps = k.ps("k_turn_ps", [P, 4, 2 * HALF], ctx, BF16)

        kv_loaded = k.sem("w_kv_loaded")
        ctx_loaded = [k.sem(f"ctx_loaded{i}") for i in range(2)]
        kv_ready, stack_zeroed, stack_ready = k.sem("kv_ready"), k.sem("k_stack_zeroed"), k.sem("k_stack_ready")
        turned, used_dve, used_act = k.sem("k_turned"), k.sem("k_turn_used_dve"), k.sem("k_turn_used_act")
        TURNS = -(-NCH // 8)
        CUT = 26 * P

        def copy_turned(eng, copy, g, used):
            cols = min(8 * P, CTX - g * 8 * P)
            eng.wait_ge(turned, g + 1)
            copy(k.key_stack[:, g * 8 * P:g * 8 * P + cols], turn_ps[0:AUG, g % 4, 0:cols]).then_inc(used, 1)

        with nc.Block() as block:
            @block.sync
            def _(sp):
                sp.dma_start(w_kv[:], d["L0_xattn_w_kv"]).then_inc(kv_loaded, 16)
                sp.dma_start(k.ctx_T[:, 0:CUT], d["ctx_T"][:, 0:CUT]).then_inc(ctx_loaded[0], 16)
                sp.dma_start(k.x_T[:], d["x_T"]).then_inc(k.x_loaded, 16)
                sp.dma_start(k.wv1[:], d["L1_xattn_Wv_T"]).then_inc(k.layer1_loaded, 16)

            @block.scalar
            def _(act):
                act.dma_start(k.ctx_T[:, CUT:CTX], d["ctx_T"][:, CUT:CTX]).then_inc(ctx_loaded[1], 16)
                act.dma_start(k.x_tok[:], d["x"].rearrange("b (t p) d -> p (b t) d", p=P)).then_inc(k.x_loaded, 16)
                act.dma_start(k.wk1[:], d["L1_xattn_Wk_T"]).then_inc(k.layer1_loaded, 16)
                for g in range(1, TURNS, 2):
                    copy_turned(act, nc.scalar.copy, g, used_act)

            @block.tensor
            def _(pe):
                pe.wait_ge(kv_loaded, 16)
                for c in range(NCH):
                    if c in (0, CUT // P):
                        pe.wait_ge(ctx_loaded[1 if c else 0], 16)
                    n = P if c < NCH - 1 else TAIL
                    ins = nc.tensor.matmul(kv_ps[0:n, c, :], k.ctx_T[:, c * P:c * P + n], w_kv[:], start=True, stop=True)
                ins.then_inc(kv_ready, 1)
                pe.wait_ge(stack_ready, 1)
                for c in range(NCH):
                    n = P if c < NCH - 1 else TAIL
                    g = c // 8
                    if c % 8 == 0 and g >= 4:
                        pe.wait_ge(used_act if g % 2 else used_dve, (g - 4) // 2 + 1)
                    ins = nc.tensor.transpose(turn_ps[0:AUG, g % 4, (c % 8) * P:(c % 8) * P + n],
                                              stack_tok[0:n, c, :], k.ident_b[0:n, 0:n])
                    if c % 8 == 7 or c == NCH - 1:
                        ins.then_inc(turned, 1)

            @block.gpsimd
            def _(pool):
                nc.gpsimd.memset(stack_tok[:, :, SHIFT:SHIFT + 3], 1.0)
                nc.gpsimd.memset(stack_tok[:, :, USED:AUG], 0.0).then_inc(stack_zeroed, 1)
                nc.gpsimd.memset(k.key_stack[:, CTX:], 0.0)

            @block.vector
            def _(dve):
                link = k.chain(dve)
                full = NCH - 1
                nc.vector.memset(k_tok[:, full, :], 0.0)
                link(nc.vector.memset(k.val_ones[:], 0.0))
                nc.vector.memset(k.val_ones[:, 0:full, HD:HD + 1], 1.0)
                link(nc.vector.memset(k.val_ones[0:TAIL, full, HD:HD + 1], 1.0))
                dve.wait_ge(kv_ready, 1)
                nc.vector.tensor_copy(k_tok[:, 0:full, :], kv_ps[:, 0:full, 0:HD])
                link(nc.vector.tensor_copy(k_tok[0:TAIL, full, :], kv_ps[0:TAIL, full, 0:HD]))
                split(nc, link, k_tok[:], [p[:] for p in part], [r[:] for r in rest])
                dve.wait_ge(stack_zeroed, 1)
                for s, which in enumerate(K_PARTS):
                    ins = nc.vector.tensor_copy(stack_tok[:, :, slot(s):slot(s) + HD], part[which][:])
                ins.then_inc(stack_ready, 1)
                nc.vector.tensor_copy(k.val_ones[:, 0:full, 0:HD], kv_ps[:, 0:full, HD:2 * HD])
                nc.vector.tensor_copy(k.val_ones[0:TAIL, full, 0:HD], kv_ps[0:TAIL, full, HD:2 * HD])
                for g in range(0, TURNS, 2):
                    copy_turned(dve, nc.vector.tensor_copy, g, used_dve)


def split(nc, link, whole, part, rest):
    link(nc.vector.tensor_copy(part[0], whole))
    link(nc.vector.tensor_tensor(rest[0], whole, part[0], ALU.subtract))
    link(nc.vector.tensor_copy(part[1], rest[0]))
    link(nc.vector.tensor_tensor(rest[1], rest[0], part[1], ALU.subtract))
    link(nc.vector.tensor_copy(part[2], rest[1]))


def mamba(k):
    nc, d = k.nc, k.dram
    DI, NS, DR, KC = 2 * D, 16, D // 16, 4
    ROWS = DR + 2 * NS
    ctx = ExitStack()
    with ctx:
        w_in = k.sb("w_in_T", [P, 2 * DI], F32, ctx)
        w_conv = k.sb("w_conv", [P, 2, KC], F32, ctx)
        w_x = k.sb("w_xproj_T", [P, 2, ROWS], F32, ctx)
        w_dt = k.sb("w_dt_T", [DR, DI], F32, ctx)
        b_dt = k.sb("b_dt", [P, 2], F32, ctx)
        a_log = k.sb("a_log", [P, 2, NS], F32, ctx)
        a_neg = k.sb("a_neg", [P, 2, NS], F32, ctx)
        d_skip = k.sb("d_skip", [P, 2], F32, ctx)
        w_out = k.sb("w_out_T", [P, 2, D], F32, ctx)
        diag = k.sb("d_diag", [P, 2, P], F32, ctx)
        PAD = KC - 1
        xpad = k.sb("xpad", [P, 2, PAD + T], F32, ctx)
        zs = k.sb("z_silu", [P, 2, T], F32, ctx)
        conv = k.sb("conv", [P, 2, T], F32, ctx)
        xc = k.sb("xc", [P, 2, T], F32, ctx)
        delta = k.sb("delta", [P, 2, T], F32, ctx)
        u = k.sb("u", [P, 2, T], F32, ctx)
        dbc_all = k.sb("dbc", [P, T], F32, ctx)
        dbc = dbc_all[0:ROWS, :]
        bc_rows = k.sb("bc_rows", [P, NS, T], BF16, ctx)
        pick = k.sb("bc_pick", [P, 2, P], BF16, ctx)
        early = k.val1[:].rearrange("p c e -> p (c e)")
        decay = early[:, 0:2 * T].rearrange("p (s t) -> p s t", s=2)
        c_all = early[:, 2 * T:4 * T].rearrange("p (s t) -> p s t", s=2)
        state = k.sb("state", [P, 2, T], F32, ctx)
        dbc_part = [state[0:ROWS, i // 2, (i % 2) * HALF:(i % 2 + 1) * HALF].bitcast(BF16) for i in range(3)]
        dbc_rest = [decay[0:ROWS, i, :] for i in range(2)]
        read = xpad[:, :, 0:T]
        soft = drive = conv

        loaded = k.sem("mamba_loaded")
        xz_ready, xpad_ready, conv_ready = k.sem("xz_ready"), k.sem("xpad_ready"), k.sem("conv_ready")
        xc_ready, z_used, dbc_ready, dbc_copied = k.sem("xc_ready"), k.sem("z_used"), k.sem("dbc_ready"), k.sem("dbc_copied")
        dbc_split, dlt_ready, log_ready = k.sem("dbc_split"), k.sem("dlt_ready"), k.sem("log_ready")
        act_step, a_exp = k.sem("mamba_act_step"), k.sem("a_exp")
        rows_moved, pick_set, rows_zeroed = k.sem("rows_moved"), k.sem("pick_set"), k.sem("bc_rows_zeroed")
        b_ready, c_ready, b_used, c_copied = k.sem("b_ready"), k.sem("c_ready"), k.sem("b_used"), k.sem("c_copied")
        decay_ready, read_ready, y_added = k.sem("decay_ready"), k.sem("read_ready"), k.sem("y_added")
        scanned = k.sem("scanned")
        gated, out_ready = k.sem("y_gated"), k.sem("mamba_out_ready")

        with ExitStack() as front:
            xz = [k.ps(f"xz{c}", [P, T], front) for c in range(4)]
            with nc.Block() as block:
                @block.sync
                def _(sp):
                    sp.dma_start(w_in[:], d["L0_attn_W_in_T"]).then_inc(loaded, 16)
                    sp.dma_start(w_conv[:], d["L0_attn_W_conv"].rearrange("(s p) o k -> p s (o k)", p=P)).then_inc(loaded, 16)
                    sp.dma_start(w_x[:], d["L0_attn_W_xproj_T"].rearrange("(s p) r -> p s r", p=P)).then_inc(loaded, 16)
                    sp.dma_start(w_dt[:], d["L0_attn_W_dt_T"]).then_inc(loaded, 16)
                    sp.dma_start(w_out[:], d["L0_attn_W_out_T"].rearrange("(s p) m -> p s m", p=P)).then_inc(loaded, 16)
                    with nc.allow_non_contiguous_dma(reason="two floats to a partition"):
                        sp.dma_start(b_dt[:], d["L0_attn_b_dt"].rearrange("(s p) -> p s", p=P)).then_inc(loaded, 16)
                        sp.dma_start(d_skip[:], d["L0_attn_D"].rearrange("(s p) -> p s", p=P)).then_inc(loaded, 16)
                    sp.dma_start(a_log[:], d["L0_attn_A_log"].rearrange("(s p) n -> p s n", p=P)).then_inc(loaded, 16)
                    sp.wait_ge(dbc_split, 1)
                    sp.wait_ge(rows_zeroed, 1)
                    for i in range(3):
                        for base, first in ((0, DR), (3, DR + NS)):
                            sp.dma_start(bc_rows[base + i:base + i + 1, :, :],
                                         dbc_part[i][first:first + NS, :]).then_inc(rows_moved, 16)
                    sp.wait_ge(rows_moved, 16 * 6)

                @block.gpsimd
                def _(pool):
                    nc.gpsimd.memset(pick[:], 1.0).then_inc(pick_set, 1)
                    pool.wait_ge(pick_set, 1)
                    nc.gpsimd.affine_select(out=pick[:, 0, :], in_=pick[:, 0, :], compare_op=ALU.is_ge, fill=0.0, base=2,
                                            pattern=[[0, P]], channel_multiplier=-1)
                    nc.gpsimd.affine_select(out=pick[:, 1, :], in_=pick[:, 1, :], compare_op=ALU.is_ge, fill=0.0, base=-3,
                                            pattern=[[0, P]], channel_multiplier=1).then_inc(pick_set, 1)
                    pool.wait_ge(pick_set, 2)
                    nc.gpsimd.affine_select(out=pick[:, 1, :], in_=pick[:, 1, :], compare_op=ALU.is_ge, fill=0.0, base=5,
                                            pattern=[[0, P]], channel_multiplier=-1)
                    nc.gpsimd.memset(bc_rows[:], 0.0).then_inc(rows_zeroed, 1)

                @block.tensor
                def _(pe):
                    pe.wait_ge(loaded, 16 * 8)
                    pe.wait_ge(k.x_loaded, 32)
                    for c in range(4):
                        for h in range(2):
                            ins = nc.tensor.matmul(xz[c][:, h * HALF:(h + 1) * HALF], w_in[:, c * P:(c + 1) * P],
                                                   k.x_T[:, h * HALF:(h + 1) * HALF], start=True, stop=True)
                        ins.then_inc(xz_ready, 1)
                    pe.wait_ge(xpad_ready, 1)
                    pe.wait_ge(xc_ready, 2)
                    for h in range(2):
                        for s in range(2):
                            ins = nc.tensor.matmul(xz[0][0:ROWS, h * HALF:(h + 1) * HALF], w_x[:, s, :],
                                                   xc[:, s, h * HALF:(h + 1) * HALF], start=(s == 0), stop=(s == 1))
                    ins.then_inc(dbc_ready, 1)
                    pe.wait_ge(dbc_copied, 1)
                    pe.wait_ge(z_used, 2)
                    for s in range(2):
                        for h in range(2):
                            ins = nc.tensor.matmul(xz[2 + s][:, h * HALF:(h + 1) * HALF], w_dt[:, s * P:(s + 1) * P],
                                                   dbc[0:DR, h * HALF:(h + 1) * HALF], start=True, stop=True)
                        ins.then_inc(dlt_ready, 1)

                @block.scalar
                def _(act):
                    link = Chain(act, act_step)
                    for s in range(2):
                        act.wait_ge(xz_ready, s + 1)
                        nc.scalar.copy(xpad[:, s, PAD:PAD + T], xz[s][:]).then_inc(xpad_ready, 1)
                    for s in range(2):
                        act.wait_ge(xz_ready, 3 + s)
                        nc.scalar.activation(zs[:, s, :], xz[2 + s][:], ACT.Silu).then_inc(z_used, 1)
                    for s in range(2):
                        act.wait_ge(conv_ready, s + 1)
                        nc.scalar.activation(xc[:, s, :], conv[:, s, :], ACT.Silu).then_inc(xc_ready, 1)
                    act.wait_ge(loaded, 16 * 8)
                    nc.scalar.activation(a_neg[:], a_log[:], ACT.Exp).then_inc(a_exp, 1)
                    for s in range(2):
                        act.wait_ge(dlt_ready, s + 1)
                        link(nc.scalar.activation(soft[:, s, :], xz[2 + s][:], ACT.Abs, bias=b_dt[:, s:s + 1]))
                    for s in range(2):
                        link(nc.scalar.activation(soft[:, s, :], soft[:, s, :], ACT.Exp, scale=-1.0))
                    for s in range(2):
                        nc.scalar.activation(soft[:, s, :], soft[:, s, :], ACT.Ln, bias=1.0).then_inc(log_ready, 1)

                @block.vector
                def _(dve):
                    link = k.chain(dve)
                    link(nc.vector.memset(xpad[:, :, 0:PAD], 0.0))
                    dve.wait_ge(loaded, 16 * 8)
                    dve.wait_ge(k.consts_ready, 1)
                    for s in range(2):
                        nc.vector.tensor_scalar(diag[:, s, :], k.ident[:], d_skip[:, s:s + 1], None, ALU.mult)
                    for s in range(2):
                        dve.wait_ge(xpad_ready, s + 1)
                        link(nc.vector.tensor_scalar(conv[:, s, :], xpad[:, s, 0:T], w_conv[:, s, 0:1], None, ALU.mult))
                        for j in range(1, KC):
                            ins = nc.vector.scalar_tensor_tensor(
                                out=conv[:, s, :], in0=xpad[:, s, j:j + T], scalar=w_conv[:, s, j:j + 1],
                                in1=conv[:, s, :], op0=ALU.mult, op1=ALU.add)
                            if j < KC - 1:
                                link(ins)
                        ins.then_inc(conv_ready, 1)
                    dve.wait_ge(dbc_ready, 1)
                    nc.vector.tensor_copy(dbc[:], xz[0][0:ROWS, :]).then_inc(dbc_copied, 1)
                    dve.wait_ge(dbc_copied, 1)
                    split(nc, link, dbc, dbc_part, dbc_rest)
                    nc.vector.engine_nop().then_inc(dbc_split, 1)
                    dve.wait_ge(a_exp, 1)
                    link(nc.vector.tensor_scalar(a_neg[:], a_neg[:], -1.0, None, ALU.mult))
                    for s in range(2):
                        dve.wait_ge(log_ready, s + 1)
                        link(nc.vector.tensor_scalar(delta[:, s, :], xz[2 + s][:], b_dt[:, s:s + 1], 0.0, ALU.add, ALU.max))
                        link(nc.vector.tensor_tensor(delta[:, s, :], delta[:, s, :], soft[:, s, :], ALU.add))
                        nc.vector.tensor_tensor(u[:, s, :], delta[:, s, :], xc[:, s, :], ALU.mult)

        y = [k.ps(f"y{s}", [P, T], ctx) for s in range(2)]
        b_all = k.ps("b_all", [P, T], ctx)
        out_ps = b_all[:].rearrange("p (t e) -> p t e", t=NT)
        with ExitStack() as mid:
            c_ps = k.ps("c_all", [P, T], mid)

            def spread(pe, dst, which, n, ready):
                for h in range(2):
                    ins = nc.tensor.matmul(dst[:, h * HALF:(h + 1) * HALF], pick[:, which, :],
                                           bc_rows[:, n, h * HALF:(h + 1) * HALF], start=True, stop=True)
                ins.then_inc(ready, 1)

            def next_b(pe, n):
                pe.wait_ge(b_used, 2 * n)
                spread(pe, b_all, 0, n, b_ready)

            def next_c(pe, n):
                pe.wait_ge(c_copied, n)
                spread(pe, c_ps, 1, n, c_ready)

            def add_read(pe, n, s):
                pe.wait_ge(read_ready, 2 * n + s + 1)
                for h in range(2):
                    ins = nc.tensor.matmul(y[s][:, h * HALF:(h + 1) * HALF], k.ident[:],
                                           read[:, s, h * HALF:(h + 1) * HALF], start=False, stop=True,
                                           skip_group_check=True)
                ins.then_inc(y_added, 1)

            def decay_and_c(act, n, parity, first):
                for s in range(2):
                    if not first:
                        act.wait_ge(scanned, 2 * n + s - 1)
                    nc.scalar.activation(decay[:, s, :], delta[:, s, :], ACT.Exp,
                                         scale=a_neg[:, s, bass.ds(n, 1)]).then_inc(decay_ready, 1)
                act.wait_ge(c_ready, n + 1)
                if not (isinstance(n, int) and n < 2):
                    act.wait_ge(read_ready, 2 * n - 2)
                nc.scalar.copy(c_all[:, parity, :], c_ps[:]).then_inc(c_copied, 1)

            def scan(dve, n, first):
                dve.wait_ge(b_ready, n + 1)
                for s in range(2):
                    if not first:
                        dve.wait_ge(scanned, 2 * n + s - 1)
                    nc.vector.tensor_tensor(drive[:, s, :], b_all[:], u[:, s, :], ALU.mult).then_inc(b_used, 1)
                for s in range(2):
                    dve.wait_ge(b_used, 2 * n + s + 1)
                    dve.wait_ge(decay_ready, 2 * n + s + 1)
                    if not first:
                        dve.wait_ge(read_ready, 2 * n + s - 1)
                    nc.vector.tensor_tensor_scan(state[:, s, :], decay[:, s, :], drive[:, s, :], 0.0,
                                                 ALU.mult, ALU.add).then_inc(scanned, 1)

            def read_out(pool, n, parity, first):
                pool.wait_ge(c_copied, n + 1)
                for s in range(2):
                    pool.wait_ge(scanned, 2 * n + s + 1)
                    if not first:
                        pool.wait_ge(y_added, 2 * n + s - 1)
                    nc.gpsimd.tensor_tensor(read[:, s, :], state[:, s, :], c_all[:, parity, :], ALU.mult).then_inc(read_ready, 1)

            with nc.Block() as block:
                @block.tensor
                def _(pe):
                    spread(pe, b_all, 0, 0, b_ready)
                    spread(pe, c_ps, 1, 0, c_ready)
                    for s in range(2):
                        for h in range(2):
                            nc.tensor.matmul(y[s][:, h * HALF:(h + 1) * HALF], diag[:, s, :],
                                             xc[:, s, h * HALF:(h + 1) * HALF], start=True, stop=True,
                                             skip_group_check=True)
                    next_b(pe, 1)
                    next_c(pe, 1)
                    with nc.tensor.Fori(1, NS - 1) as n:
                        add_read(pe, n - 1, 0)
                        next_b(pe, n + 1)
                        add_read(pe, n - 1, 1)
                        next_c(pe, n + 1)
                    for n in (NS - 2, NS - 1):
                        for s in range(2):
                            add_read(pe, n, s)
                    pe.wait_ge(gated, 2)
                    for t in range(NT):
                        for s in range(2):
                            ins = nc.tensor.matmul(out_ps[:, t, :], state[:, s, t * P:(t + 1) * P], w_out[:, s, :],
                                                   start=(s == 0), stop=(s == 1))
                    ins.then_inc(out_ready, 1)

                @block.scalar
                def _(act):
                    nc.scalar.preload_act_table(ACT.Exp)
                    decay_and_c(act, 0, 0, True)
                    decay_and_c(act, 1, 1, False)
                    with nc.scalar.Fori(1, NS // 2) as p:
                        for parity in range(2):
                            decay_and_c(act, 2 * p + parity, parity, False)

                @block.vector
                def _(dve):
                    scan(dve, 0, True)
                    with nc.vector.Fori(1, NS) as n:
                        scan(dve, n, False)
                    for s in range(2):
                        dve.wait_ge(y_added, 2 * NS - 1 + s)
                        nc.vector.tensor_tensor(state[:, s, :], y[s][:], zs[:, s, :], ALU.mult).then_inc(gated, 1)

                @block.gpsimd
                def _(pool):
                    read_out(pool, 0, 0, True)
                    read_out(pool, 1, 1, False)
                    with nc.gpsimd.Fori(1, NS // 2) as p:
                        for parity in range(2):
                            read_out(pool, 2 * p + parity, parity, False)
        residual_norm(k, "norm0", out_ps)


def stack_queries(nc, link, whole, part, rest, stack, parts):
    split(nc, link, whole, part, rest)
    for s, which in enumerate(parts):
        ins = nc.vector.tensor_copy(stack[:, :, slot(s):slot(s) + HD], part[which])
    return ins


def negated_maximum(nc, link, partial, neg, rests, part3):
    link(nc.vector.tensor_reduce(neg, partial, AX.X, ALU.max, negate=True))
    link(nc.vector.tensor_copy(part3[:, :, 0], neg))
    link(nc.vector.tensor_tensor(rests[0], neg, part3[:, :, 0], ALU.subtract))
    link(nc.vector.tensor_copy(part3[:, :, 1], rests[0]))
    link(nc.vector.tensor_tensor(rests[1], rests[0], part3[:, :, 1], ALU.subtract))
    return nc.vector.tensor_copy(part3[:, :, 2], rests[1])


def context_attention(k):
    nc, d = k.nc, k.dram
    BLK = H * P
    JOBS = BLK // HALF
    WIDE = 2 * HALF
    RANGES = [(c0, min(WIDE, CTX - c0)) for c0 in range(0, CTX, WIDE)]
    NR = len(RANGES)
    UNITS = H * NR
    ctx = ExitStack()
    with ctx:
        stack_T = k.sb("q_stack_T", [AUG, NT, BLK], BF16, ctx)
        gathered = k.sb("gathered", [P, NT, HALF], F32, ctx)
        w_out = k.sb("w_concat", [P, D], F32, ctx)
        with ExitStack() as tmp:
            w_q = k.sb("w_q", [P, D], F32, tmp)
            early = k.val1[:].rearrange("p c e -> p (c e)")
            q_tok, *rest = [early[:, i * T:(i + 1) * T].rearrange("p (a b) -> p a b", b=HD) for i in range(3)]
            part = [k.sb(f"q_part{i}", [P, NT * H, HD], BF16, tmp) for i in range(3)]
            stack = k.sb("q_stack", [P, NT * H, AUG], BF16, tmp)
            q_ps = k.ps("q_ps", [P, NT * D], tmp)
            turn_ps = k.ps("q_turn_ps", [P, 4, 8 * P], tmp, BF16)
            loaded, q_ready = k.sem("wq_loaded"), k.sem("q_ready")
            stack_ready, turned, used_dve, used_act = (k.sem("q_stack_ready"), k.sem("q_turned"),
                                                       k.sem("q_turn_used_dve"), k.sem("q_turn_used_act"))
            with nc.Block() as block:
                @block.sync
                def _(sp):
                    sp.dma_start(w_q[:], d["L0_xattn_w_q"]).then_inc(loaded, 16)
                    sp.dma_start(w_out[:], d["L0_xattn_w_concat"]).then_inc(loaded, 16)

                @block.tensor
                def _(pe):
                    pe.wait_ge(loaded, 32)
                    for t in range(NT):
                        ins = nc.tensor.matmul(q_ps[:, t * D:(t + 1) * D], k.x_T[:, t * P:(t + 1) * P], w_q[:],
                                               start=True, stop=True)
                    ins.then_inc(q_ready, 1)
                    pe.wait_ge(stack_ready, 1)
                    for g in range(NT * H // 8):
                        if g >= 4:
                            pe.wait_ge(used_act if g % 2 else used_dve, (g - 4) // 2 + 1)
                        for j in range(8):
                            ins = nc.tensor.transpose(turn_ps[0:AUG, g % 4, j * P:(j + 1) * P],
                                                      stack[:, g * 8 + j, :], k.ident_b[:])
                        ins.then_inc(turned, 1)

                @block.vector
                def _(dve):
                    link = k.chain(dve)
                    nc.vector.memset(stack[:, :, USED:AUG], 0.0)
                    link(nc.vector.memset(stack[:, :, SHIFT:SHIFT + 3], 0.0))
                    dve.wait_ge(q_ready, 1)
                    link(nc.vector.tensor_scalar(q_tok.rearrange("p a b -> p (a b)"), q_ps[:], float(HD) ** -0.5,
                                                 None, ALU.mult))
                    stack_queries(nc, link, q_tok, [x[:] for x in part], rest, stack,
                                  Q_PARTS).then_inc(stack_ready, 1)
                    for g in range(0, NT * H // 8, 2):
                        dve.wait_ge(turned, g + 1)
                        nc.vector.tensor_copy(stack_T[:, g // 2, 0:8 * P], turn_ps[0:AUG, g % 4, :]).then_inc(used_dve, 1)

                @block.scalar
                def _(act):
                    for g in range(1, NT * H // 8, 2):
                        act.wait_ge(turned, g + 1)
                        nc.scalar.copy(stack_T[:, g // 2, 8 * P:16 * P], turn_ps[0:AUG, g % 4, :]).then_inc(used_act, 1)
                    nc.scalar.preload_act_table(ACT.Exp)

        with ExitStack() as tmp:
            probs = k.sb("probs", [P, 3, JOBS, HALF], F32, tmp)
            partial = k.sb("max_partial", [P, H, NR], F32, tmp)
            neg = k.sb("neg_max", [P, H], F32, tmp)
            rests = [k.sb(f"neg_rest{i}", [P, H], F32, tmp) for i in range(2)]
            part3 = k.sb("neg_part", [P, H, 3], BF16, tmp)
            score_ps = k.ps("score_ps", [P, 3, HALF], tmp)
            max_ps = k.ps("max_ps", [P, 2, WIDE], tmp)
            acc_ps = k.ps("acc_ps", [P, HALF], tmp)
            shift_ps = max_ps[:, 0, :].bitcast(BF16)
            steps_before = k.steps.n
            q_ready = k.sem("q_block_ready")
            unit_ready, unit_used, parts_ready, shift_turned = (k.sem("max_ready"), k.sem("max_used"),
                                                                k.sem("neg_parts_ready"), k.sem("shift_turned"))
            score_ready, exp_done, pv_done, acc_used = (k.sem("score_ready"), k.sem("exp_done"), k.sem("pv_done"),
                                                        k.sem("acc_used"))
            job_ready, job_copied = k.sem("layer1_job_ready"), k.sem("layer1_job_copied")
            EXPS = NCH * JOBS
            LINKED = 5

            def columns(blk, c0, n):
                x = stack_T[:, at(blk), c0:c0 + n]
                return x if isinstance(blk, int) else x.rearrange("p o c -> p (o c)")

            def max_unit(pe, blk, u):
                h, r = u // NR, u % NR
                if not (isinstance(blk, int) and blk == 0 and u < 2):
                    pe.wait_ge(unit_used, blk * UNITS + u - 1)
                c0, cols = RANGES[r]
                for a in range(0, cols, HALF):
                    n = min(HALF, cols - a)
                    ins = nc.tensor.matmul(max_ps[:, u % 2, a:a + n], columns(blk, h * P, P),
                                           k.key_stack[:, c0 + a:c0 + a + n], start=True, stop=True)
                ins.then_inc(unit_ready, 1)

            def turn_shift(pe, blk):
                pe.wait_ge(parts_ready, blk + 1)
                for h in range(H):
                    ins = nc.tensor.transpose(shift_ps[0:3, h * P:(h + 1) * P], part3[:, h, :], k.ident_b[:])
                ins.then_inc(shift_turned, 1)

            key_jobs = [(c0, min(HALF, CTX - c0)) for c0 in range(0, CTX, HALF)]
            val_jobs = [(c, min(4, NCH - 1 - c)) for c in range(0, NCH - 1, 4)] + [(NCH - 1, 1)]
            JOBS1 = len(key_jobs) + len(val_jobs)

            def layer1_job(pe, i):
                if i >= 3:
                    pe.wait_ge(job_copied, i - 2)
                bank = score_ps[:, i % 3, :]
                if i < len(key_jobs):
                    c0, cols = key_jobs[i]
                    ins = nc.tensor.matmul(bank[:, 0:cols], k.wk1[:], k.ctx_T[:, c0:c0 + cols], start=True, stop=True)
                else:
                    c, m = val_jobs[i - len(key_jobs)]
                    n = P if c < NCH - 1 else TAIL
                    for j in range(m):
                        ins = nc.tensor.matmul(bank[0:n, j * D:(j + 1) * D], k.ctx_T[:, (c + j) * P:(c + j) * P + n],
                                               k.wv1[:], start=True, stop=True)
                ins.then_inc(job_ready, 1)

            def copy_layer1_job(act, i):
                act.wait_ge(job_ready, i + 1)
                bank = score_ps[:, i % 3, :]
                if i < len(key_jobs):
                    c0, cols = key_jobs[i]
                    ins = nc.scalar.copy(k.key1_T[:, c0:c0 + cols], bank[:, 0:cols])
                else:
                    c, m = val_jobs[i - len(key_jobs)]
                    n = P if c < NCH - 1 else TAIL
                    ins = nc.scalar.copy(k.val1[0:n, c:c + m, :], bank[0:n, 0:m * D].rearrange("p (j e) -> p j e", j=m))
                ins.then_inc(job_copied, 1)

            def weigh(pe, blk, v):
                if v == 0 and not (isinstance(blk, int) and blk == 0):
                    pe.wait_ge(acc_used, blk)
                pe.wait_ge(exp_done, blk * EXPS + JOBS * (v + 1))
                for j in range(JOBS):
                    ins = nc.tensor.matmul(acc_ps[32 * j:32 * j + 32, :], k.val_ones[:, v, :],
                                           probs[:, v % 3, j, :], start=(v == 0), stop=(v == NCH - 1))
                ins.then_inc(pv_done, 1)

            LAST = NCH - 4
            extra = UNITS - 2 * (LAST + 1)
            after_weighing = {(LAST + 1) * (i + 1) // extra - 1 for i in range(extra)}

            def attend(pe, blk, with_max):
                pe.wait_ge(q_ready, blk + 1)
                u = 0
                for c in range(NCH):
                    for j in range(JOBS):
                        e = c * JOBS + j
                        if not (isinstance(blk, int) and blk == 0 and e < 3):
                            pe.wait_ge(exp_done, blk * EXPS + e - 2)
                        nc.tensor.matmul(score_ps[:, e % 3, :], k.key_stack[:, c * P:(c + 1) * P],
                                         columns(blk, j * HALF, HALF), start=True, stop=True).then_inc(score_ready, 1)
                        if with_max and c <= LAST and j in (0, 2):
                            max_unit(pe, blk + 1, u)
                            u += 1
                    if c >= 1:
                        weigh(pe, blk, c - 1)
                    elif not (isinstance(blk, int) and blk == 0):
                        weigh(pe, blk - 1, NCH - 1)
                    if with_max and c in after_weighing:
                        max_unit(pe, blk + 1, u)
                        u += 1
                    if with_max and c == NCH - 2:
                        turn_shift(pe, blk + 1)

            def take_acc(act, blk):
                act.wait_ge(pv_done, (blk + 1) * NCH)
                dst = gathered[:, at(blk), :]
                nc.scalar.copy(dst if isinstance(blk, int) else dst.rearrange("p o c -> p (o c)"),
                               acc_ps[:]).then_inc(acc_used, 1)

            def exponentiate(act, blk):
                for c in range(NCH):
                    n = P if c < NCH - 1 else TAIL
                    if not (isinstance(blk, int) and blk == 0 and c < 3):
                        act.wait_ge(pv_done, blk * NCH + c - 2)
                    for j in range(JOBS):
                        e = c * JOBS + j
                        act.wait_ge(score_ready, blk * EXPS + e + 1)
                        nc.scalar.activation(probs[0:n, c % 3, j, :], score_ps[0:n, e % 3, :], ACT.Exp).then_inc(exp_done, 1)
                    if c == 0 and not (isinstance(blk, int) and blk == 0):
                        take_acc(act, blk - 1)

            def maxima(dve, blk):
                for u in range(UNITS):
                    h, r = u // NR, u % NR
                    dve.wait_ge(unit_ready, blk * UNITS + u + 1)
                    nc.vector.tensor_reduce(partial[:, h, r:r + 1], max_ps[:, u % 2, 0:RANGES[r][1]], AX.X,
                                            ALU.max).then_inc(unit_used, 1)
                dve.wait_ge(unit_used, (blk + 1) * UNITS)
                link = k.chain(dve)
                link.n = steps_before + blk * LINKED
                negated_maximum(nc, link, partial[:], neg[:], [x[:] for x in rests], part3[:]).then_inc(parts_ready, 1)
                dve.wait_ge(shift_turned, blk + 1)
                dst = stack_T[SHIFT:SHIFT + 3, at(blk), :]
                nc.vector.tensor_copy(dst if isinstance(blk, int) else dst.rearrange("p o c -> p (o c)"),
                                      shift_ps[0:3, :]).then_inc(q_ready, 1)
                dve.wait_ge(q_ready, blk + 1)

            def at(blk):
                return blk if isinstance(blk, int) else bass.ds(blk, 1)

            with nc.Block() as block:
                @block.tensor
                def _(pe):
                    pe.wait_ge(k.layer1_loaded, 32)
                    for u in range(UNITS):
                        max_unit(pe, 0, u)
                        for i in range(JOBS1 * u // UNITS, JOBS1 * (u + 1) // UNITS):
                            layer1_job(pe, i)
                    turn_shift(pe, 0)
                    pe.wait_ge(job_copied, JOBS1)
                    attend(pe, 0, True)
                    with nc.tensor.Fori(1, NT - 1) as i:
                        attend(pe, i, True)
                    attend(pe, NT - 1, False)
                    weigh(pe, NT - 1, NCH - 1)

                @block.scalar
                def _(act):
                    for i in range(JOBS1):
                        copy_layer1_job(act, i)
                    exponentiate(act, 0)
                    with nc.scalar.Fori(1, NT) as i:
                        exponentiate(act, i)
                    take_acc(act, NT - 1)

                @block.vector
                def _(dve):
                    maxima(dve, 0)
                    with nc.vector.Fori(1, NT) as i:
                        maxima(dve, i)
                    k.steps.n = steps_before + NT * LINKED

        with ExitStack() as tmp:
            merged = k.sb("merged", [P, NT, D], F32, tmp)
            k.out_ps = k.ps("xattn0_out_ps", [P, NT, D], tmp)
            finish_heads(k, "xattn0", gathered, merged, w_out, k.out_ps, by_tile=True)
            residual_norm(k, "norm1", k.out_ps)
    k.layer0.close()


def finish_heads(k, tag, gathered, merged, w_out, out_ps, by_tile):
    nc = k.nc
    with ExitStack() as tmp:
        turn_ps = k.ps(tag + "_turn_ps", [P, 4, 4, P], tmp)
        recip = k.sb(tag + "_recip", [P, 4, 4, 4], F32, tmp)
        turned, used, recip_ready = k.sem(tag + "_turned"), k.sem(tag + "_turn_used"), k.sem(tag + "_recip")
        per_m = gathered.shape[2] // P
        M = gathered.shape[1]
        GROUPS = M * per_m // 4
        with nc.Block() as block:
            @block.tensor
            def _(pe):
                for g in range(GROUPS):
                    if g >= 4:
                        pe.wait_ge(used, g - 3)
                    for i in range(4):
                        w = g * 4 + i
                        m, s = w // per_m, w % per_m
                        ins = nc.tensor.transpose(turn_ps[:, g % 4, i, :], gathered[:, m, s * P:(s + 1) * P], k.ident[:])
                    ins.then_inc(turned, 1)
            @block.vector
            def _(dve):
                for g in range(GROUPS):
                    dve.wait_ge(turned, g + 1)
                    rows = turn_ps[:, g % 4, :, :].rearrange("p i (q r) -> p i q r", q=4)
                    nc.vector.reciprocal(recip[:, g % 4, :, :], rows[:, :, :, HD]).then_inc(recip_ready, 1)
                    dve.wait_ge(recip_ready, g + 1)
                    for i in range(4):
                        src = turn_ps[:, g % 4, i, :].rearrange("p (q r) -> p q r", q=4)[:, :, 0:HD]
                        w = g * 4 + i
                        m, s = w // per_m, w % per_m
                        if by_tile:
                            dst = merged[:, m, :].rearrange("p (q s e) -> p s q e", q=4, s=4)[:, s, :, :]
                        else:
                            dst = merged[:].rearrange("p (q s) (h e) -> p s h q e", s=2, h=H)[:, s, m, :, :]
                        ins = nc.vector.tensor_tensor(dst, src, recip[:, g % 4, i, :].unsqueeze(2).to_broadcast([P, 4, HD]),
                                                      ALU.mult)
                    ins.then_inc(used, 1)
    project(k, tag, merged, w_out, out_ps)


def project(k, tag, merged, w_out, out_ps):
    nc = k.nc
    with ExitStack() as tmp:
        back_ps = k.ps(tag + "_back_ps", [P, T], tmp)
        merged_T = k.sb(tag + "_merged_T", [P, T], F32, tmp)
        back, back_copied = k.sem(tag + "_back"), k.sem(tag + "_back_copied")
        with nc.Block() as block:
            @block.tensor
            def _(pe):
                for t in range(NT):
                    ins = nc.tensor.transpose(back_ps[:, t * P:(t + 1) * P], merged[:, t, :], k.ident[:])
                    if t % 4 == 3:
                        ins.then_inc(back, 1)
                for t in range(NT):
                    if t % 4 == 0:
                        pe.wait_ge(back_copied, t // 4 + 1)
                    nc.tensor.matmul(out_ps[:, t, :], merged_T[:, t * P:(t + 1) * P], w_out[:], start=True, stop=True)

            @block.scalar
            def _(act):
                for h in range(2):
                    act.wait_ge(back, h + 1)
                    nc.scalar.copy(merged_T[:, h * HALF:(h + 1) * HALF],
                                   back_ps[:, h * HALF:(h + 1) * HALF]).then_inc(back_copied, 1)


def choose(nc, link, values, width, pads, n_top, lowest, top8, wanted, left, chosen):
    mark = 2.0 * lowest
    for t in range(NT):
        ins = nc.vector.max(top8[:, t, :], values[:, t, :])
    link(ins)
    link(nc.vector.tensor_copy(wanted[:, :, 0:n_top], top8[:, :, 0:n_top]))
    for t in range(NT):
        ins = nc.vector.match_replace(left[:, t, :], wanted[:, t, :], values[:, t, :], mark)
    link(ins)
    link(nc.vector.tensor_scalar(chosen, left[:, :, 0:width], mark, None, ALU.is_equal))


def experts0(k):
    nc, d = k.nc, k.dram
    E, F, TOP = 15, 2 * P, 3
    STEPS = E + 2
    PADS = 8 - TOP
    LOWEST = -1.0
    ctx = ExitStack()
    with ctx:
        w1 = k.sb("e0_w1", [P, 2, F], F32, ctx)
        w2 = k.sb("e0_w2", [P, 2, 2, D], F32, ctx)
        b1 = k.sb("e0_b1", [P, STEPS * 2], F32, ctx)
        b2 = k.sb("e0_b2", [E + 1, D], F32, ctx)
        gw = k.sb("e0_gw", [P, E], F32, ctx)
        gb = k.sb("e0_gb", [P, E], F32, ctx)
        acc = k.sb("e0_acc", [P, NT, D], F32, ctx)
        gates = k.sb("e0_gates", [P, NT, STEPS], F32, ctx)
        hidden = k.sb("e0_hidden", [P, 2, 2, T], F32, ctx)
        gates_loaded, late_loaded = k.sem("e0_gates_loaded"), k.sem("e0_late_loaded")
        w1_loaded = [k.sem(f"e0_w1_slot{i}_loaded") for i in range(2)]
        w2_loaded = [k.sem(f"e0_w2_slot{i}_loaded") for i in range(2)]
        out_done, added = k.sem("e0_out_done"), [k.sem("e0_added_even"), k.sem("e0_added_odd")]

        def load_w1(sp, s, src):
            sp.dma_start(w1[:, s, :], src).then_inc(w1_loaded[s], 16)

        def load_w2(sp, s, src):
            sp.dma_start(w2[:, s, :, :], src.rearrange("(f p) m -> p f m", p=P)).then_inc(w2_loaded[s], 16)

        with ExitStack() as tmp:
            logits = k.sb("e0_logits", [P, NT, E], F32, tmp)
            top = k.sb("e0_top", [P, NT], F32, tmp)
            weights = k.sb("e0_weights", [P, NT, E + PADS], F32, tmp)
            total = k.sb("e0_total", [P, NT], F32, tmp)
            top8 = k.sb("e0_top8", [P, NT, 8], F32, tmp)
            wanted = k.sb("e0_wanted", [P, NT, 8], F32, tmp)
            left = k.sb("e0_left", [P, NT, E + PADS], F32, tmp)
            chosen = k.sb("e0_chosen", [P, NT, E], F32, tmp)
            gates_T = k.sb("e0_gates_T", [E + 1, T], F32, tmp)
            logit_ps = k.ps("e0_logit_ps", [P, NT, 16], tmp)
            turn_ps = k.ps("e0_turn_ps", [E + 1, T], tmp)
            b2_ps = k.ps("e0_b2_ps", [P, NT, D], tmp)
            logits_ready, shifted, exp_ready = (k.sem("e0_logits_ready"), k.sem("e0_shifted"),
                                                       k.sem("e0_exp_ready"))
            gates_ready, turned, turn_copied, b2_ready = (k.sem("e0_gates_ready"), k.sem("e0_turned"),
                                                          k.sem("e0_turn_copied"), k.sem("e0_b2_ready"))
            with nc.Block() as block:
                @block.sync
                def _(sp):
                    sp.dma_start(gw[:], d["L0_ffn_gW"]).then_inc(gates_loaded, 16)
                    sp.dma_start(gb[:], d["L0_ffn_gb"].unsqueeze(0).to_broadcast([P, E])).then_inc(gates_loaded, 16)
                    sp.dma_start(b2[0:1, :], d["L0_ffn_sb2"]).then_inc(late_loaded, 16)
                    sp.dma_start(b2[1:E + 1, :], d["L0_ffn_rb2"]).then_inc(late_loaded, 16)
                    sp.dma_start(b1[:, 0:4], d["L0_ffn_sb1_p"]).then_inc(late_loaded, 16)
                    sp.dma_start(b1[:, 4:], d["L0_ffn_rb1_p"]).then_inc(late_loaded, 16)
                    for s in range(2):
                        load_w1(sp, s, d["L0_ffn_sW1"][0][:, s * F:(s + 1) * F])
                        load_w2(sp, s, d["L0_ffn_sW2"][0][s * F:(s + 1) * F, :])
                    sp.wait_ge(late_loaded, 64)

                @block.tensor
                def _(pe):
                    pe.wait_ge(gates_loaded, 32)
                    for t in range(NT):
                        ins = nc.tensor.matmul(logit_ps[:, t, 0:E], k.x_T[:, t * P:(t + 1) * P], gw[:], start=True, stop=True)
                    ins.then_inc(logits_ready, 1)
                    pe.wait_ge(gates_ready, 1)
                    for t in range(NT):
                        ins = nc.tensor.transpose(turn_ps[:, t * P:(t + 1) * P], gates[:, t, 1:STEPS], k.ident[:])
                    ins.then_inc(turned, 1)
                    pe.wait_ge(turn_copied, 1)
                    pe.wait_ge(late_loaded, 64)
                    for t in range(NT):
                        ins = nc.tensor.matmul(b2_ps[:, t, :], gates_T[:, t * P:(t + 1) * P], b2[:], start=True, stop=True)
                    ins.then_inc(b2_ready, 1)

                @block.scalar
                def _(act):
                    act.wait_ge(shifted, 1)
                    nc.scalar.activation(weights[:, :, 0:E], logits[:], ACT.Exp).then_inc(exp_ready, 1)
                    act.wait_ge(turned, 1)
                    nc.scalar.copy(gates_T[:], turn_ps[:]).then_inc(turn_copied, 1)
                    nc.scalar.preload_act_table(ACT.Gelu)

                @block.vector
                def _(dve):
                    link = k.chain(dve)

                    def spread(x, n):
                        return x[:].unsqueeze(2).to_broadcast([P, NT, n])
                    nc.vector.memset(weights[:, :, E:E + PADS], LOWEST)
                    nc.vector.memset(wanted[:], LOWEST)
                    nc.vector.memset(gates[:, :, 0:2], 1.0)
                    dve.wait_ge(gates_loaded, 32)
                    dve.wait_ge(logits_ready, 1)
                    link(nc.vector.tensor_tensor(logits[:], logit_ps[:, :, 0:E], gb[:].unsqueeze(1).to_broadcast([P, NT, E]),
                                                 ALU.add))
                    link(nc.vector.tensor_reduce(top[:], logits[:], AX.X, ALU.max))
                    nc.vector.tensor_tensor(logits[:], logits[:], spread(top, E), ALU.subtract).then_inc(shifted, 1)
                    dve.wait_ge(exp_ready, 1)
                    link(nc.vector.tensor_reduce(total[:], weights[:, :, 0:E], AX.X, ALU.add))
                    link(nc.vector.reciprocal(total[:], total[:]))
                    link(nc.vector.tensor_tensor(weights[:, :, 0:E], weights[:, :, 0:E], spread(total, E), ALU.mult))
                    choose(nc, link, weights, E, PADS, TOP, LOWEST, top8, wanted, left, chosen[:])
                    nc.vector.tensor_tensor(gates[:, :, 2:STEPS], weights[:, :, 0:E], chosen[:], ALU.mult).then_inc(gates_ready, 1)
                    dve.wait_ge(b2_ready, 1)
                    nc.vector.tensor_tensor(acc[:], b2_ps[:], k.x_tok[:], ALU.add)

        with ExitStack() as tmp:
            hid_ps = k.ps("e0_hid_ps", [P, 2, T], tmp)
            out_ps = k.ps("e0_out_ps", [P, 2, NT, D], tmp)
            hid_ready, gelu_done = k.sem("e0_hid_ready"), k.sem("e0_gelu_done")

            def hid(pe, step, s, uses):
                pe.wait_ge(w1_loaded[s], 16 * (uses + 1))
                for f in range(2):
                    if not (isinstance(step, int) and step == 0):
                        pe.wait_ge(gelu_done, 2 * step - 1 + f)
                    for h in range(2):
                        ins = nc.tensor.matmul(hid_ps[:, f, h * HALF:(h + 1) * HALF], w1[:, s, f * P:(f + 1) * P],
                                               k.x_T[:, h * HALF:(h + 1) * HALF], start=True, stop=True)
                    ins.then_inc(hid_ready, 1)

            def out(pe, step, s, uses):
                pe.wait_ge(gelu_done, 2 * step + 2)
                pe.wait_ge(w2_loaded[s], 16 * (uses + 1))
                if not (isinstance(uses, int) and uses == 0):
                    pe.wait_ge(added[s], uses)
                for t in range(NT):
                    for f in range(2):
                        ins = nc.tensor.matmul(out_ps[:, s, t, :], hidden[:, s, f, t * P:(t + 1) * P], w2[:, s, f, :],
                                               start=(f == 0), stop=(f == 1))
                ins.then_inc(out_done, 1)

            def gelu(act, step, s):
                if not (isinstance(step, int) and step < 2):
                    act.wait_ge(out_done, step - 1)
                for f in range(2):
                    act.wait_ge(hid_ready, 2 * step + f + 1)
                    nc.scalar.activation(hidden[:, s, f, :], hid_ps[:, f, :], ACT.Gelu,
                                         bias=b1[:, bass.ds(2 * step + f, 1)]).then_inc(gelu_done, 1)

            def add_up(dve, step, s, uses):
                dve.wait_ge(out_done, step + 1)
                if s == 1:
                    dve.wait_ge(added[0], uses + 1)
                elif not (isinstance(uses, int) and uses == 0):
                    dve.wait_ge(added[1], uses)
                for t in range(NT):
                    ins = nc.vector.scalar_tensor_tensor(out=acc[:, t, :], in0=out_ps[:, s, t, :],
                                                         scalar=gates[:, t, bass.ds(step, 1)], in1=acc[:, t, :],
                                                         op0=ALU.mult, op1=ALU.add)
                ins.then_inc(added[s], 1)

            def next_w1(sp, e, s):
                sp.wait_ge(hid_ready, 2 * e + 2)
                load_w1(sp, s, one(d["L0_ffn_rW1"], e))

            def next_w2(sp, e, s):
                sp.wait_ge(out_done, e + 1)
                load_w2(sp, s, one(d["L0_ffn_rW2"], e))

            PAIRS = (STEPS - 1) // 2
            with nc.Block() as block:
                @block.sync
                def _(sp):
                    next_w1(sp, 0, 0)
                    with nc.sync.Fori(0, PAIRS - 1) as p:
                        next_w1(sp, 2 * p + 1, 1)
                        next_w2(sp, 2 * p, 0)
                        next_w1(sp, 2 * p + 2, 0)
                        next_w2(sp, 2 * p + 1, 1)
                    next_w2(sp, E - 1, 0)

                @block.tensor
                def _(pe):
                    hid(pe, 0, 0, 0)
                    hid(pe, 1, 1, 0)
                    out(pe, 0, 0, 0)
                    hid(pe, 2, 0, 1)
                    out(pe, 1, 1, 0)
                    with nc.tensor.Fori(1, PAIRS) as p:
                        hid(pe, 2 * p + 1, 1, p)
                        out(pe, 2 * p, 0, p)
                        hid(pe, 2 * p + 2, 0, p + 1)
                        out(pe, 2 * p + 1, 1, p)
                    out(pe, STEPS - 1, 0, PAIRS)

                @block.scalar
                def _(act):
                    gelu(act, 0, 0)
                    gelu(act, 1, 1)
                    with nc.scalar.Fori(1, PAIRS) as p:
                        for s in range(2):
                            gelu(act, 2 * p + s, s)
                    gelu(act, STEPS - 1, 0)

                @block.vector
                def _(dve):
                    add_up(dve, 0, 0, 0)
                    add_up(dve, 1, 1, 0)
                    with nc.vector.Fori(1, PAIRS) as p:
                        for s in range(2):
                            add_up(dve, 2 * p + s, s, p)
                    add_up(dve, STEPS - 1, 0, PAIRS)
        residual_norm(k, "norm2", acc)


def one(ap, e):
    return ap[bass.ds(e, 1)].rearrange("o a b -> (o a) b")


def turn_stack(k, tag, stack, stack_T, turn_ps, stack_ready, used_dve, used_act, turned, base=0):
    nc = k.nc
    G = NT * H // 8

    def on_pe(pe):
        pe.wait_ge(stack_ready, base + 1)
        for g in range(G):
            if g >= 4 or base:
                pe.wait_ge(used_act if g % 2 else used_dve, base * G // 2 + (g - 4) // 2 + 1)
            for j in range(8):
                ins = nc.tensor.transpose(turn_ps[:, g % 4, j * P:(j + 1) * P], stack[:, g * 8 + j, :], k.ident_b[:])
            ins.then_inc(turned, 1)

    def on_dve(dve):
        for g in range(0, G, 2):
            dve.wait_ge(turned, base * G + g + 1)
            nc.vector.tensor_copy(stack_T[:, g // 2, 0:8 * P], turn_ps[:, g % 4, :]).then_inc(used_dve, 1)

    def on_act(act):
        for g in range(1, G, 2):
            act.wait_ge(turned, base * G + g + 1)
            nc.scalar.copy(stack_T[:, g // 2, 8 * P:16 * P], turn_ps[:, g % 4, :]).then_inc(used_act, 1)

    return on_pe, on_dve, on_act


def self_attention(k):
    nc, d = k.nc, k.dram
    R = 16
    LORA = 32.0 / R
    ctx = ExitStack()
    with ctx:
        q_T = k.sb("s_q_stack_T", [P, NT, H * P], BF16, ctx)
        k_T = k.sb("s_k_stack_T", [P, NT, H * P], BF16, ctx)
        val = k.sb("s_val_ones", [P, NT, H, 32], F32, ctx)
        w_proj = k.sb("s_w_proj", [P, D], F32, ctx)
        b_proj = k.sb("s_b_proj", [P, D], F32, ctx)
        with ExitStack() as tmp:
            w = k.sb("s_w_qkv", [P, 3 * D], F32, tmp)
            b_feat = k.sb("s_b_feat", [P, 3], F32, tmp)
            b_k = k.sb("s_b_k", [P, D], F32, tmp)
            lora_a = k.sb("s_lora_a", [R, 2, H, HD], F32, tmp)
            lora_b = k.sb("s_lora_b", [R, 2, H, HD], F32, tmp)
            mask = k.sb("s_mask", [P, H, HD], F32, tmp)
            mix = k.sb("s_mix", [P, 2, D], F32, tmp)
            before = k.sb("s_before", [P, 2, T], F32, tmp)
            tok = k.sb("s_tok", [P, NT * H, HD], F32, tmp)
            part = [k.sb(f"s_part{i}", [P, NT * H, HD], BF16, tmp) for i in range(3)]
            rest = [before[:, i, :].rearrange("p (a b) -> p a b", b=HD) for i in range(2)]
            stack = k.sb("s_stack", [P, NT * H, AUG], BF16, tmp)
            proj_ps = k.ps("s_proj_ps", [P, 2, T], tmp)
            turn_ps = k.ps("s_turn_ps", [P, 4, 8 * P], tmp, BF16)
            loaded = k.sem("s_loaded")
            masked0, masked1, masked2 = k.sem("s_masked0"), k.sem("s_masked1"), k.sem("s_masked2")
            mix_raw, mix_ready, raw_ready, biased = (k.sem("s_mix_raw"), k.sem("s_mix_ready"), k.sem("s_raw_ready"),
                                                     k.sem("s_biased"))
            tok_ready, tok_taken, stack_ready = k.sem("s_tok_ready"), k.sem("s_tok_taken"), k.sem("s_stack_ready")
            turned, used_dve, used_act = k.sem("s_turned"), k.sem("s_turn_used_dve"), k.sem("s_turn_used_act")
            turns = [turn_stack(k, "s", stack, x, turn_ps, stack_ready, used_dve, used_act, turned, base=i)
                     for i, x in enumerate((q_T, k_T))]
            with nc.Block() as block:
                @block.sync
                def _(sp):
                    sp.dma_start(w[:], d["L1_attn_w_qkv"]).then_inc(loaded, 16)
                    with nc.allow_non_contiguous_dma(reason="three floats to a partition; 256 of a LoRA matrix"):
                        sp.dma_start(b_feat[:], d["L1_attn_b_qkv"].rearrange("(s p) -> p s", p=P)).then_inc(loaded, 16)
                        for i, n in enumerate("qv"):
                            sp.dma_start(lora_a[:, i], d[f"L1_attn_a_{n}_T"].unsqueeze(1).to_broadcast([R, H, HD])).then_inc(loaded, 16)
                            sp.dma_start(lora_b[:, i], d[f"L1_attn_b_{n}"].unsqueeze(1).to_broadcast([R, H, HD])).then_inc(loaded, 16)
                    sp.dma_start(b_k[:], d["L1_attn_b_qkv"][D:2 * D].unsqueeze(0).to_broadcast([P, D])).then_inc(loaded, 16)
                    sp.dma_start(w_proj[:], d["L1_attn_w_proj"]).then_inc(loaded, 16)
                    sp.dma_start(b_proj[:], d["L1_attn_b_proj"].unsqueeze(0).to_broadcast([P, D])).then_inc(loaded, 16)

                @block.gpsimd
                def _(pool):
                    nc.gpsimd.memset(mask[:], LORA).then_inc(masked0, 1)
                    pool.wait_ge(masked0, 1)
                    nc.gpsimd.affine_select(out=mask[:], in_=mask[:], compare_op=ALU.is_ge, fill=0.0, base=0,
                                            pattern=[[-HD, H], [0, HD]], channel_multiplier=1).then_inc(masked1, 1)
                    pool.wait_ge(masked1, 1)
                    nc.gpsimd.affine_select(out=mask[:], in_=mask[:], compare_op=ALU.is_ge, fill=0.0, base=HD - 1,
                                            pattern=[[HD, H], [0, HD]], channel_multiplier=-1).then_inc(masked2, 1)

                @block.tensor
                def _(pe):
                    pe.wait_ge(loaded, 16 * 9)
                    for i in range(2):
                        ins = nc.tensor.matmul(proj_ps[:, i, 0:D], lora_a[:, i].rearrange("r h e -> r (h e)"),
                                               lora_b[:, i].rearrange("r h e -> r (h e)"), start=True, stop=True)
                    ins.then_inc(mix_raw, 1)
                    pe.wait_ge(mix_ready, 1)
                    for i, col in enumerate((0, 2 * D)):
                        for h in range(2):
                            ins = nc.tensor.matmul(proj_ps[:, i, h * HALF:(h + 1) * HALF], w[:, col:col + D],
                                                   k.x_T[:, h * HALF:(h + 1) * HALF], start=True, stop=True)
                        ins.then_inc(raw_ready, 1)
                    for i in range(2):
                        pe.wait_ge(biased, i + 1)
                        for t in range(NT):
                            ins = nc.tensor.matmul(proj_ps[:, i, t * P:(t + 1) * P], before[:, i, t * P:(t + 1) * P],
                                                   mix[:, i, :], start=True, stop=True)
                        ins.then_inc(tok_ready, 1)
                    pe.wait_ge(tok_taken, 1)
                    for t in range(NT):
                        ins = nc.tensor.matmul(proj_ps[:, 0, t * P:(t + 1) * P], k.x_T[:, t * P:(t + 1) * P],
                                               w[:, D:2 * D], start=True, stop=True)
                    ins.then_inc(tok_ready, 1)
                    for on_pe, _, _ in turns:
                        on_pe(pe)

                @block.scalar
                def _(act):
                    for i, col in enumerate((0, 2)):
                        act.wait_ge(raw_ready, i + 1)
                        nc.scalar.activation(before[:, i, :], proj_ps[:, i, :], ACT.Identity,
                                             bias=b_feat[:, col:col + 1]).then_inc(biased, 1)
                    for _, _, on_act in turns:
                        on_act(act)
                    nc.scalar.preload_act_table(ACT.Exp)

                @block.vector
                def _(dve):
                    link = k.chain(dve)
                    flat = tok[:].rearrange("p a b -> p (a b)")
                    nc.vector.memset(val[:], 0.0)
                    nc.vector.memset(stack[:, :, USED:AUG], 0.0)
                    link(nc.vector.memset(stack[:, :, SHIFT:SHIFT + 3], 0.0))
                    link(nc.vector.memset(val[:, :, :, HD:HD + 1], 1.0))
                    dve.wait_ge(mix_raw, 1)
                    dve.wait_ge(masked2, 1)
                    for i in range(2):
                        link(nc.vector.tensor_tensor(mix[:, i, :], proj_ps[:, i, 0:D], mask[:].rearrange("p h e -> p (h e)"),
                                                     ALU.mult))
                    link(nc.vector.tensor_tensor(mix[:, 0, :], mix[:, 0, :], k.ident[:], ALU.add))
                    nc.vector.tensor_tensor(mix[:, 1, :], mix[:, 1, :], k.ident[:], ALU.add).then_inc(mix_ready, 1)
                    dve.wait_ge(tok_ready, 1)
                    dve.wait_ge(tok_ready, 2)
                    nc.vector.tensor_scalar(flat, proj_ps[:, 0, :], float(HD) ** -0.5, None, ALU.mult).then_inc(tok_taken, 1)
                    dve.wait_ge(tok_taken, 1)
                    nc.vector.tensor_copy(val[:, :, :, 0:HD], proj_ps[:, 1, :].rearrange("p (t h e) -> p t h e", t=NT, h=H))
                    stack_queries(nc, link, tok[:], [x[:] for x in part], rest, stack, Q_PARTS).then_inc(stack_ready, 1)
                    turns[0][1](dve)
                    dve.wait_ge(tok_ready, 3)
                    dve.wait_ge(turned, NT * H // 8)
                    nc.vector.memset(stack[:, :, SHIFT:SHIFT + 3], 1.0)
                    link(nc.vector.tensor_tensor(tok[:].rearrange("p (t h) e -> p t (h e)", t=NT),
                                                 proj_ps[:, 0, :].rearrange("p (t f) -> p t f", t=NT),
                                                 b_k[:].unsqueeze(1).to_broadcast([P, NT, D]), ALU.add))
                    stack_queries(nc, link, tok[:], [x[:] for x in part], rest, stack, K_PARTS).then_inc(stack_ready, 1)
                    turns[1][1](dve)

        gathered = k.sb("s_gathered", [P, H, 2 * P], F32, ctx)
        with ExitStack() as tmp:
            v_buf = k.sb("s_v_buf", [P, 2, NT, 32], F32, tmp)
            probs = k.sb("s_probs", [P, 2, T], F32, tmp)
            partial = k.sb("s_max_partial", [P, NT, 2], F32, tmp)
            neg = k.sb("s_neg_max", [P, NT], F32, tmp)
            rests = [k.sb(f"s_neg_rest{i}", [P, NT], F32, tmp) for i in range(2)]
            part3 = k.sb("s_neg_part", [P, NT, 3], BF16, tmp)
            score_ps = k.ps("s_score_ps", [P, 2, T], tmp)
            max_ps = k.ps("s_max_ps", [P, 2, HALF], tmp)
            acc_ps = k.ps("s_acc_ps", [P, HALF], tmp)
            shift_ps = k.ps("s_shift_ps", [P, T], tmp, BF16)
            steps_before = k.steps.n
            LINKED = 5
            q_ready, val_ready = k.sem("s_q_ready"), k.sem("s_val_ready")
            unit_ready, unit_used, parts_ready, shift_turned = (k.sem("s_max_ready"), k.sem("s_max_used"),
                                                                k.sem("s_neg_parts_ready"), k.sem("s_shift_turned"))
            score_ready, exp_done, pv_done, acc_used = (k.sem("s_score_ready"), k.sem("s_exp_done"), k.sem("s_pv_done"),
                                                        k.sem("s_acc_used"))
            UNITS = 2 * NT
            QUART = T // 4
            AHEAD = 6

            def at(h):
                return h if isinstance(h, int) else bass.ds(h, 1)

            def block_of(ap, h, t):
                return ap[:, t, h * P:(h + 1) * P] if isinstance(h, int) else ap[:, t, bass.ds(h * P, P)]

            def half_of(ap, h, half):
                x = ap[:].rearrange("p t (h c) -> p t h c", h=H)[:, 4 * half:4 * half + 4, at(h), :]
                return x if isinstance(h, int) else x.rearrange("p t o c -> p t (o c)")

            def max_unit(pe, h, u):
                if not (isinstance(h, int) and h == 0 and u < 2):
                    pe.wait_ge(unit_used, h * UNITS + u - 1)
                nc.tensor.matmul(max_ps[:, u % 2, :].rearrange("p (t c) -> p t c", t=4), block_of(q_T, h, u // 2),
                                 half_of(k_T, h, u % 2), start=True, stop=True).then_inc(unit_ready, 1)

            def turn_shift(pe, h):
                pe.wait_ge(parts_ready, h + 1)
                for t in range(NT):
                    ins = nc.tensor.transpose(shift_ps[0:3, t * P:(t + 1) * P], part3[:, t, :], k.ident_b[:])
                ins.then_inc(shift_turned, 1)

            def weigh(pe, h, s, v):
                if v == 0:
                    pe.wait_ge(val_ready, h + 1)
                    if not (isinstance(h, int) and h == 0):
                        pe.wait_ge(acc_used, h)
                pe.wait_ge(exp_done, h * NT + v + 1)
                for j in range(4):
                    ins = nc.tensor.matmul(acc_ps[32 * j:32 * j + 32, 0:QUART], v_buf[:, s, v, :],
                                           probs[:, v % 2, j * QUART:(j + 1) * QUART],
                                           start=(v == 0), stop=(v == NT - 1))
                ins.then_inc(pv_done, 1)

            def attend(pe, h, s):
                pe.wait_ge(q_ready, h + 1)
                for c in range(NT):
                    if c == NT - 2 and not (isinstance(h, int) and h == H - 1):
                        turn_shift(pe, h + 1)
                    if not (isinstance(h, int) and h == 0 and c < 2):
                        pe.wait_ge(exp_done, h * NT + c - 1)
                    ahead = [divmod(2 * c + AHEAD + i, UNITS) for i in range(2)]
                    ahead = [(h + 1 + later, u) for later, u in ahead if not (isinstance(h, int) and h + 1 + later >= H)]
                    if ahead:
                        max_unit(pe, *ahead[0])
                    for half in range(2):
                        ins = nc.tensor.matmul(score_ps[:, c % 2, half * HALF:(half + 1) * HALF].rearrange(
                            "p (t c) -> p t c", t=4), block_of(k_T, h, c), half_of(q_T, h, half), start=True, stop=True)
                    ins.then_inc(score_ready, 1)
                    if ahead:
                        max_unit(pe, *ahead[1])
                    if c >= 1:
                        weigh(pe, h, s, c - 1)
                    elif not (isinstance(h, int) and h == 0):
                        weigh(pe, h - 1, 1 - s, NT - 1)

            def take_acc(act, h):
                act.wait_ge(pv_done, (h + 1) * NT)
                nc.scalar.copy(gathered[:, at(h), :] if isinstance(h, int) else gathered[:, at(h), :].rearrange(
                    "p o c -> p (o c)"), acc_ps[:, 0:QUART]).then_inc(acc_used, 1)

            def take_shift(act, h):
                act.wait_ge(shift_turned, h + 1)
                dst = q_T[:].rearrange("p t (h c) -> p t h c", h=H)[SHIFT:SHIFT + 3, :, at(h), :]
                if not isinstance(h, int):
                    dst = dst.rearrange("p t o c -> p t (o c)")
                nc.scalar.copy(dst, shift_ps[0:3, :].rearrange("p (t c) -> p t c", t=NT)).then_inc(q_ready, 1)

            def exponentiate(act, h):
                for c in range(NT):
                    act.wait_ge(score_ready, h * NT + c + 1)
                    if not (isinstance(h, int) and h == 0 and c < 2):
                        act.wait_ge(pv_done, h * NT + c - 1)
                    nc.scalar.activation(probs[:, c % 2, :], score_ps[:, c % 2, :], ACT.Exp).then_inc(exp_done, 1)
                    if c == 0 and not (isinstance(h, int) and h == 0):
                        take_acc(act, h - 1)
                    if c == NT - 3 and not (isinstance(h, int) and h == H - 1):
                        take_shift(act, h + 1)

            def maxima(dve, h):
                for u in range(UNITS):
                    dve.wait_ge(unit_ready, h * UNITS + u + 1)
                    nc.vector.tensor_reduce(partial[:, u // 2, u % 2:u % 2 + 1], max_ps[:, u % 2, :], AX.X,
                                            ALU.max).then_inc(unit_used, 1)
                dve.wait_ge(unit_used, (h + 1) * UNITS)
                if not (isinstance(h, int) and h == 0):
                    dve.wait_ge(shift_turned, h)
                link = k.chain(dve)
                link.n = steps_before + h * LINKED
                negated_maximum(nc, link, partial[:], neg[:], [x[:] for x in rests], part3[:]).then_inc(parts_ready, 1)
                dve.wait_ge(parts_ready, h + 1)

            def values(pool, h, s):
                out = v_buf[:, s, :, :] if isinstance(h, int) else v_buf[:, s, :, :].unsqueeze(2)
                nc.gpsimd.tensor_copy(out, val[:, :, at(h), :]).then_inc(val_ready, 1)

            with nc.Block() as block:
                @block.tensor
                def _(pe):
                    for u in range(UNITS):
                        max_unit(pe, 0, u)
                    for u in range(AHEAD):
                        max_unit(pe, 1, u)
                    turn_shift(pe, 0)
                    attend(pe, 0, 0)
                    attend(pe, 1, 1)
                    with nc.tensor.Fori(1, H // 2 - 1) as p:
                        for s in range(2):
                            attend(pe, 2 * p + s, s)
                    attend(pe, H - 2, 0)
                    attend(pe, H - 1, 1)
                    weigh(pe, H - 1, 1, NT - 1)

                @block.scalar
                def _(act):
                    take_shift(act, 0)
                    exponentiate(act, 0)
                    with nc.scalar.Fori(1, H - 1) as h:
                        exponentiate(act, h)
                    exponentiate(act, H - 1)
                    take_acc(act, H - 1)

                @block.gpsimd
                def _(pool):
                    for h in range(2):
                        values(pool, h, h)
                    with nc.gpsimd.Fori(1, H // 2) as p:
                        for s in range(2):
                            pool.wait_ge(pv_done, (2 * p + s - 1) * NT)
                            values(pool, 2 * p + s, s)

                @block.vector
                def _(dve):
                    maxima(dve, 0)
                    with nc.vector.Fori(1, H) as h:
                        maxima(dve, h)
                    k.steps.n = steps_before + H * LINKED

        with ExitStack() as tmp:
            merged = k.sb("s_merged", [P, NT, D], F32, tmp)
            out_ps = k.ps("s_out_ps", [P, NT, D], tmp)
            finish_heads(k, "self", gathered, merged, w_proj, out_ps, by_tile=False)
            residual_norm(k, "norm3", out_ps, bias=b_proj)


def context_attention1(k):
    nc, d = k.nc, k.dram
    WIDE = 2 * HALF
    RANGES = [(c0, min(WIDE, CTX - c0)) for c0 in range(0, CTX, WIDE)]
    NR = len(RANGES)
    GROUPS = [(c, min(4, NCH - c)) for c in range(0, NCH, 4)]
    NG = len(GROUPS)
    SCALE = float(D) ** -0.5
    ctx = ExitStack()
    with ctx:
        q_T = k.sb("x1_q_T", [P, T], F32, ctx)
        merged = k.sb("x1_merged", [P, NT, D], F32, ctx)
        w_out = k.sb("x1_w_out", [P, D], F32, ctx)
        b_out = k.sb("x1_b_out", [P, D], F32, ctx)
        b_v = k.sb("x1_b_v", [P, D], F32, ctx)
        with ExitStack() as tmp:
            w_q = k.sb("x1_w_q", [P, D], F32, tmp)
            b_q = k.sb("x1_b_q", [P, 1], F32, tmp)
            b_scaled = k.sb("x1_b_scaled", [P, 1], F32, tmp)
            q_ps = k.ps("x1_q_ps", [P, T], tmp)
            loaded, q_ready, scaled = k.sem("x1_loaded"), k.sem("x1_q_ready"), k.sem("x1_scaled")
            with nc.Block() as block:
                @block.sync
                def _(sp):
                    sp.dma_start(w_q[:], d["L1_xattn_Wq_T"]).then_inc(loaded, 16)
                    with nc.allow_non_contiguous_dma(reason="a float to a partition"):
                        sp.dma_start(b_q[:], d["L1_xattn_bq"].unsqueeze(1)).then_inc(loaded, 16)
                    sp.dma_start(w_out[:], d["L1_xattn_Wo_T"]).then_inc(loaded, 16)
                    sp.dma_start(b_v[:], d["L1_xattn_bv"].unsqueeze(0).to_broadcast([P, D])).then_inc(loaded, 16)
                    sp.dma_start(b_out[:], d["L1_xattn_bo"].unsqueeze(0).to_broadcast([P, D])).then_inc(loaded, 16)

                @block.tensor
                def _(pe):
                    pe.wait_ge(loaded, 80)
                    for h in range(2):
                        nc.tensor.matmul(q_ps[:, h * HALF:(h + 1) * HALF], w_q[:], k.x_T[:, h * HALF:(h + 1) * HALF],
                                         start=True, stop=True).then_inc(q_ready, 1)

                @block.vector
                def _(dve):
                    dve.wait_ge(loaded, 80)
                    nc.vector.tensor_scalar(b_scaled[:], b_q[:], SCALE, None, ALU.mult).then_inc(scaled, 1)

                @block.scalar
                def _(act):
                    act.wait_ge(scaled, 1)
                    for h in range(2):
                        act.wait_ge(q_ready, h + 1)
                        nc.scalar.activation(q_T[:, h * HALF:(h + 1) * HALF], q_ps[:, h * HALF:(h + 1) * HALF],
                                             ACT.Identity, bias=b_scaled[:], scale=SCALE)
                    nc.scalar.preload_act_table(ACT.Exp)

        with ExitStack() as tmp:
            q_buf = k.sb("x1_q_buf", [P, 2, P], F32, tmp)
            scores = k.sb("x1_scores", [P, 2, CTX], F32, tmp)
            turned = k.sb("x1_turned", [P, 2, HALF], F32, tmp)
            top = k.sb("x1_top", [P, 2, NR], F32, tmp)
            neg = k.sb("x1_neg", [P, 2], F32, tmp)
            sums = k.sb("x1_sums", [P, 2, NR], F32, tmp)
            total = k.sb("x1_total", [P, 2], F32, tmp)
            recip = k.sb("x1_recip", [P, 2], F32, tmp)
            score_ps = k.ps("x1_score_ps", [P, 2, WIDE], tmp)
            turn_ps = k.ps("x1_turn_ps", [P, 2, HALF], tmp)
            acc_ps = k.ps("x1_acc_ps", [P, 2, HALF], tmp)
            q_ready, range_ready, taken = k.sem("x1_q_buf_ready"), k.sem("x1_range_ready"), k.sem("x1_taken")
            neg_ready, exp_done, group_turned = k.sem("x1_neg_ready"), k.sem("x1_exp_done"), k.sem("x1_group_turned")
            copied = [k.sem("x1_copied_even"), k.sem("x1_copied_odd")]
            pv_done, summed, recip_ready, merged_ready = (k.sem("x1_pv_done"), k.sem("x1_summed"), k.sem("x1_recip_ready"),
                                                          k.sem("x1_merged_ready"))

            def tile_of(p, s):
                return 2 * p + s

            def score_step(pe, p, s, g):
                t = tile_of(p, s)
                r, n = g // 2, min(HALF, CTX - g * HALF)
                local = NR * s + r
                if g == 0:
                    pe.wait_ge(q_ready, t + 1)
                if g % 2 == 0 and not (isinstance(p, int) and p == 0 and local < 2):
                    pe.wait_ge(taken, 2 * NR * p + local - 1)
                ins = nc.tensor.matmul(score_ps[:, local % 2, (g % 2) * HALF:(g % 2) * HALF + n], q_buf[:, s, :],
                                       k.key1_T[:, g * HALF:g * HALF + n], start=True, stop=True)
                if g % 2 == 1 or g == NG - 1:
                    ins.then_inc(range_ready, 1)

            def weigh_turn(pe, p, s, g):
                t, local = tile_of(p, s), NG * s + g
                c0, m = GROUPS[g]
                last_key = min(CTX, (c0 + m) * P)
                pe.wait_ge(exp_done, NR * t + (last_key - 1) // WIDE + 1)
                pe.wait_ge(copied[local % 2], NG * p + local // 2)
                for j in range(m):
                    keys = min(P, CTX - (c0 + j) * P)
                    ins = nc.tensor.transpose(turn_ps[0:keys, local % 2, j * P:(j + 1) * P],
                                              scores[:, s, (c0 + j) * P:(c0 + j) * P + keys], k.ident[:])
                ins.then_inc(group_turned, 1)

            def weigh_add(pe, p, s, g):
                t, local = tile_of(p, s), NG * s + g
                c0, m = GROUPS[g]
                pe.wait_ge(copied[local % 2], NG * p + local // 2 + 1)
                if g == 0:
                    pe.wait_ge(merged_ready, 2 * p + max(0, s - 1))
                for j in range(m):
                    keys = min(P, CTX - (c0 + j) * P)
                    ins = nc.tensor.matmul(acc_ps[:, s, 0:D], turned[0:keys, local % 2, j * P:(j + 1) * P],
                                           k.val1[0:keys, c0 + j, :], start=(c0 + j == 0), stop=(c0 + j == NCH - 1))
                ins.then_inc(pv_done, 1)

            def copy_group(eng, copy, p, s, g):
                local = NG * s + g
                c0, m = GROUPS[g]
                eng.wait_ge(group_turned, 2 * NG * p + local + 1)
                eng.wait_ge(pv_done, 2 * NG * p + max(0, local - 1))
                full = min(m, NCH - 1 - c0)
                ins = copy(turned[:, local % 2, 0:full * P], turn_ps[:, local % 2, 0:full * P])
                if full < m:
                    ins = copy(turned[0:TAIL, local % 2, full * P:m * P], turn_ps[0:TAIL, local % 2, full * P:m * P])
                ins.then_inc(copied[local % 2], 1)

            def tile_on_pe(pe, p, s, nxt):
                for g in range(NG + 1):
                    if g < NG:
                        if nxt:
                            score_step(pe, *nxt, g)
                        weigh_turn(pe, p, s, g)
                    if g >= 1:
                        weigh_add(pe, p, s, g - 1)

            def take_range(dve, p, s, r):
                t, local = tile_of(p, s), NR * s + r
                c0, cols = RANGES[r]
                dve.wait_ge(range_ready, 2 * NR * p + local + 1)
                nc.vector.tensor_scalar(scores[:, s, c0:c0 + cols], score_ps[:, local % 2, 0:cols], 1.0, None, ALU.mult,
                                        ALU.max, accum_out=top[:, s, r:r + 1]).then_inc(taken, 1)
                if r == NR - 1:
                    dve.wait_ge(taken, NR * (t + 1))
                    nc.vector.tensor_reduce(neg[:, s:s + 1], top[:, s, :], AX.X, ALU.max, negate=True).then_inc(neg_ready, 1)

            def fetch_query(dve, p, s):
                t = tile_of(p, s)
                src = q_T[:, t * P:(t + 1) * P] if isinstance(p, int) else q_T[:, bass.ds(t * P, P)]
                nc.vector.tensor_copy(q_buf[:, s, :], src).then_inc(q_ready, 1)

            def tile_on_dve(dve, p, s, nxt):
                if nxt:
                    fetch_query(dve, *nxt)
                for g in range(NG):
                    if nxt and (g % 2 == 1 or g == NG - 1):
                        take_range(dve, *nxt, g // 2)
                    if (NG * s + g) % 2 == 0:
                        copy_group(dve, nc.vector.tensor_copy, p, s, g)
                t = tile_of(p, s)
                dve.wait_ge(exp_done, NR * (t + 1))
                nc.vector.tensor_reduce(total[:, s:s + 1], sums[:, s, :], AX.X, ALU.add).then_inc(summed, 1)
                dve.wait_ge(summed, t + 1)
                nc.vector.reciprocal(recip[:, s:s + 1], total[:, s:s + 1]).then_inc(recip_ready, 1)
                dve.wait_ge(recip_ready, t + 1)
                dve.wait_ge(pv_done, NG * (t + 1))
                out = merged[:, t, :] if isinstance(p, int) else merged[:, bass.ds(t, 1), :].rearrange("p o e -> p (o e)")
                nc.vector.scalar_tensor_tensor(out=out, in0=acc_ps[:, s, 0:D], scalar=recip[:, s:s + 1], in1=b_v[:],
                                               op0=ALU.mult, op1=ALU.add).then_inc(merged_ready, 1)

            def exponentiate(act, p, s):
                t = tile_of(p, s)
                act.wait_ge(neg_ready, t + 1)
                act.wait_ge(summed, 2 * p + max(0, s - 1))
                for r, (c0, cols) in enumerate(RANGES):
                    nc.scalar.activation(scores[:, s, c0:c0 + cols], scores[:, s, c0:c0 + cols], ACT.Exp,
                                         bias=neg[:, s:s + 1], accum_out=sums[:, s, r:r + 1]).then_inc(exp_done, 1)

            def tile_on_act(act, p, s):
                exponentiate(act, p, s)
                for g in range(NG):
                    if (NG * s + g) % 2 == 1:
                        copy_group(act, nc.scalar.copy, p, s, g)

            LAST = NT // 2 - 1
            with nc.Block() as block:
                @block.tensor
                def _(pe):
                    for g in range(NG):
                        score_step(pe, 0, 0, g)
                    with nc.tensor.Fori(0, LAST) as p:
                        tile_on_pe(pe, p, 0, (p, 1))
                        tile_on_pe(pe, p, 1, (p + 1, 0))
                    tile_on_pe(pe, LAST, 0, (LAST, 1))
                    tile_on_pe(pe, LAST, 1, None)

                @block.vector
                def _(dve):
                    fetch_query(dve, 0, 0)
                    for r in range(NR):
                        take_range(dve, 0, 0, r)
                    with nc.vector.Fori(0, LAST) as p:
                        tile_on_dve(dve, p, 0, (p, 1))
                        tile_on_dve(dve, p, 1, (p + 1, 0))
                    tile_on_dve(dve, LAST, 0, (LAST, 1))
                    tile_on_dve(dve, LAST, 1, None)

                @block.scalar
                def _(act):
                    with nc.scalar.Fori(0, NT // 2) as p:
                        for s in range(2):
                            tile_on_act(act, p, s)

        with ExitStack() as tmp:
            out_ps = k.ps("x1_out_ps", [P, NT, D], tmp)
            project(k, "x1", merged, w_out, out_ps)
            residual_norm(k, "norm4", out_ps, bias=b_out)


def experts1(k, store=None):
    nc, d = k.nc, k.dram
    E, F, TOP = 8, 2 * P, 2
    PADS = 8 - TOP
    LOWEST = -1e38
    ctx = ExitStack()
    with ctx:
        w1 = k.sb("e1_w1", [P, 2, F], F32, ctx)
        w2 = k.sb("e1_w2", [P, 2, F], F32, ctx)
        w3 = k.sb("e1_w3", [P, 2, 2, D], F32, ctx)
        b1 = k.sb("e1_b1", [P, E * 2], F32, ctx)
        b2 = k.sb("e1_b2", [P, E * 2], F32, ctx)
        b3 = k.sb("e1_b3", [E, D], F32, ctx)
        wg = k.sb("e1_wg", [P, E], F32, ctx)
        acc = k.sb("e1_acc", [P, NT, D], F32, ctx)
        gates = k.sb("e1_gates", [P, NT, E], F32, ctx)
        gate_act = k.sb("e1_silu", [P, 2, T], F32, ctx)
        hidden = k.sb("e1_hidden", [P, 2, 2, T], F32, ctx)
        early_loaded, late_loaded = k.sem("e1_early_loaded"), k.sem("e1_late_loaded")
        up_loaded = [k.sem(f"e1_w12_slot{i}_loaded") for i in range(2)]
        down_loaded = [k.sem(f"e1_w3_slot{i}_loaded") for i in range(2)]
        out_done, added = k.sem("e1_out_done"), [k.sem("e1_added_even"), k.sem("e1_added_odd")]

        def load_up(sp, e, s):
            for buf, n in ((w1, "W1"), (w2, "W2")):
                sp.dma_start(buf[:, s, :], one(d[f"L1_ffn_{n}_T"], e)).then_inc(up_loaded[s], 16)

        def load_down(sp, e, s):
            sp.dma_start(w3[:, s, :, :], one(d["L1_ffn_W3_T"], e).rearrange("(f p) m -> p f m", p=P)).then_inc(
                down_loaded[s], 16)

        with ExitStack() as tmp:
            scores = k.sb("e1_scores", [P, NT, E + PADS], F32, tmp)
            top8 = k.sb("e1_top8", [P, NT, 8], F32, tmp)
            wanted = k.sb("e1_wanted", [P, NT, 8], F32, tmp)
            left = k.sb("e1_left", [P, NT, E + PADS], F32, tmp)
            chosen = k.sb("e1_chosen", [P, NT, E], F32, tmp)
            raised = k.sb("e1_raised", [P, NT, E], F32, tmp)
            total = k.sb("e1_total", [P, NT], F32, tmp)
            gates_T = k.sb("e1_gates_T", [E, T], F32, tmp)
            score_ps = k.ps("e1_score_ps", [P, NT, E], tmp)
            turn_ps = k.ps("e1_turn_ps", [E, T], tmp)
            b3_ps = k.ps("e1_b3_ps", [P, NT, D], tmp)
            scores_ready, shifted, exp_ready = (k.sem("e1_scores_ready"), k.sem("e1_shifted"),
                                                      k.sem("e1_exp_ready"))
            gates_ready, turned, turn_copied, b3_ready = (k.sem("e1_gates_ready"), k.sem("e1_turned"),
                                                          k.sem("e1_turn_copied"), k.sem("e1_b3_ready"))
            with nc.Block() as block:
                @block.sync
                def _(sp):
                    sp.dma_start(wg[:], d["L1_ffn_Wg_T"]).then_inc(early_loaded, 16)
                    sp.dma_start(b3[:], d["L1_ffn_b3"]).then_inc(late_loaded, 16)
                    sp.dma_start(b1[:], d["L1_ffn_b1_p"]).then_inc(late_loaded, 16)
                    sp.dma_start(b2[:], d["L1_ffn_b2_p"]).then_inc(late_loaded, 16)
                    for s in range(2):
                        load_up(sp, s, s)
                        load_down(sp, s, s)
                    sp.wait_ge(late_loaded, 48)

                @block.tensor
                def _(pe):
                    pe.wait_ge(early_loaded, 16)
                    for t in range(NT):
                        ins = nc.tensor.matmul(score_ps[:, t, :], k.x_T[:, t * P:(t + 1) * P], wg[:], start=True, stop=True)
                    ins.then_inc(scores_ready, 1)
                    pe.wait_ge(gates_ready, 1)
                    for t in range(NT):
                        ins = nc.tensor.transpose(turn_ps[:, t * P:(t + 1) * P], gates[:, t, :], k.ident[:])
                    ins.then_inc(turned, 1)
                    pe.wait_ge(turn_copied, 1)
                    pe.wait_ge(late_loaded, 48)
                    for t in range(NT):
                        ins = nc.tensor.matmul(b3_ps[:, t, :], gates_T[:, t * P:(t + 1) * P], b3[:], start=True, stop=True)
                    ins.then_inc(b3_ready, 1)

                @block.scalar
                def _(act):
                    act.wait_ge(shifted, 1)
                    nc.scalar.activation(raised[:], raised[:], ACT.Exp).then_inc(exp_ready, 1)
                    act.wait_ge(turned, 1)
                    nc.scalar.copy(gates_T[:], turn_ps[:]).then_inc(turn_copied, 1)
                    nc.scalar.preload_act_table(ACT.Silu)

                @block.vector
                def _(dve):
                    link = k.chain(dve)
                    nc.vector.memset(scores[:, :, E:E + PADS], LOWEST)
                    nc.vector.memset(wanted[:], LOWEST)
                    dve.wait_ge(scores_ready, 1)
                    link(nc.vector.tensor_copy(scores[:, :, 0:E], score_ps[:]))
                    choose(nc, link, scores, E, PADS, TOP, LOWEST, top8, wanted, left, chosen[:])
                    nc.vector.tensor_tensor(raised[:], scores[:, :, 0:E], top8[:, :, 0:1].to_broadcast([P, NT, E]),
                                            ALU.subtract).then_inc(shifted, 1)
                    dve.wait_ge(exp_ready, 1)
                    link(nc.vector.tensor_tensor(raised[:], raised[:], chosen[:], ALU.mult))
                    link(nc.vector.tensor_reduce(total[:], raised[:], AX.X, ALU.add))
                    link(nc.vector.reciprocal(total[:], total[:]))
                    nc.vector.tensor_tensor(gates[:], raised[:], total[:].unsqueeze(2).to_broadcast([P, NT, E]),
                                            ALU.mult).then_inc(gates_ready, 1)
                    dve.wait_ge(b3_ready, 1)
                    nc.vector.tensor_copy(acc[:], b3_ps[:])

        with ExitStack() as tmp:
            a_ps = k.ps("e1_a_ps", [P, T], tmp)
            b_ps = k.ps("e1_b_ps", [P, T], tmp)
            out_ps = k.ps("e1_out_ps", [P, 2, NT, D], tmp)
            a_ready, b_ready, silu_done, hidden_done = (k.sem("e1_a_ready"), k.sem("e1_b_ready"), k.sem("e1_silu_done"),
                                                        k.sem("e1_hidden_done"))

            def up(pe, e, s, f, uses):
                pe.wait_ge(up_loaded[s], 32 * (uses + 1))
                first = isinstance(e, int) and e == 0 and f == 0
                for w, ps, ready, used in ((w1, a_ps, a_ready, silu_done), (w2, b_ps, b_ready, hidden_done)):
                    if not first:
                        pe.wait_ge(used, 2 * e + f)
                    for h in range(2):
                        ins = nc.tensor.matmul(ps[:, h * HALF:(h + 1) * HALF], w[:, s, f * P:(f + 1) * P],
                                               k.x_T[:, h * HALF:(h + 1) * HALF], start=True, stop=True)
                    ins.then_inc(ready, 1)

            def down(pe, e, s, uses, part):
                if part == 0:
                    pe.wait_ge(hidden_done, 2 * e + 2)
                    pe.wait_ge(down_loaded[s], 16 * (uses + 1))
                    if not (isinstance(uses, int) and uses == 0):
                        pe.wait_ge(added[s], uses)
                for t in range(part * NT // 2, (part + 1) * NT // 2):
                    for f in range(2):
                        ins = nc.tensor.matmul(out_ps[:, s, t, :], hidden[:, s, f, t * P:(t + 1) * P], w3[:, s, f, :],
                                               start=(f == 0), stop=(f == 1))
                if part:
                    ins.then_inc(out_done, 1)

            def activate(act, e, s, f):
                act.wait_ge(a_ready, 2 * e + f + 1)
                if not (isinstance(e, int) and e == 0):
                    act.wait_ge(hidden_done, 2 * e + f - 1)
                nc.scalar.activation(gate_act[:, f, :], a_ps[:], ACT.Silu,
                                     bias=b1[:, bass.ds(2 * e + f, 1)]).then_inc(silu_done, 1)

            def combine(dve, e, s, f):
                dve.wait_ge(b_ready, 2 * e + f + 1)
                dve.wait_ge(silu_done, 2 * e + f + 1)
                nc.vector.scalar_tensor_tensor(out=hidden[:, s, f, :], in0=b_ps[:], scalar=b2[:, bass.ds(2 * e + f, 1)],
                                               in1=gate_act[:, f, :], op0=ALU.add, op1=ALU.mult).then_inc(hidden_done, 1)

            def add_up(dve, e, s, uses):
                dve.wait_ge(out_done, e + 1)
                if not (isinstance(e, int) and e == 0):
                    dve.wait_ge(added[1 - s], uses + s)
                for t in range(NT):
                    ins = nc.vector.scalar_tensor_tensor(out=acc[:, t, :], in0=out_ps[:, s, t, :],
                                                         scalar=gates[:, t, bass.ds(e, 1)], in1=acc[:, t, :],
                                                         op0=ALU.mult, op1=ALU.add)
                ins.then_inc(added[s], 1)

            with nc.Block() as block:
                @block.sync
                def _(sp):
                    with nc.sync.Fori(1, E // 2) as p:
                        for s in range(2):
                            sp.wait_ge(b_ready, 4 * p + 2 * s - 2)
                            load_up(sp, 2 * p + s, s)
                            if s == 1:
                                sp.wait_ge(out_done, 2 * p - 1)
                                load_down(sp, 2 * p, 0)
                        sp.wait_ge(out_done, 2 * p)
                        load_down(sp, 2 * p + 1, 1)

                def pe_step(pe, e, s, uses, prev_uses):
                    up(pe, e, s, 0, uses)
                    down(pe, e - 1, 1 - s, prev_uses, 0)
                    up(pe, e, s, 1, uses)
                    down(pe, e - 1, 1 - s, prev_uses, 1)

                @block.tensor
                def _(pe):
                    for f in range(2):
                        up(pe, 0, 0, f, 0)
                    pe_step(pe, 1, 1, 0, 0)
                    with nc.tensor.Fori(1, E // 2) as p:
                        pe_step(pe, 2 * p, 0, p, p - 1)
                        pe_step(pe, 2 * p + 1, 1, p, p)
                    for part in range(2):
                        down(pe, E - 1, 1, E // 2 - 1, part)

                @block.scalar
                def _(act):
                    activate(act, 0, 0, 0)
                    activate(act, 0, 0, 1)
                    activate(act, 1, 1, 0)
                    activate(act, 1, 1, 1)
                    with nc.scalar.Fori(1, E // 2) as p:
                        for s in range(2):
                            for f in range(2):
                                activate(act, 2 * p + s, s, f)

                @block.vector
                def _(dve):
                    for f in range(2):
                        combine(dve, 0, 0, f)
                    for f in range(2):
                        combine(dve, 1, 1, f)
                    add_up(dve, 0, 0, 0)
                    with nc.vector.Fori(1, E // 2) as p:
                        for f in range(2):
                            combine(dve, 2 * p, 0, f)
                        add_up(dve, 2 * p - 1, 1, p - 1)
                        for f in range(2):
                            combine(dve, 2 * p + 1, 1, f)
                        add_up(dve, 2 * p, 0, p)
                    add_up(dve, E - 1, 1, E // 2 - 1)
        residual_norm(k, "norm5", acc, store=store)


def decoder(nc, dram, out):
    with ExitStack() as ctx:
        k = Core(nc, dram, ctx)
        load_and_constants(k)
        context_projections(k)
        mamba(k)
        context_attention(k)
        experts0(k)
        self_attention(k)
        context_attention1(k)
        experts1(k, store=out.rearrange("b (t p) d -> p (b t) d", p=P))


TRANSPOSED = ["L0_attn_W_in", "L0_attn_W_xproj", "L0_attn_W_dt", "L0_attn_W_out", "L1_xattn_Wk", "L1_xattn_Wv",
              "L1_xattn_Wq", "L1_xattn_Wo", "L1_ffn_Wg",
              "L1_attn_a_q", "L1_attn_a_v"]
PER_FEATURE = ["L0_ffn_sb1", "L0_ffn_rb1", "L1_ffn_b1", "L1_ffn_b2"]


def kernel(**inputs):
    import numpy as _np
    import concourse.bacc as _bacc
    from concourse import mybir as _mybir
    from concourse.bass_utils import run_bass_kernel_spmd as _run

    laid = {n: _np.asarray(a) for n, a in inputs.items()}
    laid["x_T"] = laid["x"][0].T
    laid["ctx_T"] = laid.pop("ctx_1024")[0].T
    for n in TRANSPOSED:
        laid[n + "_T"] = laid.pop(n).T
    for n in ("L1_ffn_W1", "L1_ffn_W2", "L1_ffn_W3"):
        laid[n + "_T"] = laid.pop(n).transpose(0, 2, 1)
    for n in PER_FEATURE:
        laid[n + "_p"] = laid.pop(n).reshape(-1, 2, P).transpose(2, 0, 1).reshape(P, -1)
    nc = _bacc.Bacc("TRN2", target_bir_lowering=False, num_devices=1)
    arrays, dram = {}, {}
    for name, a in laid.items():
        a = _np.ascontiguousarray(a)
        arrays[name] = a
        dram[name] = nc.dram_tensor(name, a.shape, _mybir.dt.from_np(a.dtype), kind="ExternalInput").ap()
    out = nc.dram_tensor("out", (1, T, D), F32, kind="ExternalOutput").ap()
    decoder(nc, dram, out)
    r = _run(nc, [arrays], core_ids=[0])
    return r.results[0]["out"]
```

```python
from contextlib import ExitStack

import concourse.bass as bass
from concourse import mybir

F32 = mybir.dt.float32
BF16 = mybir.dt.bfloat16
ALU = mybir.AluOpType
ACT = mybir.ActivationFunctionType
AX = mybir.AxisListType

P = 128
D = 128
T = 1024
NT = T // P
HALF = 512
H = 16
HD = D // H
CTX = 6404
NCH = -(-CTX // P)
TAIL = CTX - (NCH - 1) * P
EPS = 1e-5

AUG = P
SHIFT = 4 * HD
Q_PARTS = (0, 0, 0, 1, 1, 2, 1, 2, 2)
K_PARTS = (0, 1, 2, 0, 1, 0, 2, 1, 2)
USED = len(Q_PARTS) * HD + 3


def slot(s):
    return HD * s if s < 4 else HD * s + 3


def due(count):
    return not (isinstance(count, int) and count <= 0)


class Chain:

    def __init__(self, eng, sem):
        self.eng, self.sem, self.n = eng, sem, 0

    def __call__(self, ins):
        self.n += 1
        ins.then_inc(self.sem, 1)
        self.eng.wait_ge(self.sem, self.n)


class Core:

    def __init__(self, nc, dram, ctx):
        self.nc, self.dram, self.ctx = nc, dram, ctx
        self.norms = 0


    def sb(self, name, shape, dt=F32, ctx=None):
        return (ctx or self.ctx).enter_context(self.nc.sbuf_tensor("sb_" + name, shape, dt))

    def ps(self, name, shape, ctx, dt=F32):
        return ctx.enter_context(self.nc.psum_tensor("ps_" + name, shape, dt))

    def sem(self, name):
        return self.ctx.enter_context(self.nc.semaphore(name))

    def chain(self, dve):
        self.steps.eng = dve
        return self.steps


def load_and_constants(k):
    nc = k.nc
    k.x_tok = k.sb("x_tok", [P, NT, D])
    k.x_T = k.sb("x_T", [P, T])
    k.ident = k.sb("ident", [P, P])
    k.ident_b = k.sb("ident_b", [P, P], BF16)
    k.ones_b = k.sb("ones_b", [P, P], BF16)
    k.steps = Chain(None, k.sem("vector_step"))
    k.var_ready, k.sd_ready = k.sem("norm_var_ready"), k.sem("norm_sd_ready")
    k.tile_ready, k.turned_ready = k.sem("norm_tile_ready"), k.sem("norm_turned_ready")
    k.consts_ready = k.sem("consts_ready")
    k.ident_zeroed = k.sem("ident_zeroed")
    k.ident_ready = k.sem("ident_ready")

    with nc.Block() as block:
        @block.gpsimd
        def _(pool):
            nc.gpsimd.memset(k.ident[:], 0.0).then_inc(k.ident_zeroed, 1)
            pool.wait_ge(k.ident_zeroed, 1)
            nc.gpsimd.affine_select(out=k.ident[:], in_=k.ident[:], compare_op=ALU.not_equal, fill=1.0, base=0,
                                    pattern=[[-1, P]], channel_multiplier=1).then_inc(k.ident_ready, 1)

        @block.vector
        def _(dve):
            nc.vector.memset(k.ones_b[:], 1.0)
            dve.wait_ge(k.ident_ready, 1)
            nc.vector.tensor_copy(k.ident_b[:], k.ident[:]).then_inc(k.consts_ready, 1)


def residual_norm(k, tag, branch, added=False, store=None):
    nc = k.nc
    with ExitStack() as tmp:
        res = branch if added else k.sb(tag + "_res", [P, NT, D], F32, tmp)
        stats = k.sb(tag + "_stats", [P, NT, 6], F32, tmp)
        mv = k.sb(tag + "_mv", [P, NT, 2], F32, tmp)
        var = k.sb(tag + "_var", [P, NT], F32, tmp)
        sd = k.sb(tag + "_sd", [P, NT], F32, tmp)
        rstd = k.sb(tag + "_rstd", [P, NT], F32, tmp)
        turned = k.ps(tag + "_turned", [P, T], tmp)
        stored = k.sem("stored") if store is not None else None
        n = k.norms
        k.norms += 1

        with nc.Block() as block:
            @block.vector
            def _(dve):
                link = k.chain(dve)
                if not added:
                    for h in range(0, NT, 4):
                        link(nc.vector.tensor_tensor(res[:, h:h + 4, :], branch[:, h:h + 4, :], k.x_tok[:, h:h + 4, :],
                                                     ALU.add))
                for t in range(NT):
                    ins = nc.vector.bn_stats(stats[:, t, :], res[:, t, :])
                link(ins)
                for t in range(NT):
                    ins = nc.vector.bn_aggr(mv[:, t, :], stats[:, t, :])
                link(ins)
                nc.vector.tensor_scalar(var[:], mv[:, :, 1], EPS, None, ALU.add).then_inc(k.var_ready, 1)
                dve.wait_ge(k.sd_ready, n + 1)
                link(nc.vector.reciprocal(rstd[:], sd[:]))
                for t in range(NT):
                    nc.vector.tensor_scalar(k.x_tok[:, t, :], res[:, t, :], mv[:, t, 0:1], rstd[:, t:t + 1],
                                            ALU.subtract, ALU.mult).then_inc(k.tile_ready, 1)

            @block.scalar
            def _(act):
                nc.scalar.preload_act_table(ACT.Sqrt)
                act.wait_ge(k.var_ready, n + 1)
                nc.scalar.activation(sd[:], var[:], ACT.Sqrt).then_inc(k.sd_ready, 1)
                if store is None:
                    for h in range(2):
                        act.wait_ge(k.turned_ready, 2 * n + h + 1)
                        nc.scalar.copy(k.x_T[:, h * HALF:(h + 1) * HALF], turned[:, h * HALF:(h + 1) * HALF])

            @block.tensor
            def _(pe):
                if store is None:
                    for t in range(NT):
                        pe.wait_ge(k.tile_ready, NT * n + t + 1)
                        ins = nc.tensor.transpose(turned[:, t * P:(t + 1) * P], k.x_tok[:, t, :], k.ident[:])
                        if t % 4 == 3:
                            ins.then_inc(k.turned_ready, 1)

            @block.sync
            def _(sp):
                if store is not None:
                    for h in range(2):
                        sp.wait_ge(k.tile_ready, NT * n + 4 * h + 4)
                        sp.dma_start(store[:, 4 * h:4 * h + 4, :], k.x_tok[:, 4 * h:4 * h + 4, :]).then_inc(stored, 16)
                    sp.wait_ge(stored, 32)


def lay_out(k):
    k.key1_T = k.sb("key1_T", [P, CTX])
    k.val1 = k.sb("val1", [P, NCH, D])
    k.params = Params(k)
    k.wk1 = k.sb("wk1", [P, D])
    k.wv1 = k.sb("wv1", [P, D])
    k.layer0 = k.ctx.enter_context(ExitStack())
    k.ctx_T = k.sb("ctx_T", [P, CTX], F32, k.layer0)
    k.key_stack = k.sb("key_stack", [AUG, NCH * P], BF16, k.layer0)
    k.val_ones = k.sb("val_ones", [P, NCH, 32], F32, k.layer0)
    k.x_loaded, k.layer1_loaded = k.sem("x_loaded"), k.sem("layer1_loaded")


class Params:
    LOADS = 26
    E0, E1 = 16, 8
    RANK = 16

    def __init__(self, k):
        self.loaded = k.sem("params_loaded")
        self.x0_w_q, self.x0_w_concat = k.sb("x0_w_q", [P, D]), k.sb("x0_w_concat", [P, D])
        self.e0_gw, self.e0_gb = k.sb("e0_gw", [P, self.E0 - 1]), k.sb("e0_gb", [P, self.E0 - 1])
        self.e0_b1, self.e0_b2 = k.sb("e0_b1", [P, 2 * self.E0 + 2]), k.sb("e0_b2", [self.E0, D])
        self.s_w, self.s_b_feat, self.s_b_k = k.sb("s_w_qkv", [P, 3 * D]), k.sb("s_b_feat", [P, 3]), k.sb("s_b_k", [P, D])
        self.s_lora_a = k.sb("s_lora_a", [self.RANK, 2, H, HD])
        self.s_lora_b = k.sb("s_lora_b", [self.RANK, 2, H, HD])
        self.s_w_proj, self.s_b_proj = k.sb("s_w_proj", [P, D]), k.sb("s_b_proj", [P, D])
        self.x1_w_q, self.x1_b_q = k.sb("x1_w_q", [P, D]), k.sb("x1_b_q", [P, 1])
        self.x1_w_out, self.x1_b_v, self.x1_b_out = k.sb("x1_w_out", [P, D]), k.sb("x1_b_v", [P, D]), k.sb("x1_b_out", [P, D])
        self.e1_wg, self.e1_b3 = k.sb("e1_wg", [P, self.E1]), k.sb("e1_b3", [self.E1, D])
        self.e1_b1, self.e1_b2 = k.sb("e1_b1", [P, 2 * self.E1]), k.sb("e1_b2", [P, 2 * self.E1])

    def load(self, k, sp):
        d, sem = k.dram, self.loaded

        def everywhere(row):
            return row.unsqueeze(0).to_broadcast([P, row.shape[0]])
        sp.dma_start(self.x0_w_q[:], d["L0_xattn_w_q"]).then_inc(sem, 16)
        sp.dma_start(self.x0_w_concat[:], d["L0_xattn_w_concat"]).then_inc(sem, 16)
        sp.dma_start(self.e0_gw[:], d["L0_ffn_gW"]).then_inc(sem, 16)
        sp.dma_start(self.e0_gb[:], everywhere(d["L0_ffn_gb"])).then_inc(sem, 16)
        sp.dma_start(self.e0_b1[:, 0:4], d["L0_ffn_sb1_p"]).then_inc(sem, 16)
        sp.dma_start(self.e0_b1[:, 4:], d["L0_ffn_rb1_p"]).then_inc(sem, 16)
        sp.dma_start(self.e0_b2[0:1, :], d["L0_ffn_sb2"]).then_inc(sem, 16)
        sp.dma_start(self.e0_b2[1:, :], d["L0_ffn_rb2"]).then_inc(sem, 16)
        sp.dma_start(self.s_w[:], d["L1_attn_w_qkv"]).then_inc(sem, 16)
        sp.dma_start(self.s_b_k[:], everywhere(d["L1_attn_b_qkv"][D:2 * D])).then_inc(sem, 16)
        with k.nc.allow_non_contiguous_dma(reason="a few floats to a partition; 256 of a LoRA matrix"):
            sp.dma_start(self.s_b_feat[:], d["L1_attn_b_qkv"].rearrange("(s p) -> p s", p=P)).then_inc(sem, 16)
            sp.dma_start(self.x1_b_q[:], d["L1_xattn_bq"].unsqueeze(1)).then_inc(sem, 16)
            for i, n in enumerate("qv"):
                for dst, src in ((self.s_lora_a, f"L1_attn_a_{n}_T"), (self.s_lora_b, f"L1_attn_b_{n}")):
                    sp.dma_start(dst[:, i], d[src].unsqueeze(1).to_broadcast([self.RANK, H, HD])).then_inc(sem, 16)
        sp.dma_start(self.s_w_proj[:], d["L1_attn_w_proj"]).then_inc(sem, 16)
        sp.dma_start(self.s_b_proj[:], everywhere(d["L1_attn_b_proj"])).then_inc(sem, 16)
        sp.dma_start(self.x1_w_q[:], d["L1_xattn_Wq_T"]).then_inc(sem, 16)
        sp.dma_start(self.x1_w_out[:], d["L1_xattn_Wo_T"]).then_inc(sem, 16)
        sp.dma_start(self.x1_b_v[:], everywhere(d["L1_xattn_bv"])).then_inc(sem, 16)
        sp.dma_start(self.x1_b_out[:], everywhere(d["L1_xattn_bo"])).then_inc(sem, 16)
        sp.dma_start(self.e1_wg[:], d["L1_ffn_Wg_T"]).then_inc(sem, 16)
        sp.dma_start(self.e1_b3[:], d["L1_ffn_b3"]).then_inc(sem, 16)
        sp.dma_start(self.e1_b1[:], d["L1_ffn_b1_p"]).then_inc(sem, 16)
        sp.dma_start(self.e1_b2[:], d["L1_ffn_b2_p"]).then_inc(sem, 16)


class ContextKeys:

    CUT = 26
    TURNS = -(-NCH // 8)

    def __init__(self, k, banks):
        self.k = k
        early, at = k.key1_T[:], 0

        def take(n, dt=F32):
            nonlocal at
            words = n if dt == F32 else n // 2
            at += words
            x = early[:, at - words:at]
            assert at <= CTX - T
            return x if dt == F32 else x.bitcast(BF16)
        self.stack_tok = take(NCH * AUG, BF16).rearrange("p (c r) -> p c r", c=NCH)
        self.k_tok = take(NCH * HD).rearrange("p (c e) -> p c e", c=NCH)
        self.part = [take(NCH * HD, BF16).rearrange("p (c e) -> p c e", c=NCH) for i in range(3)]
        self.rest = [take(NCH * HD).rearrange("p (c e) -> p c e", c=NCH) for i in range(2)]
        self.kv_ps = banks[:, 0:2 * HALF].rearrange("p (c e) -> p c e", e=2 * HD)
        self.turn_ps = banks.bitcast(BF16).rearrange("p (b n) -> p b n", b=4)
        self.w_loaded, self.ctx_loaded = k.sem("w_kv_loaded"), [k.sem(f"ctx_loaded{i}") for i in range(2)]
        self.kv_ready, self.zeroed, self.stack_ready = k.sem("kv_ready"), k.sem("k_stack_zeroed"), k.sem("k_stack_ready")
        self.kv_taken = k.sem("kv_taken")
        self.turned, self.used_dve, self.used_act = (k.sem("k_turned"), k.sem("k_turn_used_dve"),
                                                     k.sem("k_turn_used_act"))

    def load(self, eng, i):
        cols = slice(0, self.CUT * P) if i == 0 else slice(self.CUT * P, CTX)
        eng.dma_start(self.k.ctx_T[:, cols], self.k.dram["ctx_T"][:, cols]).then_inc(self.ctx_loaded[i], 16)

    def products(self, pe, w_kv, chunks):
        nc, k = self.k.nc, self.k
        for c in chunks:
            n = P if c < NCH - 1 else TAIL
            if c in (0, self.CUT):
                pe.wait_ge(self.ctx_loaded[1 if c else 0], 16)
            ins = nc.tensor.matmul(self.kv_ps[0:n, c, :], k.ctx_T[:, c * P:c * P + n], w_kv[:], start=True, stop=True)
        if NCH - 1 in chunks:
            ins.then_inc(self.kv_ready, 1)

    def turn(self, pe):
        nc, k = self.k.nc, self.k
        pe.wait_ge(self.stack_ready, 1)
        pe.wait_ge(self.kv_taken, 1)
        for c in range(NCH):
            n = P if c < NCH - 1 else TAIL
            g = c // 8
            if c % 8 == 0 and g >= 4:
                pe.wait_ge(self.used_act if g % 2 else self.used_dve, (g - 4) // 2 + 1)
            ins = nc.tensor.transpose(self.turn_ps[0:AUG, g % 4, (c % 8) * P:(c % 8) * P + n],
                                      self.stack_tok[0:n, c, :], k.ident_b[0:n, 0:n])
            if c % 8 == 7 or c == NCH - 1:
                ins.then_inc(self.turned, 1)

    def copy_turned(self, eng, copy, parity, used):
        for g in range(parity, self.TURNS, 2):
            cols = min(8 * P, CTX - g * 8 * P)
            eng.wait_ge(self.turned, g + 1)
            copy(self.k.key_stack[:, g * 8 * P:g * 8 * P + cols], self.turn_ps[0:AUG, g % 4, 0:cols]).then_inc(used, 1)

    def zero(self, pool):
        nc = self.k.nc
        nc.gpsimd.memset(self.stack_tok[:, :, SHIFT:SHIFT + 3], 1.0)
        nc.gpsimd.memset(self.stack_tok[:, :, USED:AUG], 0.0).then_inc(self.zeroed, 1)
        nc.gpsimd.memset(self.k.key_stack[:, CTX:], 0.0)

    def prepare(self, dve, link):
        nc, k, full = self.k.nc, self.k, NCH - 1
        nc.vector.memset(self.k_tok[:, full, :], 0.0)
        link(nc.vector.memset(k.val_ones[:], 0.0))
        nc.vector.memset(k.val_ones[:, 0:full, HD:HD + 1], 1.0)
        link(nc.vector.memset(k.val_ones[0:TAIL, full, HD:HD + 1], 1.0))

    def stack(self, dve, link):
        nc, k, full = self.k.nc, self.k, NCH - 1
        dve.wait_ge(self.kv_ready, 1)
        nc.vector.tensor_copy(self.k_tok[:, 0:full, :], self.kv_ps[:, 0:full, 0:HD])
        link(nc.vector.tensor_copy(self.k_tok[0:TAIL, full, :], self.kv_ps[0:TAIL, full, 0:HD]))
        nc.vector.tensor_copy(k.val_ones[:, 0:full, 0:HD], self.kv_ps[:, 0:full, HD:2 * HD])
        nc.vector.tensor_copy(k.val_ones[0:TAIL, full, 0:HD], self.kv_ps[0:TAIL, full, HD:2 * HD]).then_inc(self.kv_taken, 1)
        split(nc, link, self.k_tok, self.part, self.rest)
        dve.wait_ge(self.zeroed, 1)
        for s, which in enumerate(K_PARTS):
            ins = nc.vector.tensor_copy(self.stack_tok[:, :, slot(s):slot(s) + HD], self.part[which])
        ins.then_inc(self.stack_ready, 1)


def split(nc, link, whole, part, rest):
    link(nc.vector.tensor_copy(part[0], whole))
    link(nc.vector.tensor_tensor(rest[0], whole, part[0], ALU.subtract))
    link(nc.vector.tensor_copy(part[1], rest[0]))
    link(nc.vector.tensor_tensor(rest[1], rest[0], part[1], ALU.subtract))
    link(nc.vector.tensor_copy(part[2], rest[1]))


def mamba(k):
    nc, d = k.nc, k.dram
    DI, NS, DR, KC = 2 * D, 16, D // 16, 4
    ROWS = DR + 2 * NS
    LOADS = 6
    ctx = ExitStack()
    with ctx:
        w_in = k.sb("w_in_T", [P, 2 * DI], F32, ctx)
        w_conv = k.sb("w_conv", [P, 2, KC], F32, ctx)
        w_x = k.sb("w_xproj_T", [P, 2, ROWS], F32, ctx)
        w_dt = k.sb("w_dt_T", [DR, DI], F32, ctx)
        b_dt = k.sb("b_dt", [P, 2], F32, ctx)
        a_log = k.sb("a_log", [P, 2, NS], F32, ctx)
        a_neg = k.sb("a_neg", [P, 2, NS], F32, ctx)
        d_skip = k.sb("d_skip", [P, 2], F32, ctx)
        w_out = k.sb("w_out_T", [P, 2, D], F32, ctx)
        diag = k.sb("d_diag", [P, 2, P], F32, ctx)
        PAD = KC - 1
        xpad = k.sb("xpad", [P, 2, PAD + T], F32, ctx)
        zs = k.sb("z_silu", [P, 2, T], F32, ctx)
        conv = k.sb("conv", [P, 2, T], F32, ctx)
        xc = k.sb("xc", [P, 2, T], F32, ctx)
        delta = k.sb("delta", [P, 2, T], F32, ctx)
        u = k.sb("u", [P, 2, T], F32, ctx)
        dbc = k.key1_T[0:ROWS, CTX - T:]
        bc_rows = k.sb("bc_rows", [P, NS, T], BF16, ctx)
        pick = k.sb("bc_pick", [P, 2, P], BF16, ctx)
        early = k.val1[:].rearrange("p c e -> p (c e)")
        decay = early[:, 0:2 * T].rearrange("p (s t) -> p s t", s=2)
        c_all = early[:, 2 * T:4 * T].rearrange("p (s t) -> p s t", s=2)
        state = early[:, 4 * T:6 * T].rearrange("p (s t) -> p s t", s=2)
        dbc_part = [state[0:ROWS, i // 2, (i % 2) * HALF:(i % 2 + 1) * HALF].bitcast(BF16) for i in range(3)]
        dbc_rest = [decay[0:ROWS, i, :] for i in range(2)]
        read = xpad[:, :, 0:T]
        soft = drive = conv

        w_kv = k.sb("w_kv", [P, 2 * HD], F32, ctx)

        in_loaded, conv_loaded, loaded = k.sem("mamba_in_loaded"), k.sem("w_conv_loaded"), k.sem("mamba_loaded")
        xz_ready, xpad_ready, conv_ready = k.sem("xz_ready"), k.sem("xpad_ready"), k.sem("conv_ready")
        xc_ready, z_used, dbc_ready, dbc_copied = k.sem("xc_ready"), k.sem("z_used"), k.sem("dbc_ready"), k.sem("dbc_copied")
        dbc_split, dlt_ready, log_ready = k.sem("dbc_split"), k.sem("dlt_ready"), k.sem("log_ready")
        act_step, a_exp = k.sem("mamba_act_step"), k.sem("a_exp")
        rows_moved, pick_set, rows_zeroed = k.sem("rows_moved"), k.sem("pick_set"), k.sem("bc_rows_zeroed")
        b_ready, c_ready, b_used, c_copied = k.sem("b_ready"), k.sem("c_ready"), k.sem("b_used"), k.sem("c_copied")
        decay_ready, read_ready, y_added = k.sem("decay_ready"), k.sem("read_ready"), k.sem("y_added")
        scanned = k.sem("scanned")
        gated, out_ready = k.sem("y_gated"), k.sem("mamba_out_ready")

        with ExitStack() as front:
            front_ps = k.ps("front_ps", [P, 4, T], front)
            xz = [front_ps[:, c, :] for c in range(4)]
            keys = ContextKeys(k, front_ps[:, 0:2, :].rearrange("p c t -> p (c t)"))
            with nc.Block() as block:
                @block.sync
                def _(sp):
                    sp.dma_start(w_in[:], d["L0_attn_W_in_T"]).then_inc(in_loaded, 16)
                    sp.dma_start(k.x_T[:], d["x_T"]).then_inc(in_loaded, 16)
                    sp.dma_start(w_conv[:], d["L0_attn_W_conv"].rearrange("(s p) o k -> p s (o k)", p=P)).then_inc(conv_loaded, 16)
                    sp.dma_start(w_kv[:], d["L0_xattn_w_kv"]).then_inc(keys.w_loaded, 16)
                    with nc.allow_non_contiguous_dma(reason="two floats to a partition"):
                        sp.dma_start(d_skip[:], d["L0_attn_D"].rearrange("(s p) -> p s", p=P)).then_inc(loaded, 16)
                    keys.load(sp, 0)
                    sp.dma_start(w_x[:], d["L0_attn_W_xproj_T"].rearrange("(s p) r -> p s r", p=P)).then_inc(loaded, 16)
                    sp.dma_start(w_dt[:], d["L0_attn_W_dt_T"]).then_inc(loaded, 16)
                    with nc.allow_non_contiguous_dma(reason="two floats to a partition"):
                        sp.dma_start(b_dt[:], d["L0_attn_b_dt"].rearrange("(s p) -> p s", p=P)).then_inc(loaded, 16)
                    sp.dma_start(a_log[:], d["L0_attn_A_log"].rearrange("(s p) n -> p s n", p=P)).then_inc(loaded, 16)
                    sp.dma_start(w_out[:], d["L0_attn_W_out_T"].rearrange("(s p) m -> p s m", p=P)).then_inc(loaded, 16)
                    sp.dma_start(k.wk1[:], d["L1_xattn_Wk_T"]).then_inc(k.layer1_loaded, 16)
                    sp.dma_start(k.wv1[:], d["L1_xattn_Wv_T"]).then_inc(k.layer1_loaded, 16)
                    k.params.load(k, sp)
                    sp.wait_ge(dbc_split, 1)
                    sp.wait_ge(rows_zeroed, 1)
                    for i in range(3):
                        for base, first in ((0, DR), (3, DR + NS)):
                            sp.dma_start(bc_rows[base + i:base + i + 1, :, :],
                                         dbc_part[i][first:first + NS, :]).then_inc(rows_moved, 16)
                    sp.wait_ge(rows_moved, 16 * 6)
                    sp.wait_ge(k.x_loaded, 16)
                    sp.wait_ge(k.layer1_loaded, 32)
                    sp.wait_ge(k.params.loaded, 16 * Params.LOADS)

                @block.gpsimd
                def _(pool):
                    keys.zero(pool)
                    nc.gpsimd.memset(pick[:], 1.0).then_inc(pick_set, 1)
                    pool.wait_ge(pick_set, 1)
                    nc.gpsimd.affine_select(out=pick[:, 0, :], in_=pick[:, 0, :], compare_op=ALU.is_ge, fill=0.0, base=2,
                                            pattern=[[0, P]], channel_multiplier=-1)
                    nc.gpsimd.affine_select(out=pick[:, 1, :], in_=pick[:, 1, :], compare_op=ALU.is_ge, fill=0.0, base=-3,
                                            pattern=[[0, P]], channel_multiplier=1).then_inc(pick_set, 1)
                    pool.wait_ge(pick_set, 2)
                    nc.gpsimd.affine_select(out=pick[:, 1, :], in_=pick[:, 1, :], compare_op=ALU.is_ge, fill=0.0, base=5,
                                            pattern=[[0, P]], channel_multiplier=-1)
                    nc.gpsimd.memset(bc_rows[:], 0.0).then_inc(rows_zeroed, 1)

                @block.tensor
                def _(pe):
                    pe.wait_ge(in_loaded, 32)
                    for c in range(4):
                        for h in range(2):
                            ins = nc.tensor.matmul(xz[c][:, h * HALF:(h + 1) * HALF], w_in[:, c * P:(c + 1) * P],
                                                   k.x_T[:, h * HALF:(h + 1) * HALF], start=True, stop=True)
                        ins.then_inc(xz_ready, 1)
                    pe.wait_ge(keys.w_loaded, 16)
                    pe.wait_ge(xpad_ready, 2)
                    keys.products(pe, w_kv, range(0, keys.CUT - 6))
                    pe.wait_ge(loaded, 16 * LOADS)
                    pe.wait_ge(xc_ready, 2)
                    for h in range(2):
                        for s in range(2):
                            ins = nc.tensor.matmul(xz[1][0:ROWS, h * HALF:(h + 1) * HALF], w_x[:, s, :],
                                                   xc[:, s, h * HALF:(h + 1) * HALF], start=(s == 0), stop=(s == 1))
                    ins.then_inc(dbc_ready, 1)
                    keys.products(pe, w_kv, range(keys.CUT - 6, keys.CUT + 2))
                    pe.wait_ge(dbc_copied, 1)
                    pe.wait_ge(z_used, 2)
                    for s in range(2):
                        for h in range(2):
                            ins = nc.tensor.matmul(xz[2 + s][:, h * HALF:(h + 1) * HALF], w_dt[:, s * P:(s + 1) * P],
                                                   dbc[0:DR, h * HALF:(h + 1) * HALF], start=True, stop=True)
                        ins.then_inc(dlt_ready, 1)
                    keys.products(pe, w_kv, range(keys.CUT + 2, NCH))
                    keys.turn(pe)

                @block.scalar
                def _(act):
                    act.wait_ge(in_loaded, 32)
                    keys.load(act, 1)
                    act.dma_start(k.x_tok[:], d["x"].rearrange("b (t p) d -> p (b t) d", p=P)).then_inc(k.x_loaded, 16)
                    link = Chain(act, act_step)
                    for s in range(2):
                        act.wait_ge(xz_ready, s + 1)
                        nc.scalar.copy(xpad[:, s, PAD:PAD + T], xz[s]).then_inc(xpad_ready, 1)
                    for s in range(2):
                        act.wait_ge(xz_ready, 3 + s)
                        nc.scalar.activation(zs[:, s, :], xz[2 + s], ACT.Silu).then_inc(z_used, 1)
                    for s in range(2):
                        act.wait_ge(conv_ready, s + 1)
                        nc.scalar.activation(xc[:, s, :], conv[:, s, :], ACT.Silu).then_inc(xc_ready, 1)
                    act.wait_ge(loaded, 16 * LOADS)
                    nc.scalar.activation(a_neg[:], a_log[:], ACT.Exp).then_inc(a_exp, 1)
                    for s in range(2):
                        act.wait_ge(dlt_ready, s + 1)
                        link(nc.scalar.activation(soft[:, s, :], xz[2 + s], ACT.Abs, bias=b_dt[:, s:s + 1]))
                    for s in range(2):
                        link(nc.scalar.activation(soft[:, s, :], soft[:, s, :], ACT.Exp, scale=-1.0))
                    for s in range(2):
                        nc.scalar.activation(soft[:, s, :], soft[:, s, :], ACT.Ln, bias=1.0).then_inc(log_ready, 1)
                    keys.copy_turned(act, nc.scalar.copy, 1, keys.used_act)

                @block.vector
                def _(dve):
                    link = k.chain(dve)
                    link(nc.vector.memset(xpad[:, :, 0:PAD], 0.0))
                    keys.prepare(dve, link)
                    dve.wait_ge(conv_loaded, 16)
                    for s in range(2):
                        dve.wait_ge(xpad_ready, s + 1)
                        link(nc.vector.tensor_scalar(conv[:, s, :], xpad[:, s, 0:T], w_conv[:, s, 0:1], None, ALU.mult))
                        for j in range(1, KC):
                            ins = nc.vector.scalar_tensor_tensor(
                                out=conv[:, s, :], in0=xpad[:, s, j:j + T], scalar=w_conv[:, s, j:j + 1],
                                in1=conv[:, s, :], op0=ALU.mult, op1=ALU.add)
                            if j < KC - 1:
                                link(ins)
                        ins.then_inc(conv_ready, 1)
                    dve.wait_ge(k.consts_ready, 1)
                    dve.wait_ge(loaded, 16 * LOADS)
                    for s in range(2):
                        nc.vector.tensor_scalar(diag[:, s, :], k.ident[:], d_skip[:, s:s + 1], None, ALU.mult)
                    dve.wait_ge(dbc_ready, 1)
                    nc.vector.tensor_copy(dbc[:], xz[1][0:ROWS, :]).then_inc(dbc_copied, 1)
                    dve.wait_ge(dbc_copied, 1)
                    split(nc, link, dbc, dbc_part, dbc_rest)
                    nc.vector.engine_nop().then_inc(dbc_split, 1)
                    keys.stack(dve, link)
                    dve.wait_ge(a_exp, 1)
                    link(nc.vector.tensor_scalar(a_neg[:], a_neg[:], -1.0, None, ALU.mult))
                    for s in range(2):
                        dve.wait_ge(log_ready, s + 1)
                        link(nc.vector.tensor_scalar(delta[:, s, :], xz[2 + s], b_dt[:, s:s + 1], 0.0, ALU.add, ALU.max))
                        link(nc.vector.tensor_tensor(delta[:, s, :], delta[:, s, :], soft[:, s, :], ALU.add))
                        nc.vector.tensor_tensor(u[:, s, :], delta[:, s, :], xc[:, s, :], ALU.mult)
                    keys.copy_turned(dve, nc.vector.tensor_copy, 0, keys.used_dve)

        y = [k.ps(f"y{s}", [P, T], ctx) for s in range(2)]
        b_all = k.ps("b_all", [P, T], ctx)
        out_ps = b_all[:].rearrange("p (t e) -> p t e", t=NT)
        with ExitStack() as mid:
            c_ps = k.ps("c_all", [P, T], mid)

            def spread(pe, dst, which, n, ready):
                for h in range(2):
                    ins = nc.tensor.matmul(dst[:, h * HALF:(h + 1) * HALF], pick[:, which, :],
                                           bc_rows[:, n, h * HALF:(h + 1) * HALF], start=True, stop=True)
                ins.then_inc(ready, 1)

            def next_b(pe, n):
                pe.wait_ge(b_used, 2 * n)
                spread(pe, b_all, 0, n, b_ready)

            def next_c(pe, n):
                pe.wait_ge(c_copied, n)
                spread(pe, c_ps, 1, n, c_ready)

            def add_read(pe, n, s):
                pe.wait_ge(read_ready, 2 * n + s + 1)
                for h in range(2):
                    ins = nc.tensor.matmul(y[s][:, h * HALF:(h + 1) * HALF], k.ident[:],
                                           read[:, s, h * HALF:(h + 1) * HALF], start=False, stop=True,
                                           skip_group_check=True)
                ins.then_inc(y_added, 1)

            def decay_and_c(act, n, parity, first):
                for s in range(2):
                    if not first:
                        act.wait_ge(scanned, 2 * n + s - 1)
                    nc.scalar.activation(decay[:, s, :], delta[:, s, :], ACT.Exp,
                                         scale=a_neg[:, s, bass.ds(n, 1)]).then_inc(decay_ready, 1)
                act.wait_ge(c_ready, n + 1)
                if not (isinstance(n, int) and n < 2):
                    act.wait_ge(read_ready, 2 * n - 2)
                nc.scalar.copy(c_all[:, parity, :], c_ps[:]).then_inc(c_copied, 1)

            def scan(dve, n, first):
                dve.wait_ge(b_ready, n + 1)
                for s in range(2):
                    if not first:
                        dve.wait_ge(scanned, 2 * n + s - 1)
                    nc.vector.tensor_tensor(drive[:, s, :], b_all[:], u[:, s, :], ALU.mult).then_inc(b_used, 1)
                for s in range(2):
                    dve.wait_ge(b_used, 2 * n + s + 1)
                    dve.wait_ge(decay_ready, 2 * n + s + 1)
                    if not first:
                        dve.wait_ge(read_ready, 2 * n + s - 1)
                    nc.vector.tensor_tensor_scan(state[:, s, :], decay[:, s, :], drive[:, s, :], 0.0,
                                                 ALU.mult, ALU.add).then_inc(scanned, 1)

            def read_out(pool, n, parity, first):
                pool.wait_ge(c_copied, n + 1)
                for s in range(2):
                    pool.wait_ge(scanned, 2 * n + s + 1)
                    if not first:
                        pool.wait_ge(y_added, 2 * n + s - 1)
                    nc.gpsimd.tensor_tensor(read[:, s, :], state[:, s, :], c_all[:, parity, :], ALU.mult).then_inc(read_ready, 1)

            with nc.Block() as block:
                @block.tensor
                def _(pe):
                    spread(pe, b_all, 0, 0, b_ready)
                    spread(pe, c_ps, 1, 0, c_ready)
                    for s in range(2):
                        for h in range(2):
                            nc.tensor.matmul(y[s][:, h * HALF:(h + 1) * HALF], diag[:, s, :],
                                             xc[:, s, h * HALF:(h + 1) * HALF], start=True, stop=True,
                                             skip_group_check=True)
                    next_b(pe, 1)
                    next_c(pe, 1)
                    with nc.tensor.Fori(1, NS - 1) as n:
                        add_read(pe, n - 1, 0)
                        next_b(pe, n + 1)
                        add_read(pe, n - 1, 1)
                        next_c(pe, n + 1)
                    for n in (NS - 2, NS - 1):
                        for s in range(2):
                            add_read(pe, n, s)
                    pe.wait_ge(gated, 2)
                    for t in range(NT):
                        for s in range(2):
                            ins = nc.tensor.matmul(out_ps[:, t, :], state[:, s, t * P:(t + 1) * P], w_out[:, s, :],
                                                   start=(s == 0), stop=(s == 1))
                    ins.then_inc(out_ready, 1)

                @block.scalar
                def _(act):
                    nc.scalar.preload_act_table(ACT.Exp)
                    decay_and_c(act, 0, 0, True)
                    decay_and_c(act, 1, 1, False)
                    with nc.scalar.Fori(1, NS // 2) as p:
                        for parity in range(2):
                            decay_and_c(act, 2 * p + parity, parity, False)

                @block.vector
                def _(dve):
                    scan(dve, 0, True)
                    with nc.vector.Fori(1, NS) as n:
                        scan(dve, n, False)
                    for s in range(2):
                        dve.wait_ge(y_added, 2 * NS - 1 + s)
                        nc.vector.tensor_tensor(state[:, s, :], y[s][:], zs[:, s, :], ALU.mult).then_inc(gated, 1)

                @block.gpsimd
                def _(pool):
                    read_out(pool, 0, 0, True)
                    read_out(pool, 1, 1, False)
                    with nc.gpsimd.Fori(1, NS // 2) as p:
                        for parity in range(2):
                            read_out(pool, 2 * p + parity, parity, False)
        residual_norm(k, "norm0", out_ps)


def stack_queries(nc, link, whole, part, rest, stack, parts):
    split(nc, link, whole, part, rest)
    for s, which in enumerate(parts):
        ins = nc.vector.tensor_copy(stack[:, :, slot(s):slot(s) + HD], part[which])
    return ins


def negated_maximum(nc, link, partial, neg, rests, part3):
    link(nc.vector.tensor_reduce(neg, partial, AX.X, ALU.max, negate=True))
    link(nc.vector.tensor_copy(part3[:, :, 0], neg))
    link(nc.vector.tensor_tensor(rests[0], neg, part3[:, :, 0], ALU.subtract))
    link(nc.vector.tensor_copy(part3[:, :, 1], rests[0]))
    link(nc.vector.tensor_tensor(rests[1], rests[0], part3[:, :, 1], ALU.subtract))
    return nc.vector.tensor_copy(part3[:, :, 2], rests[1])


def context_attention(k):
    nc = k.nc
    HB = H // 2
    BLK = HB * P
    NB = NT * H // HB
    QUART = BLK // 4
    JOBS = BLK // HALF
    WIDE = 2 * HALF
    RANGES = [(c0, min(WIDE, CTX - c0)) for c0 in range(0, CTX, WIDE)]
    NR = len(RANGES)
    UNITS = HB * NR
    ctx = ExitStack()
    with ctx:
        stack_T = k.sb("q_stack_T", [AUG, NB, BLK], BF16, ctx)
        gathered = k.sb("gathered", [P, NB, QUART], F32, ctx)
        w_q, w_out = k.params.x0_w_q, k.params.x0_w_concat
        with ExitStack() as tmp:
            early = k.val1[:].rearrange("p c e -> p (c e)")
            q_tok, *q_rest = [early[:, i * T:(i + 1) * T].rearrange("p (a b) -> p a b", b=HD) for i in range(3)]
            q_part = [early[:, (6 + i) * T // 2:(7 + i) * T // 2].bitcast(BF16).rearrange("p (a b) -> p a b", b=HD)
                      for i in range(3)]
            stack = k.sb("q_stack", [P, NT * H, AUG], BF16, tmp)
            ZEROED = 3 * NT * H // 4
            probs = k.sb("probs", [P, 3, BLK], F32, tmp)
            partial = k.sb("max_partial", [P, HB, NR], F32, tmp)
            neg = k.sb("neg_max", [P, HB], F32, tmp)
            rests = [k.sb(f"neg_rest{i}", [P, HB], F32, tmp) for i in range(2)]
            part3 = k.sb("neg_part", [P, HB, 3], BF16, tmp)
            score_ps = k.ps("score_ps", [P, 3, HALF], tmp)
            max_ps = k.ps("max_ps", [P, 2, WIDE], tmp)
            acc_ps = k.ps("acc_ps", [P, HALF], tmp)
            shift_ps = max_ps[:, 0, 0:HALF].bitcast(BF16)
            steps_before = k.steps.n
            SPLIT_STEPS = 6
            q_ps = max_ps[:, 0, :]
            q_made, pad_zeroed, stack_ready = k.sem("q_made"), k.sem("q_stack_zeroed"), k.sem("q_stack_ready")
            turned, first_copied, turn_copied = k.sem("q_turned"), k.sem("q_first_copied"), k.sem("q_turn_copied")
            q_ready = k.sem("q_block_ready")
            unit_ready, unit_used, parts_ready, shift_turned = (k.sem("max_ready"), k.sem("max_used"),
                                                                k.sem("neg_parts_ready"), k.sem("shift_turned"))
            score_ready, exp_done, pv_done, acc_used = (k.sem("score_ready"), k.sem("exp_done"), k.sem("pv_done"),
                                                        k.sem("acc_used"))
            job_ready, job_copied = k.sem("layer1_job_ready"), k.sem("layer1_job_copied")
            EXPS = NCH * JOBS
            LINKED = 5

            def at(blk):
                return blk if isinstance(blk, int) else bass.ds(blk, 1)

            def columns(blk, c0, n):
                x = stack_T[:, at(blk), c0:c0 + n]
                return x if isinstance(blk, int) else x.rearrange("p o c -> p (o c)")

            def max_unit(pe, blk, u):
                h, r = u // NR, u % NR
                if not (isinstance(blk, int) and blk == 0 and u < 2):
                    pe.wait_ge(unit_used, blk * UNITS + u - 1)
                c0, cols = RANGES[r]
                for a in range(0, cols, HALF):
                    n = min(HALF, cols - a)
                    ins = nc.tensor.matmul(max_ps[:, u % 2, a:a + n], columns(blk, h * P, P),
                                           k.key_stack[:, c0 + a:c0 + a + n], start=True, stop=True)
                ins.then_inc(unit_ready, 1)

            def turn_shift(pe, blk):
                pe.wait_ge(parts_ready, blk + 1)
                for h in range(HB):
                    ins = nc.tensor.transpose(shift_ps[0:3, h * P:(h + 1) * P], part3[:, h, :], k.ident_b[:])
                ins.then_inc(shift_turned, 1)

            def turn_block(pe, b):
                if b == 2:
                    pe.wait_ge(first_copied, 1)
                elif b > 2:
                    pe.wait_ge(turn_copied, b - 2)
                for h in range(HB):
                    ins = nc.tensor.transpose(turn_bank(b)[:, h * P:(h + 1) * P], stack[:, b * HB + h, :], k.ident_b[:])
                ins.then_inc(turned, 1)

            def turn_bank(b):
                return score_ps[:, b % 2, :].bitcast(BF16)

            def copy_block(act, b):
                act.wait_ge(turned, b + 1)
                nc.scalar.copy(stack_T[:, b, :], turn_bank(b)).then_inc(turn_copied, 1)

            key_jobs = [(c0, min(HALF, CTX - c0)) for c0 in range(0, CTX, HALF)]
            val_jobs = [(c, min(4, NCH - 1 - c)) for c in range(0, NCH - 1, 4)] + [(NCH - 1, 1)]
            JOBS1 = len(key_jobs) + len(val_jobs)

            def job_bank(i):
                return acc_ps[:] if i % 2 else score_ps[:, 2, :]

            def jobs_at(u):
                return range(JOBS1 * u // UNITS, JOBS1 * (u + 1) // UNITS)

            def turns_at(u):
                return range(1 + (NB - 1) * u // UNITS, 1 + (NB - 1) * (u + 1) // UNITS)

            def layer1_job(pe, i):
                if i >= 2:
                    pe.wait_ge(job_copied, i - 1)
                bank = job_bank(i)
                if i < len(key_jobs):
                    c0, cols = key_jobs[i]
                    ins = nc.tensor.matmul(bank[:, 0:cols], k.wk1[:], k.ctx_T[:, c0:c0 + cols], start=True, stop=True)
                else:
                    c, m = val_jobs[i - len(key_jobs)]
                    n = P if c < NCH - 1 else TAIL
                    for j in range(m):
                        ins = nc.tensor.matmul(bank[0:n, j * D:(j + 1) * D], k.ctx_T[:, (c + j) * P:(c + j) * P + n],
                                               k.wv1[:], start=True, stop=True)
                ins.then_inc(job_ready, 1)

            def copy_layer1_job(act, i):
                act.wait_ge(job_ready, i + 1)
                bank = job_bank(i)
                if i < len(key_jobs):
                    c0, cols = key_jobs[i]
                    ins = nc.scalar.copy(k.key1_T[:, c0:c0 + cols], bank[:, 0:cols])
                else:
                    c, m = val_jobs[i - len(key_jobs)]
                    n = P if c < NCH - 1 else TAIL
                    ins = nc.scalar.copy(k.val1[0:n, c:c + m, :], bank[0:n, 0:m * D].rearrange("p (j e) -> p j e", j=m))
                ins.then_inc(job_copied, 1)

            def weigh(pe, blk, v):
                if v == 0 and not (isinstance(blk, int) and blk == 0):
                    pe.wait_ge(acc_used, blk)
                pe.wait_ge(exp_done, blk * EXPS + JOBS * (v + 1))
                for q in range(4):
                    ins = nc.tensor.matmul(acc_ps[32 * q:32 * q + 32, 0:QUART], k.val_ones[:, v, :],
                                           probs[:, v % 3, q * QUART:(q + 1) * QUART], start=(v == 0), stop=(v == NCH - 1))
                ins.then_inc(pv_done, 1)

            LAST = NCH - 5
            extra = UNITS - (LAST + 1)
            after_weighing = {(LAST + 1) * (i + 1) // extra - 1 for i in range(extra)}

            def attend(pe, blk, with_max):
                pe.wait_ge(q_ready, blk + 1)
                u = 0
                for c in range(NCH):
                    for j in range(JOBS):
                        e = c * JOBS + j
                        if not (isinstance(blk, int) and blk == 0 and e < 3):
                            pe.wait_ge(exp_done, blk * EXPS + e - 2)
                        nc.tensor.matmul(score_ps[:, e % 3, :], k.key_stack[:, c * P:(c + 1) * P],
                                         columns(blk, j * HALF, HALF), start=True, stop=True).then_inc(score_ready, 1)
                        if with_max and c <= LAST and j == 0:
                            max_unit(pe, blk + 1, u)
                            u += 1
                    if c >= 1:
                        weigh(pe, blk, c - 1)
                    elif not (isinstance(blk, int) and blk == 0):
                        weigh(pe, blk - 1, NCH - 1)
                    if with_max and c in after_weighing:
                        max_unit(pe, blk + 1, u)
                        u += 1
                    if with_max and c == NCH - 2:
                        turn_shift(pe, blk + 1)

            def take_acc(act, blk):
                act.wait_ge(pv_done, (blk + 1) * NCH)
                dst = gathered[:, at(blk), :]
                nc.scalar.copy(dst if isinstance(blk, int) else dst.rearrange("p o c -> p (o c)"),
                               acc_ps[:, 0:QUART]).then_inc(acc_used, 1)

            def exponentiate(act, blk):
                for c in range(NCH):
                    n = P if c < NCH - 1 else TAIL
                    if not (isinstance(blk, int) and blk == 0 and c < 3):
                        act.wait_ge(pv_done, blk * NCH + c - 2)
                    for j in range(JOBS):
                        e = c * JOBS + j
                        act.wait_ge(score_ready, blk * EXPS + e + 1)
                        nc.scalar.activation(probs[0:n, c % 3, j * HALF:(j + 1) * HALF], score_ps[0:n, e % 3, :],
                                             ACT.Exp).then_inc(exp_done, 1)
                    if c == 0 and not (isinstance(blk, int) and blk == 0):
                        take_acc(act, blk - 1)

            def maxima(dve, blk):
                for u in range(UNITS):
                    h, r = u // NR, u % NR
                    dve.wait_ge(unit_ready, blk * UNITS + u + 1)
                    nc.vector.tensor_reduce(partial[:, h, r:r + 1], max_ps[:, u % 2, 0:RANGES[r][1]], AX.X,
                                            ALU.max).then_inc(unit_used, 1)
                dve.wait_ge(unit_used, (blk + 1) * UNITS)
                link = k.chain(dve)
                link.n = steps_before + SPLIT_STEPS + blk * LINKED
                negated_maximum(nc, link, partial[:], neg[:], [x[:] for x in rests], part3[:]).then_inc(parts_ready, 1)
                dve.wait_ge(shift_turned, blk + 1)
                dst = stack_T[SHIFT:SHIFT + 3, at(blk), :]
                nc.vector.tensor_copy(dst if isinstance(blk, int) else dst.rearrange("p o c -> p (o c)"),
                                      shift_ps[0:3, :]).then_inc(q_ready, 1)
                dve.wait_ge(q_ready, blk + 1)

            with nc.Block() as block:
                @block.tensor
                def _(pe):
                    for t in range(NT):
                        ins = nc.tensor.matmul(q_ps[:, t * D:(t + 1) * D], k.x_T[:, t * P:(t + 1) * P], w_q[:],
                                               start=True, stop=True)
                    ins.then_inc(q_made, 1)
                    pe.wait_ge(stack_ready, 1)
                    turn_block(pe, 0)
                    pe.wait_ge(first_copied, 1)
                    pe.wait_ge(stack_ready, 2)
                    for u in range(UNITS):
                        max_unit(pe, 0, u)
                        for i in jobs_at(u):
                            layer1_job(pe, i)
                        for b in turns_at(u):
                            turn_block(pe, b)
                    turn_shift(pe, 0)
                    pe.wait_ge(turn_copied, NB - 1)
                    pe.wait_ge(job_copied, JOBS1)
                    attend(pe, 0, True)
                    with nc.tensor.Fori(1, NB - 1) as i:
                        attend(pe, i, True)
                    attend(pe, NB - 1, False)
                    weigh(pe, NB - 1, NCH - 1)

                @block.scalar
                def _(act):
                    nc.scalar.preload_act_table(ACT.Exp)
                    for u in range(UNITS):
                        for i in jobs_at(u):
                            copy_layer1_job(act, i)
                        for b in turns_at(u):
                            copy_block(act, b)
                    exponentiate(act, 0)
                    with nc.scalar.Fori(1, NB) as i:
                        exponentiate(act, i)
                    take_acc(act, NB - 1)

                @block.gpsimd
                def _(pool):
                    nc.gpsimd.memset(stack[:, :, SHIFT:SHIFT + 3], 0.0)
                    nc.gpsimd.memset(stack[:, 0:ZEROED, USED:AUG], 0.0).then_inc(pad_zeroed, 1)

                @block.vector
                def _(dve):
                    link = k.chain(dve)
                    link.n = steps_before
                    nc.vector.memset(stack[:, ZEROED:, USED:AUG], 0.0)
                    dve.wait_ge(q_made, 1)
                    link(nc.vector.tensor_scalar(q_tok.rearrange("p a b -> p (a b)"), q_ps, float(HD) ** -0.5,
                                                 None, ALU.mult))
                    split(nc, link, q_tok, q_part, q_rest)
                    dve.wait_ge(pad_zeroed, 1)
                    for heads in (slice(0, HB), slice(HB, NT * H)):
                        for s, which in enumerate(Q_PARTS):
                            ins = nc.vector.tensor_copy(stack[:, heads, slot(s):slot(s) + HD],
                                                        q_part[which][:, heads, :])
                        ins.then_inc(stack_ready, 1)
                    dve.wait_ge(turned, 1)
                    nc.vector.tensor_copy(stack_T[:, 0, :], turn_bank(0)).then_inc(first_copied, 1)
                    maxima(dve, 0)
                    with nc.vector.Fori(1, NB) as i:
                        maxima(dve, i)
                    k.steps.n = steps_before + SPLIT_STEPS + NB * LINKED

        with ExitStack() as tmp:
            merged = k.sb("merged", [P, NT, D], F32, tmp)
            k.out_ps = k.ps("xattn0_out_ps", [P, NT, D], tmp)
            finish_heads(k, "xattn0", gathered, merged, w_out, k.out_ps, by_tile=True)
            residual_norm(k, "norm1", k.out_ps)
    k.layer0.close()


def finish_heads(k, tag, gathered, merged, w_out, out_ps, by_tile):
    nc = k.nc
    with ExitStack() as tmp:
        turn_ps = k.ps(tag + "_turn_ps", [P, 4, 4, P], tmp)
        recip = k.sb(tag + "_recip", [P, 4, 4, 4], F32, tmp)
        turned, used, recip_ready = k.sem(tag + "_turned"), k.sem(tag + "_turn_used"), k.sem(tag + "_recip")
        projection = Projection(k, tag, merged, w_out, out_ps, tmp)
        per_m = gathered.shape[2] // P
        M = gathered.shape[1]
        GROUPS = M * per_m // 4
        with nc.Block() as block:
            @block.tensor
            def _(pe):
                for g in range(GROUPS):
                    if g >= 4:
                        pe.wait_ge(used, g - 3)
                    for i in range(4):
                        w = g * 4 + i
                        m, s = w // per_m, w % per_m
                        ins = nc.tensor.transpose(turn_ps[:, g % 4, i, :], gathered[:, m, s * P:(s + 1) * P], k.ident[:])
                    ins.then_inc(turned, 1)
                    if by_tile and g >= 2:
                        pe.wait_ge(used, g - 1)
                        projection.turn(pe, g - 2)
                pe.wait_ge(used, GROUPS)
                for t in range(NT - 2 if by_tile else 0, NT):
                    projection.turn(pe, t)
                projection.multiply(pe)

            @block.scalar
            def _(act):
                projection.copy(act)

            @block.vector
            def _(dve):
                for g in range(GROUPS):
                    dve.wait_ge(turned, g + 1)
                    rows = turn_ps[:, g % 4, :, :].rearrange("p i (q r) -> p i q r", q=4)
                    nc.vector.reciprocal(recip[:, g % 4, :, :], rows[:, :, :, HD]).then_inc(recip_ready, 1)
                    dve.wait_ge(recip_ready, g + 1)
                    for i in range(4):
                        src = turn_ps[:, g % 4, i, :].rearrange("p (q r) -> p q r", q=4)[:, :, 0:HD]
                        w = g * 4 + i
                        m, s = w // per_m, w % per_m
                        if by_tile:
                            dst = merged[:, m // 2, :].rearrange("p (a q s e) -> p a s q e", a=2, q=4, s=2)[:, m % 2, s, :, :]
                        else:
                            dst = merged[:].rearrange("p (q s) (h e) -> p s h q e", s=2, h=H)[:, s, m, :, :]
                        ins = nc.vector.tensor_tensor(dst, src, recip[:, g % 4, i, :].unsqueeze(2).to_broadcast([P, 4, HD]),
                                                      ALU.mult)
                    ins.then_inc(used, 1)


class Projection:

    def __init__(self, k, tag, merged, w_out, out_ps, ctx):
        self.k, self.merged, self.w_out, self.out_ps = k, merged, w_out, out_ps
        self.back_ps = k.ps(tag + "_back_ps", [P, T], ctx)
        self.merged_T = k.sb(tag + "_merged_T", [P, T], F32, ctx)
        self.back, self.back_copied = k.sem(tag + "_back"), k.sem(tag + "_back_copied")

    def turn(self, pe, t):
        ins = self.k.nc.tensor.transpose(self.back_ps[:, t * P:(t + 1) * P], self.merged[:, t, :], self.k.ident[:])
        if t % 4 == 3:
            ins.then_inc(self.back, 1)

    def copy(self, act):
        for h in range(2):
            act.wait_ge(self.back, h + 1)
            self.k.nc.scalar.copy(self.merged_T[:, h * HALF:(h + 1) * HALF],
                                  self.back_ps[:, h * HALF:(h + 1) * HALF]).then_inc(self.back_copied, 1)

    def multiply(self, pe):
        for t in range(NT):
            if t % 4 == 0:
                pe.wait_ge(self.back_copied, t // 4 + 1)
            self.k.nc.tensor.matmul(self.out_ps[:, t, :], self.merged_T[:, t * P:(t + 1) * P], self.w_out[:],
                                    start=True, stop=True)


def choose(nc, link, values, width, pads, n_top, lowest, top8, wanted, left, chosen):
    mark = 2.0 * lowest
    for t in range(NT):
        ins = nc.vector.max(top8[:, t, :], values[:, t, :])
    link(ins)
    link(nc.vector.tensor_copy(wanted[:, :, 0:n_top], top8[:, :, 0:n_top]))
    for t in range(NT):
        ins = nc.vector.match_replace(left[:, t, :], wanted[:, t, :], values[:, t, :], mark)
    link(ins)
    link(nc.vector.tensor_scalar(chosen, left[:, :, 0:width], mark, None, ALU.is_equal))


def experts0(k):
    nc, d = k.nc, k.dram
    E, F, TOP = 15, 2 * P, 3
    STEPS = E + 2
    PADS = 8 - TOP
    LOWEST = -1.0
    ctx = ExitStack()
    with ctx:
        w1 = k.sb("e0_w1", [P, 2, F], F32, ctx)
        w2 = k.sb("e0_w2", [P, 2, 2, D], F32, ctx)
        gw, gb, b1, b2 = k.params.e0_gw, k.params.e0_gb, k.params.e0_b1, k.params.e0_b2
        acc = k.sb("e0_acc", [P, NT, D], F32, ctx)
        gates = k.sb("e0_gates", [P, NT, STEPS], F32, ctx)
        hidden = k.sb("e0_hidden", [P, 2, 2, T], F32, ctx)
        w1_loaded = [k.sem(f"e0_w1_slot{i}_loaded") for i in range(2)]
        w2_loaded = [k.sem(f"e0_w2_slot{i}_loaded") for i in range(2)]
        out_done, added = k.sem("e0_out_done"), [k.sem("e0_added_even"), k.sem("e0_added_odd")]

        def load_w1(sp, s, src):
            sp.dma_start(w1[:, s, :], src).then_inc(w1_loaded[s], 16)

        def load_w2(sp, s, src):
            sp.dma_start(w2[:, s, :, :], src.rearrange("(f p) m -> p f m", p=P)).then_inc(w2_loaded[s], 16)

        logits = k.sb("e0_logits", [P, NT, E], F32, ctx)
        top = k.sb("e0_top", [P, NT], F32, ctx)
        weights = k.sb("e0_weights", [P, NT, E + PADS], F32, ctx)
        total = k.sb("e0_total", [P, NT], F32, ctx)
        top8 = k.sb("e0_top8", [P, NT, 8], F32, ctx)
        wanted = k.sb("e0_wanted", [P, NT, 8], F32, ctx)
        left = k.sb("e0_left", [P, NT, E + PADS], F32, ctx)
        chosen = k.sb("e0_chosen", [P, NT, E], F32, ctx)
        gates_T = k.sb("e0_gates_T", [E + 1, T], F32, ctx)
        logits_ready, shifted, exp_ready = k.sem("e0_logits_ready"), k.sem("e0_shifted"), k.sem("e0_exp_ready")
        gates_ready, turned, turn_copied, b2_ready = (k.sem("e0_gates_ready"), k.sem("e0_turned"),
                                                      k.sem("e0_turn_copied"), k.sem("e0_b2_ready"))

        with ExitStack() as tmp:
            hid_ps = k.ps("e0_hid_ps", [P, 2, T], tmp)
            out_ps = k.ps("e0_out_ps", [P, 2, NT, D], tmp)
            logit_ps = out_ps[:, 0, :, 0:16]
            b2_ps = out_ps[:, 0, :, :]
            turn_ps = out_ps[0:E + 1, 1, :, :].rearrange("e t d -> e (t d)")
            acc_ready = k.sem("e0_acc_ready")
            hid_ready, gelu_done = k.sem("e0_hid_ready"), k.sem("e0_gelu_done")

            def hid(pe, step, s, uses):
                pe.wait_ge(w1_loaded[s], 16 * (uses + 1))
                for f in range(2):
                    if not (isinstance(step, int) and step == 0):
                        pe.wait_ge(gelu_done, 2 * step - 1 + f)
                    for h in range(2):
                        ins = nc.tensor.matmul(hid_ps[:, f, h * HALF:(h + 1) * HALF], w1[:, s, f * P:(f + 1) * P],
                                               k.x_T[:, h * HALF:(h + 1) * HALF], start=True, stop=True)
                    ins.then_inc(hid_ready, 1)

            def out(pe, step, s, uses):
                pe.wait_ge(gelu_done, 2 * step + 2)
                pe.wait_ge(w2_loaded[s], 16 * (uses + 1))
                if not (isinstance(uses, int) and uses == 0):
                    pe.wait_ge(added[s], uses)
                for t in range(NT):
                    for f in range(2):
                        ins = nc.tensor.matmul(out_ps[:, s, t, :], hidden[:, s, f, t * P:(t + 1) * P], w2[:, s, f, :],
                                               start=(f == 0), stop=(f == 1))
                ins.then_inc(out_done, 1)

            def gelu(act, step, s):
                if not (isinstance(step, int) and step < 2):
                    act.wait_ge(out_done, step - 1)
                for f in range(2):
                    act.wait_ge(hid_ready, 2 * step + f + 1)
                    nc.scalar.activation(hidden[:, s, f, :], hid_ps[:, f, :], ACT.Gelu,
                                         bias=b1[:, bass.ds(2 * step + f, 1)]).then_inc(gelu_done, 1)

            def add_up(dve, step, s, uses):
                dve.wait_ge(out_done, step + 1)
                if s == 1:
                    dve.wait_ge(added[0], uses + 1)
                elif not (isinstance(uses, int) and uses == 0):
                    dve.wait_ge(added[1], uses)
                for t in range(NT):
                    ins = nc.vector.scalar_tensor_tensor(out=acc[:, t, :], in0=out_ps[:, s, t, :],
                                                         scalar=gates[:, t, bass.ds(step, 1)], in1=acc[:, t, :],
                                                         op0=ALU.mult, op1=ALU.add)
                ins.then_inc(added[s], 1)

            def next_w1(sp, e, s):
                sp.wait_ge(hid_ready, 2 * e + 2)
                load_w1(sp, s, one(d["L0_ffn_rW1"], e))

            def next_w2(sp, e, s):
                sp.wait_ge(out_done, e + 1)
                load_w2(sp, s, one(d["L0_ffn_rW2"], e))

            def load_early(sp):
                for s in range(2):
                    load_w1(sp, s, d["L0_ffn_sW1"][0][:, s * F:(s + 1) * F])
                    load_w2(sp, s, d["L0_ffn_sW2"][0][s * F:(s + 1) * F, :])

            def score(pe):
                for t in range(NT):
                    ins = nc.tensor.matmul(logit_ps[:, t, 0:E], k.x_T[:, t * P:(t + 1) * P], gw[:], start=True, stop=True)
                ins.then_inc(logits_ready, 1)

            def turn_gates(pe):
                pe.wait_ge(gates_ready, 1)
                for t in range(NT):
                    ins = nc.tensor.transpose(turn_ps[:, t * P:(t + 1) * P], gates[:, t, 1:STEPS], k.ident[:])
                ins.then_inc(turned, 1)
                pe.wait_ge(turn_copied, 1)
                for t in range(NT):
                    ins = nc.tensor.matmul(b2_ps[:, t, :], gates_T[:, t * P:(t + 1) * P], b2[:], start=True, stop=True)
                ins.then_inc(b2_ready, 1)

            def raise_logits(act):
                act.wait_ge(shifted, 1)
                nc.scalar.activation(weights[:, :, 0:E], logits[:], ACT.Exp).then_inc(exp_ready, 1)
                nc.scalar.preload_act_table(ACT.Gelu)

            def copy_gates(act):
                act.wait_ge(turned, 1)
                nc.scalar.copy(gates_T[:], turn_ps).then_inc(turn_copied, 1)

            def choose_gates(dve):
                link = k.chain(dve)

                def spread(x, n):
                    return x[:].unsqueeze(2).to_broadcast([P, NT, n])
                nc.vector.memset(weights[:, :, E:E + PADS], LOWEST)
                nc.vector.memset(wanted[:], LOWEST)
                nc.vector.memset(gates[:, :, 0:2], 1.0)
                dve.wait_ge(logits_ready, 1)
                link(nc.vector.tensor_tensor(logits[:], logit_ps[:, :, 0:E], gb[:].unsqueeze(1).to_broadcast([P, NT, E]),
                                             ALU.add))
                link(nc.vector.tensor_reduce(top[:], logits[:], AX.X, ALU.max))
                nc.vector.tensor_tensor(logits[:], logits[:], spread(top, E), ALU.subtract).then_inc(shifted, 1)
                dve.wait_ge(exp_ready, 1)
                link(nc.vector.tensor_reduce(total[:], weights[:, :, 0:E], AX.X, ALU.add))
                link(nc.vector.reciprocal(total[:], total[:]))
                link(nc.vector.tensor_tensor(weights[:, :, 0:E], weights[:, :, 0:E], spread(total, E), ALU.mult))
                choose(nc, link, weights, E, PADS, TOP, LOWEST, top8, wanted, left, chosen[:])
                nc.vector.tensor_tensor(gates[:, :, 2:STEPS], weights[:, :, 0:E], chosen[:], ALU.mult).then_inc(gates_ready, 1)
                dve.wait_ge(b2_ready, 1)
                nc.vector.scalar_tensor_tensor(out=acc[:], in0=k.x_tok[:], scalar=2.0, in1=b2_ps, op0=ALU.mult, op1=ALU.add).then_inc(acc_ready, 1)

            PAIRS = (STEPS - 1) // 2
            with nc.Block() as block:
                @block.sync
                def _(sp):
                    load_early(sp)
                    next_w1(sp, 0, 0)
                    with nc.sync.Fori(0, PAIRS - 1) as p:
                        next_w1(sp, 2 * p + 1, 1)
                        next_w2(sp, 2 * p, 0)
                        next_w1(sp, 2 * p + 2, 0)
                        next_w2(sp, 2 * p + 1, 1)
                    next_w2(sp, E - 1, 0)

                @block.tensor
                def _(pe):
                    score(pe)
                    hid(pe, 0, 0, 0)
                    hid(pe, 1, 1, 0)
                    turn_gates(pe)
                    pe.wait_ge(acc_ready, 1)
                    out(pe, 0, 0, 0)
                    hid(pe, 2, 0, 1)
                    out(pe, 1, 1, 0)
                    with nc.tensor.Fori(1, PAIRS) as p:
                        hid(pe, 2 * p + 1, 1, p)
                        out(pe, 2 * p, 0, p)
                        hid(pe, 2 * p + 2, 0, p + 1)
                        out(pe, 2 * p + 1, 1, p)
                    out(pe, STEPS - 1, 0, PAIRS)

                @block.scalar
                def _(act):
                    raise_logits(act)
                    gelu(act, 0, 0)
                    copy_gates(act)
                    gelu(act, 1, 1)
                    with nc.scalar.Fori(1, PAIRS) as p:
                        for s in range(2):
                            gelu(act, 2 * p + s, s)
                    gelu(act, STEPS - 1, 0)

                @block.vector
                def _(dve):
                    choose_gates(dve)
                    dve.wait_ge(acc_ready, 1)
                    add_up(dve, 0, 0, 0)
                    add_up(dve, 1, 1, 0)
                    with nc.vector.Fori(1, PAIRS) as p:
                        for s in range(2):
                            add_up(dve, 2 * p + s, s, p)
                    add_up(dve, STEPS - 1, 0, PAIRS)
        residual_norm(k, "norm2", acc, added=True)


def one(ap, e):
    return ap[bass.ds(e, 1)].rearrange("o a b -> (o a) b")


def turn_stack(k, tag, stack, stack_T, turn_ps, stack_ready, used_dve, used_act, turned, base=0):
    nc = k.nc
    G = NT * H // 8

    def on_pe(pe):
        pe.wait_ge(stack_ready, base + 1)
        for g in range(G):
            if g >= 4 or base:
                pe.wait_ge(used_act if g % 2 else used_dve, base * G // 2 + (g - 4) // 2 + 1)
            for j in range(8):
                ins = nc.tensor.transpose(turn_ps[:, g % 4, j * P:(j + 1) * P], stack[:, g * 8 + j, :], k.ident_b[:])
            ins.then_inc(turned, 1)

    def on_dve(dve, g):
        dve.wait_ge(turned, base * G + g + 1)
        nc.vector.tensor_copy(stack_T[:, g // 2, 0:8 * P], turn_ps[:, g % 4, :]).then_inc(used_dve, 1)

    def on_act(act):
        for g in range(1, G, 2):
            act.wait_ge(turned, base * G + g + 1)
            nc.scalar.copy(stack_T[:, g // 2, 8 * P:16 * P], turn_ps[:, g % 4, :]).then_inc(used_act, 1)

    return on_pe, on_dve, on_act


def hi_of(nc, link, hi, whole):
    link(nc.vector.tensor_copy(hi, whole))
    return hi


def self_attention(k):
    nc = k.nc
    LORA = 32.0 / Params.RANK
    ctx = ExitStack()
    with ctx:
        q_T = k.sb("s_q_stack_T", [P, NT, H * P], BF16, ctx)
        k_T = k.sb("s_k_stack_T", [P, NT, H * P], BF16, ctx)
        val = k.sb("s_val_ones", [P, NT, H, 32], F32, ctx)
        w_proj, b_proj = k.params.s_w_proj, k.params.s_b_proj
        with ExitStack() as tmp:
            w, b_feat, b_k = k.params.s_w, k.params.s_b_feat, k.params.s_b_k
            lora_a, lora_b = k.params.s_lora_a, k.params.s_lora_b
            mask = k.sb("s_mask", [P, H, HD], F32, tmp)
            mix = k.sb("s_mix", [P, 2, D], F32, tmp)
            before = q_T[:, 0:2, :].rearrange("p t n -> p (t n)").bitcast(F32).rearrange("p (i t) -> p i t", i=2)
            tok = k.sb("s_tok", [P, NT * H, HD], F32, tmp)
            part = [k.sb(f"s_part{i}", [P, NT * H, HD], BF16, tmp) for i in range(3)]
            rest = [k.sb(f"s_rest{i}", [P, NT * H, HD], F32, tmp) for i in range(2)]
            stack = k.sb("s_stack", [P, NT * H, AUG], BF16, tmp)
            proj_ps = k.ps("s_proj_ps", [P, 2, T], tmp)
            turn_ps = k.ps("s_turn_ps", [P, 4, 8 * P], tmp, BF16)
            raw_ps = turn_ps[:].rearrange("p b n -> p (b n)").bitcast(F32).rearrange("p (i t) -> p i t", i=2)
            mix_ps = proj_ps[:, 1, 0:2 * D].rearrange("p (i e) -> p i e", i=2)
            pool_done = k.sem("s_constants_set")
            MASK_SET, STACK_SET, VAL_SET = 3, 4, 6
            mix_raw, mix_ready, raw_ready, biased = (k.sem("s_mix_raw"), k.sem("s_mix_ready"), k.sem("s_raw_ready"),
                                                     k.sem("s_biased"))
            key_ready, key_taken, tok_ready = k.sem("s_key_ready"), k.sem("s_key_taken"), k.sem("s_tok_ready")
            stack_ready = k.sem("s_stack_ready")
            turned, used_dve, used_act = k.sem("s_turned"), k.sem("s_turn_used_dve"), k.sem("s_turn_used_act")
            turns = [turn_stack(k, "s", stack, x, turn_ps, stack_ready, used_dve, used_act, turned, base=i)
                     for i, x in enumerate((k_T, q_T))]
            G = NT * H // 8
            with nc.Block() as block:
                @block.gpsimd
                def _(pool):
                    nc.gpsimd.memset(mask[:], LORA).then_inc(pool_done, 1)
                    pool.wait_ge(pool_done, 1)
                    nc.gpsimd.affine_select(out=mask[:], in_=mask[:], compare_op=ALU.is_ge, fill=0.0, base=0,
                                            pattern=[[-HD, H], [0, HD]], channel_multiplier=1).then_inc(pool_done, 1)
                    pool.wait_ge(pool_done, 2)
                    nc.gpsimd.affine_select(out=mask[:], in_=mask[:], compare_op=ALU.is_ge, fill=0.0, base=HD - 1,
                                            pattern=[[HD, H], [0, HD]], channel_multiplier=-1).then_inc(pool_done, 1)
                    nc.gpsimd.memset(stack[:, :, SHIFT:SHIFT + 3], 1.0)
                    nc.gpsimd.memset(stack[:, :, USED:AUG], 0.0).then_inc(pool_done, 1)
                    nc.gpsimd.memset(val[:], 0.0).then_inc(pool_done, 1)
                    pool.wait_ge(pool_done, 5)
                    nc.gpsimd.memset(val[:, :, :, HD:HD + 1], 1.0).then_inc(pool_done, 1)
                    nc.gpsimd.tensor_tensor(k.x_tok[:], k.x_tok[:], b_proj[:].unsqueeze(1).to_broadcast([P, NT, D]), ALU.add)

                @block.tensor
                def _(pe):
                    for t in range(NT):
                        ins = nc.tensor.matmul(proj_ps[:, 0, t * P:(t + 1) * P], k.x_T[:, t * P:(t + 1) * P],
                                               w[:, D:2 * D], start=True, stop=True)
                    ins.then_inc(key_ready, 1)
                    for i in range(2):
                        ins = nc.tensor.matmul(mix_ps[:, i, :], lora_a[:, i].rearrange("r h e -> r (h e)"),
                                               lora_b[:, i].rearrange("r h e -> r (h e)"), start=True, stop=True)
                    ins.then_inc(mix_raw, 1)
                    for i, col in enumerate((0, 2 * D)):
                        for h in range(2):
                            ins = nc.tensor.matmul(raw_ps[:, i, h * HALF:(h + 1) * HALF], w[:, col:col + D],
                                                   k.x_T[:, h * HALF:(h + 1) * HALF], start=True, stop=True)
                        ins.then_inc(raw_ready, 1)
                    pe.wait_ge(mix_ready, 1)
                    pe.wait_ge(key_taken, 1)
                    for i in range(2):
                        pe.wait_ge(biased, i + 1)
                        for t in range(NT):
                            ins = nc.tensor.matmul(proj_ps[:, i, t * P:(t + 1) * P], before[:, i, t * P:(t + 1) * P],
                                                   mix[:, i, :], start=True, stop=True)
                        ins.then_inc(tok_ready, 1)
                    for on_pe, _, _ in turns:
                        on_pe(pe)

                @block.scalar
                def _(act):
                    for i, col in enumerate((0, 2)):
                        act.wait_ge(raw_ready, i + 1)
                        nc.scalar.activation(before[:, i, :], raw_ps[:, i, :], ACT.Identity,
                                             bias=b_feat[:, col:col + 1]).then_inc(biased, 1)
                    for _, _, on_act in turns:
                        on_act(act)
                    nc.scalar.preload_act_table(ACT.Exp)

                @block.vector
                def _(dve):
                    link = k.chain(dve)
                    turn_k, turn_q = turns[0][1], turns[1][1]
                    dve.wait_ge(key_ready, 1)
                    nc.vector.tensor_tensor(tok[:].rearrange("p (t h) e -> p t (h e)", t=NT),
                                            proj_ps[:, 0, :].rearrange("p (t f) -> p t f", t=NT),
                                            b_k[:].unsqueeze(1).to_broadcast([P, NT, D]), ALU.add).then_inc(key_taken, 1)
                    dve.wait_ge(mix_raw, 1)
                    dve.wait_ge(pool_done, MASK_SET)
                    for i in range(2):
                        link(nc.vector.tensor_tensor(mix[:, i, :], mix_ps[:, i, :], mask[:].rearrange("p h e -> p (h e)"),
                                                     ALU.mult))
                    link(nc.vector.tensor_tensor(mix[:, 0, :], mix[:, 0, :], k.ident[:], ALU.add))
                    nc.vector.tensor_tensor(mix[:, 1, :], mix[:, 1, :], k.ident[:], ALU.add).then_inc(mix_ready, 1)
                    dve.wait_ge(key_taken, 1)
                    dve.wait_ge(pool_done, STACK_SET)
                    stack_queries(nc, link, tok[:], [x[:] for x in part], [x[:] for x in rest], stack,
                                  K_PARTS).then_inc(stack_ready, 1)
                    dve.wait_ge(tok_ready, 1)
                    link(nc.vector.tensor_scalar(tok[:].rearrange("p a b -> p (a b)"), proj_ps[:, 0, :],
                                                 float(HD) ** -0.5, None, ALU.mult))
                    turn_k(dve, 0)
                    link(nc.vector.tensor_tensor(rest[0][:], tok[:], hi_of(nc, link, part[0][:], tok[:]), ALU.subtract))
                    turn_k(dve, 2)
                    turn_k(dve, 4)
                    link(nc.vector.tensor_tensor(rest[1][:], rest[0][:], hi_of(nc, link, part[1][:], rest[0][:]), ALU.subtract))
                    turn_k(dve, 6)
                    turn_k(dve, 8)
                    hi_of(nc, link, part[2][:], rest[1][:])
                    turn_k(dve, 10)
                    dve.wait_ge(tok_ready, 2)
                    dve.wait_ge(pool_done, VAL_SET)
                    nc.vector.tensor_copy(val[:, :, :, 0:HD], proj_ps[:, 1, :].rearrange("p (t h e) -> p t h e", t=NT, h=H))
                    turn_k(dve, 12)
                    turn_k(dve, 14)
                    dve.wait_ge(turned, G)
                    nc.vector.memset(stack[:, :, SHIFT:SHIFT + 3], 0.0)
                    for s, which in enumerate(Q_PARTS):
                        ins = nc.vector.tensor_copy(stack[:, :, slot(s):slot(s) + HD], part[which][:])
                    ins.then_inc(stack_ready, 1)
                    for g in range(0, G, 2):
                        turn_q(dve, g)

        gathered = k.sb("s_gathered", [P, H, 2 * P], F32, ctx)
        with ExitStack() as tmp:
            v_buf = k.sb("s_v_buf", [P, 2, NT, 32], F32, tmp)
            probs = k.sb("s_probs", [P, 2, T], F32, tmp)
            partial = k.sb("s_max_partial", [P, NT, 2], F32, tmp)
            neg = k.sb("s_neg_max", [P, NT], F32, tmp)
            rests = [k.sb(f"s_neg_rest{i}", [P, NT], F32, tmp) for i in range(2)]
            part3 = k.sb("s_neg_part", [P, NT, 3], BF16, tmp)
            one = k.ones_b[:, 0:NT]
            score_ps = k.ps("s_score_ps", [P, 2, T], tmp)
            max_ps = k.ps("s_max_ps", [P, 2, HALF], tmp)
            acc_ps = k.ps("s_acc_ps", [P, HALF], tmp)
            shift_ps = k.ps("s_shift_ps", [P, T], tmp, BF16)
            neg_ready, part_step = k.sem("s_neg_ready"), k.sem("s_part_step")
            LINKED = 4
            q_ready, val_ready = k.sem("s_q_ready"), k.sem("s_val_ready")
            unit_ready, unit_used, parts_ready, shift_turned = (k.sem("s_max_ready"), k.sem("s_max_used"),
                                                                k.sem("s_neg_parts_ready"), k.sem("s_shift_turned"))
            score_ready, exp_done, pv_done, acc_used = (k.sem("s_score_ready"), k.sem("s_exp_done"), k.sem("s_pv_done"),
                                                        k.sem("s_acc_used"))
            UNITS = 2 * NT
            QUART = T // 4
            AHEAD = 6

            def at(h):
                return h if isinstance(h, int) else bass.ds(h, 1)

            def block_of(ap, h, t):
                return ap[:, t, h * P:(h + 1) * P] if isinstance(h, int) else ap[:, t, bass.ds(h * P, P)]

            def half_of(ap, h, half):
                x = ap[:].rearrange("p t (h c) -> p t h c", h=H)[:, 4 * half:4 * half + 4, at(h), :]
                return x if isinstance(h, int) else x.rearrange("p t o c -> p t (o c)")

            def max_unit(pe, h, u):
                if not (isinstance(h, int) and h == 0 and u < 2):
                    pe.wait_ge(unit_used, h * UNITS + u - 1)
                nc.tensor.matmul(max_ps[:, u % 2, :].rearrange("p (t c) -> p t c", t=4), block_of(q_T, h, u // 2),
                                 half_of(k_T, h, u % 2), start=True, stop=True).then_inc(unit_ready, 1)

            def turn_shift(pe, h):
                pe.wait_ge(parts_ready, h + 1)
                for t in range(NT):
                    ins = nc.tensor.transpose(shift_ps[0:3, t * P:(t + 1) * P], part3[:, t, :], k.ident_b[:])
                ins.then_inc(shift_turned, 1)

            def weigh(pe, h, s, v):
                if v == 0:
                    pe.wait_ge(val_ready, h + 1)
                    if not (isinstance(h, int) and h == 0):
                        pe.wait_ge(acc_used, h)
                pe.wait_ge(exp_done, h * NT + v + 1)
                for j in range(4):
                    ins = nc.tensor.matmul(acc_ps[32 * j:32 * j + 32, 0:QUART], v_buf[:, s, v, :],
                                           probs[:, v % 2, j * QUART:(j + 1) * QUART],
                                           start=(v == 0), stop=(v == NT - 1))
                ins.then_inc(pv_done, 1)

            def attend(pe, h, s):
                pe.wait_ge(q_ready, h + 1)
                for c in range(NT):
                    if c == NT - 2 and not (isinstance(h, int) and h == H - 1):
                        turn_shift(pe, h + 1)
                    if not (isinstance(h, int) and h == 0 and c < 2):
                        pe.wait_ge(exp_done, h * NT + c - 1)
                    ahead = [divmod(2 * c + AHEAD + i, UNITS) for i in range(2)]
                    ahead = [(h + 1 + later, u) for later, u in ahead if not (isinstance(h, int) and h + 1 + later >= H)]
                    if ahead:
                        max_unit(pe, *ahead[0])
                    for half in range(2):
                        ins = nc.tensor.matmul(score_ps[:, c % 2, half * HALF:(half + 1) * HALF].rearrange(
                            "p (t c) -> p t c", t=4), block_of(k_T, h, c), half_of(q_T, h, half), start=True, stop=True)
                    ins.then_inc(score_ready, 1)
                    for unit in ahead[1:]:
                        max_unit(pe, *unit)
                    if c >= 1:
                        weigh(pe, h, s, c - 1)
                    elif not (isinstance(h, int) and h == 0):
                        weigh(pe, h - 1, 1 - s, NT - 1)

            def take_acc(act, h):
                act.wait_ge(pv_done, (h + 1) * NT)
                nc.scalar.copy(gathered[:, at(h), :] if isinstance(h, int) else gathered[:, at(h), :].rearrange(
                    "p o c -> p (o c)"), acc_ps[:, 0:QUART]).then_inc(acc_used, 1)

            def take_shift(act, h):
                act.wait_ge(shift_turned, h + 1)
                dst = q_T[:].rearrange("p t (h c) -> p t h c", h=H)[SHIFT:SHIFT + 3, :, at(h), :]
                if not isinstance(h, int):
                    dst = dst.rearrange("p t o c -> p t (o c)")
                nc.scalar.copy(dst, shift_ps[0:3, :].rearrange("p (t c) -> p t c", t=NT)).then_inc(q_ready, 1)

            def exponentiate(act, h):
                for c in range(NT):
                    act.wait_ge(score_ready, h * NT + c + 1)
                    if not (isinstance(h, int) and h == 0 and c < 2):
                        act.wait_ge(pv_done, h * NT + c - 1)
                    nc.scalar.activation(probs[:, c % 2, :], score_ps[:, c % 2, :], ACT.Exp).then_inc(exp_done, 1)
                    if c == 0 and not (isinstance(h, int) and h == 0):
                        take_acc(act, h - 1)
                    if c == NT - 3 and not (isinstance(h, int) and h == H - 1):
                        take_shift(act, h + 1)

            def maxima(dve, h):
                for u in range(UNITS):
                    dve.wait_ge(unit_ready, h * UNITS + u + 1)
                    nc.vector.tensor_reduce(partial[:, u // 2, u % 2:u % 2 + 1], max_ps[:, u % 2, :], AX.X,
                                            ALU.max).then_inc(unit_used, 1)
                dve.wait_ge(unit_used, (h + 1) * UNITS)
                if due(h):
                    dve.wait_ge(parts_ready, h)
                nc.vector.tensor_reduce(neg[:], partial[:], AX.X, ALU.max, negate=True).then_inc(neg_ready, 1)
                dve.wait_ge(neg_ready, h + 1)

            def parts(pool, h):
                pool.wait_ge(neg_ready, h + 1)
                if due(h):
                    pool.wait_ge(shift_turned, h)
                link = Chain(pool, part_step)
                link.n = h * LINKED
                link(nc.gpsimd.tensor_tensor(part3[:, :, 0], neg[:], one, ALU.mult))
                link(nc.gpsimd.tensor_tensor(rests[0][:], neg[:], part3[:, :, 0], ALU.subtract))
                link(nc.gpsimd.tensor_tensor(part3[:, :, 1], rests[0][:], one, ALU.mult))
                link(nc.gpsimd.tensor_tensor(rests[1][:], rests[0][:], part3[:, :, 1], ALU.subtract))
                nc.gpsimd.tensor_tensor(part3[:, :, 2], rests[1][:], one, ALU.mult).then_inc(parts_ready, 1)

            def values(pool, h, s):
                out = v_buf[:, s, :, :] if isinstance(h, int) else v_buf[:, s, :, :].unsqueeze(2)
                nc.gpsimd.tensor_copy(out, val[:, :, at(h), :]).then_inc(val_ready, 1)

            with nc.Block() as block:
                @block.tensor
                def _(pe):
                    for u in range(UNITS):
                        max_unit(pe, 0, u)
                    for u in range(AHEAD):
                        max_unit(pe, 1, u)
                    turn_shift(pe, 0)
                    attend(pe, 0, 0)
                    attend(pe, 1, 1)
                    with nc.tensor.Fori(1, H // 2 - 1) as p:
                        for s in range(2):
                            attend(pe, 2 * p + s, s)
                    attend(pe, H - 2, 0)
                    attend(pe, H - 1, 1)
                    weigh(pe, H - 1, 1, NT - 1)

                @block.scalar
                def _(act):
                    take_shift(act, 0)
                    exponentiate(act, 0)
                    with nc.scalar.Fori(1, H - 1) as h:
                        exponentiate(act, h)
                    exponentiate(act, H - 1)
                    take_acc(act, H - 1)

                @block.gpsimd
                def _(pool):
                    for h in range(2):
                        values(pool, h, h)
                        parts(pool, h)
                    with nc.gpsimd.Fori(1, H // 2) as p:
                        for s in range(2):
                            parts(pool, 2 * p + s)
                            pool.wait_ge(pv_done, (2 * p + s - 1) * NT)
                            values(pool, 2 * p + s, s)

                @block.vector
                def _(dve):
                    maxima(dve, 0)
                    with nc.vector.Fori(1, H) as h:
                        maxima(dve, h)

        with ExitStack() as tmp:
            merged = k.sb("s_merged", [P, NT, D], F32, tmp)
            out_ps = k.ps("s_out_ps", [P, NT, D], tmp)
            finish_heads(k, "self", gathered, merged, w_proj, out_ps, by_tile=False)
            residual_norm(k, "norm3", out_ps)


def context_attention1(k):
    nc = k.nc
    WIDE = 2 * HALF
    RANGES = [(c0, min(WIDE, CTX - c0)) for c0 in range(0, CTX, WIDE)]
    NR = len(RANGES)
    GROUPS = [(c, min(4, NCH - c)) for c in range(0, NCH, 4)]
    NG = len(GROUPS)
    SCALE = float(D) ** -0.5
    ctx = ExitStack()
    with ctx:
        q_T = k.sb("x1_q_T", [P, T], F32, ctx)
        merged = k.sb("x1_merged", [P, NT, D], F32, ctx)
        w_q, b_q, w_out = k.params.x1_w_q, k.params.x1_b_q, k.params.x1_w_out
        b_out, b_v = k.params.x1_b_out, k.params.x1_b_v
        with ExitStack() as tmp:
            b_scaled = k.sb("x1_b_scaled", [P, 1], F32, tmp)
            q_ps = k.ps("x1_q_ps", [P, T], tmp)
            q_ready, scaled = k.sem("x1_q_ready"), k.sem("x1_scaled")
            with nc.Block() as block:
                @block.tensor
                def _(pe):
                    for h in range(2):
                        nc.tensor.matmul(q_ps[:, h * HALF:(h + 1) * HALF], w_q[:], k.x_T[:, h * HALF:(h + 1) * HALF],
                                         start=True, stop=True).then_inc(q_ready, 1)

                @block.gpsimd
                def _(pool):
                    nc.gpsimd.tensor_tensor(k.x_tok[:], k.x_tok[:], b_out[:].unsqueeze(1).to_broadcast([P, NT, D]), ALU.add)

                @block.vector
                def _(dve):
                    nc.vector.tensor_scalar(b_scaled[:], b_q[:], SCALE, None, ALU.mult).then_inc(scaled, 1)

                @block.scalar
                def _(act):
                    act.wait_ge(scaled, 1)
                    for h in range(2):
                        act.wait_ge(q_ready, h + 1)
                        nc.scalar.activation(q_T[:, h * HALF:(h + 1) * HALF], q_ps[:, h * HALF:(h + 1) * HALF],
                                             ACT.Identity, bias=b_scaled[:], scale=SCALE)
                    nc.scalar.preload_act_table(ACT.Exp)

        with ExitStack() as tmp:
            q_buf = k.sb("x1_q_buf", [P, 2, P], F32, tmp)
            scores = k.sb("x1_scores", [P, 2, CTX], F32, tmp)
            turned = k.sb("x1_turned", [P, 2, HALF], F32, tmp)
            top = k.sb("x1_top", [P, 2, NR], F32, tmp)
            neg = k.sb("x1_neg", [P, 2], F32, tmp)
            sums = k.sb("x1_sums", [P, 2, NR], F32, tmp)
            total = k.sb("x1_total", [P, 2], F32, tmp)
            recip = k.sb("x1_recip", [P, 2], F32, tmp)
            score_ps = k.ps("x1_score_ps", [P, 2, WIDE], tmp)
            turn_ps = k.ps("x1_turn_ps", [P, 2, HALF], tmp)
            acc_ps = k.ps("x1_acc_ps", [P, 2, HALF], tmp)
            q_ready, range_ready, taken = k.sem("x1_q_buf_ready"), k.sem("x1_range_ready"), k.sem("x1_taken")
            neg_ready, exp_done, group_turned = k.sem("x1_neg_ready"), k.sem("x1_exp_done"), k.sem("x1_group_turned")
            copied = [k.sem("x1_copied_even"), k.sem("x1_copied_odd")]
            pv_done, summed, recip_ready, merged_ready = (k.sem("x1_pv_done"), k.sem("x1_summed"), k.sem("x1_recip_ready"),
                                                          k.sem("x1_merged_ready"))

            def tile_of(p, s):
                return 2 * p + s

            SPREAD = NG - 2
            out_after = [min(NG, -(-NG * (g + 1) // SPREAD)) for g in range(NG)]
            steps_at = [range(out_after[g - 1] if g else 0, out_after[g]) for g in range(NG)]
            ranges_at = [[i // 2 for i in steps_at[g] if i % 2 == 1 or i == NG - 1] for g in range(NG)]

            def score_step(pe, p, s, g):
                t = tile_of(p, s)
                r, n = g // 2, min(HALF, CTX - g * HALF)
                local = NR * s + r
                if g == 0:
                    pe.wait_ge(q_ready, t + 1)
                if g % 2 == 0 and not (isinstance(p, int) and p == 0 and local < 2):
                    pe.wait_ge(taken, 2 * NR * p + local - 1)
                ins = nc.tensor.matmul(score_ps[:, local % 2, (g % 2) * HALF:(g % 2) * HALF + n], q_buf[:, s, :],
                                       k.key1_T[:, g * HALF:g * HALF + n], start=True, stop=True)
                if g % 2 == 1 or g == NG - 1:
                    ins.then_inc(range_ready, 1)

            def weigh_turn(pe, p, s, g):
                t, local = tile_of(p, s), NG * s + g
                c0, m = GROUPS[g]
                last_key = min(CTX, (c0 + m) * P)
                pe.wait_ge(exp_done, NR * t + (last_key - 1) // WIDE + 1)
                if due(NG * p + local // 2):
                    pe.wait_ge(copied[local % 2], NG * p + local // 2)
                for j in range(m):
                    keys = min(P, CTX - (c0 + j) * P)
                    ins = nc.tensor.transpose(turn_ps[0:keys, local % 2, j * P:(j + 1) * P],
                                              scores[:, s, (c0 + j) * P:(c0 + j) * P + keys], k.ident[:])
                ins.then_inc(group_turned, 1)

            def weigh_add(pe, p, s, g):
                t, local = tile_of(p, s), NG * s + g
                c0, m = GROUPS[g]
                pe.wait_ge(copied[local % 2], NG * p + local // 2 + 1)
                if g == 0 and due(t - 1):
                    pe.wait_ge(merged_ready, t - 1)
                for j in range(m):
                    keys = min(P, CTX - (c0 + j) * P)
                    ins = nc.tensor.matmul(acc_ps[:, s, 0:D], turned[0:keys, local % 2, j * P:(j + 1) * P],
                                           k.val1[0:keys, c0 + j, :], start=(c0 + j == 0), stop=(c0 + j == NCH - 1))
                ins.then_inc(pv_done, 1)

            def copy_group(eng, copy, p, s, g):
                local = NG * s + g
                c0, m = GROUPS[g]
                eng.wait_ge(group_turned, 2 * NG * p + local + 1)
                if due(2 * NG * p + local - 1):
                    eng.wait_ge(pv_done, 2 * NG * p + local - 1)
                full = min(m, NCH - 1 - c0)
                ins = copy(turned[:, local % 2, 0:full * P], turn_ps[:, local % 2, 0:full * P])
                if full < m:
                    ins = copy(turned[0:TAIL, local % 2, full * P:m * P], turn_ps[0:TAIL, local % 2, full * P:m * P])
                ins.then_inc(copied[local % 2], 1)

            def tile_on_pe(pe, p, s, nxt):
                for g in range(NG + 1):
                    if g < NG:
                        if nxt:
                            for i in steps_at[g]:
                                score_step(pe, *nxt, i)
                        weigh_turn(pe, p, s, g)
                    if g >= 1:
                        weigh_add(pe, p, s, g - 1)

            def take_range(dve, p, s, r):
                t, local = tile_of(p, s), NR * s + r
                c0, cols = RANGES[r]
                dve.wait_ge(range_ready, 2 * NR * p + local + 1)
                nc.vector.tensor_scalar(scores[:, s, c0:c0 + cols], score_ps[:, local % 2, 0:cols], 1.0, None, ALU.mult,
                                        ALU.max, accum_out=top[:, s, r:r + 1]).then_inc(taken, 1)
                if r == NR - 1:
                    dve.wait_ge(taken, NR * (t + 1))
                    nc.vector.tensor_reduce(neg[:, s:s + 1], top[:, s, :], AX.X, ALU.max, negate=True).then_inc(neg_ready, 1)

            def fetch_query(dve, p, s):
                t = tile_of(p, s)
                src = q_T[:, t * P:(t + 1) * P] if isinstance(p, int) else q_T[:, bass.ds(t * P, P)]
                nc.vector.tensor_copy(q_buf[:, s, :], src).then_inc(q_ready, 1)

            def tile_on_dve(dve, p, s, nxt):
                if nxt:
                    fetch_query(dve, *nxt)
                for g in range(NG):
                    if nxt:
                        for r in ranges_at[g]:
                            take_range(dve, *nxt, r)
                    if (NG * s + g) % 2 == 0:
                        copy_group(dve, nc.vector.tensor_copy, p, s, g)
                t = tile_of(p, s)
                dve.wait_ge(exp_done, NR * (t + 1))
                nc.vector.tensor_reduce(total[:, s:s + 1], sums[:, s, :], AX.X, ALU.add).then_inc(summed, 1)
                dve.wait_ge(summed, t + 1)
                nc.vector.reciprocal(recip[:, s:s + 1], total[:, s:s + 1]).then_inc(recip_ready, 1)
                dve.wait_ge(recip_ready, t + 1)
                dve.wait_ge(pv_done, NG * (t + 1))
                out = merged[:, t, :] if isinstance(p, int) else merged[:, bass.ds(t, 1), :].rearrange("p o e -> p (o e)")
                nc.vector.scalar_tensor_tensor(out=out, in0=acc_ps[:, s, 0:D], scalar=recip[:, s:s + 1], in1=b_v[:],
                                               op0=ALU.mult, op1=ALU.add).then_inc(merged_ready, 1)

            def exponentiate(act, p, s, r):
                t = tile_of(p, s)
                c0, cols = RANGES[r]
                if r == 0:
                    act.wait_ge(neg_ready, t + 1)
                    if due(t - 1):
                        act.wait_ge(summed, t - 1)
                nc.scalar.activation(scores[:, s, c0:c0 + cols], scores[:, s, c0:c0 + cols], ACT.Exp,
                                     bias=neg[:, s:s + 1], accum_out=sums[:, s, r:r + 1]).then_inc(exp_done, 1)

            def tile_on_act(act, p, s, nxt):
                mine = [g for g in range(NG) if (NG * s + g) % 2 == 1]
                for i, g in enumerate(mine[:-1]):
                    exponentiate(act, p, s, i + 1)
                    copy_group(act, nc.scalar.copy, p, s, g)
                if len(mine) < NR:
                    exponentiate(act, p, s, NR - 1)
                if len(mine) == NR and nxt:
                    exponentiate(act, *nxt, 0)
                copy_group(act, nc.scalar.copy, p, s, mine[-1])
                if len(mine) < NR and nxt:
                    exponentiate(act, *nxt, 0)

            LAST = NT // 2 - 1
            with nc.Block() as block:
                @block.tensor
                def _(pe):
                    for g in range(NG):
                        score_step(pe, 0, 0, g)
                    tile_on_pe(pe, 0, 0, (0, 1))
                    tile_on_pe(pe, 0, 1, (1, 0))
                    with nc.tensor.Fori(1, LAST) as p:
                        tile_on_pe(pe, p, 0, (p, 1))
                        tile_on_pe(pe, p, 1, (p + 1, 0))
                    tile_on_pe(pe, LAST, 0, (LAST, 1))
                    tile_on_pe(pe, LAST, 1, None)

                @block.vector
                def _(dve):
                    fetch_query(dve, 0, 0)
                    for r in range(NR):
                        take_range(dve, 0, 0, r)
                    tile_on_dve(dve, 0, 0, (0, 1))
                    tile_on_dve(dve, 0, 1, (1, 0))
                    with nc.vector.Fori(1, LAST) as p:
                        tile_on_dve(dve, p, 0, (p, 1))
                        tile_on_dve(dve, p, 1, (p + 1, 0))
                    tile_on_dve(dve, LAST, 0, (LAST, 1))
                    tile_on_dve(dve, LAST, 1, None)

                @block.scalar
                def _(act):
                    exponentiate(act, 0, 0, 0)
                    tile_on_act(act, 0, 0, (0, 1))
                    tile_on_act(act, 0, 1, (1, 0))
                    with nc.scalar.Fori(1, LAST) as p:
                        tile_on_act(act, p, 0, (p, 1))
                        tile_on_act(act, p, 1, (p + 1, 0))
                    tile_on_act(act, LAST, 0, (LAST, 1))
                    tile_on_act(act, LAST, 1, None)

        with ExitStack() as tmp:
            out_ps = k.ps("x1_out_ps", [P, NT, D], tmp)
            projection = Projection(k, "x1", merged, w_out, out_ps, tmp)
            with nc.Block() as block:
                @block.tensor
                def _(pe):
                    for t in range(NT):
                        projection.turn(pe, t)
                    projection.multiply(pe)

                @block.scalar
                def _(act):
                    projection.copy(act)
            residual_norm(k, "norm4", out_ps)


def experts1(k, store=None):
    nc, d = k.nc, k.dram
    E, F, TOP = 8, 2 * P, 2
    PADS = 8 - TOP
    LOWEST = -1e38
    ctx = ExitStack()
    with ctx:
        w1 = k.sb("e1_w1", [P, 2, F], F32, ctx)
        w2 = k.sb("e1_w2", [P, 2, F], F32, ctx)
        w3 = k.sb("e1_w3", [P, 2, 2, D], F32, ctx)
        wg, b1, b2, b3 = k.params.e1_wg, k.params.e1_b1, k.params.e1_b2, k.params.e1_b3
        acc = k.sb("e1_acc", [P, NT, D], F32, ctx)
        gates = k.sb("e1_gates", [P, NT, E], F32, ctx)
        gate_act = k.sb("e1_silu", [P, 2, T], F32, ctx)
        hidden = k.sb("e1_hidden", [P, 2, 2, T], F32, ctx)
        up_loaded = [k.sem(f"e1_w12_slot{i}_loaded") for i in range(2)]
        down_loaded = [k.sem(f"e1_w3_slot{i}_loaded") for i in range(2)]
        out_done, added = k.sem("e1_out_done"), [k.sem("e1_added_even"), k.sem("e1_added_odd")]

        def load_up(sp, e, s):
            for buf, n in ((w1, "W1"), (w2, "W2")):
                sp.dma_start(buf[:, s, :], one(d[f"L1_ffn_{n}_T"], e)).then_inc(up_loaded[s], 16)

        def load_down(sp, e, s):
            sp.dma_start(w3[:, s, :, :], one(d["L1_ffn_W3_T"], e).rearrange("(f p) m -> p f m", p=P)).then_inc(
                down_loaded[s], 16)

        scores = k.sb("e1_scores", [P, NT, E + PADS], F32, ctx)
        top8 = k.sb("e1_top8", [P, NT, 8], F32, ctx)
        wanted = k.sb("e1_wanted", [P, NT, 8], F32, ctx)
        left = k.sb("e1_left", [P, NT, E + PADS], F32, ctx)
        chosen = k.sb("e1_chosen", [P, NT, E], F32, ctx)
        raised = k.sb("e1_raised", [P, NT, E], F32, ctx)
        total = k.sb("e1_total", [P, NT], F32, ctx)
        gates_T = k.sb("e1_gates_T", [E, T], F32, ctx)
        scores_ready, shifted, exp_ready = (k.sem("e1_scores_ready"), k.sem("e1_shifted"),
                                                  k.sem("e1_exp_ready"))
        gates_ready, turned, turn_copied, b3_ready = (k.sem("e1_gates_ready"), k.sem("e1_turned"),
                                                      k.sem("e1_turn_copied"), k.sem("e1_b3_ready"))

        with ExitStack() as tmp:
            a_ps = k.ps("e1_a_ps", [P, T], tmp)
            b_ps = k.ps("e1_b_ps", [P, T], tmp)
            out_ps = k.ps("e1_out_ps", [P, 2, NT, D], tmp)
            score_ps = out_ps[:, 0, :, 0:E]
            b3_ps = out_ps[:, 0, :, :]
            turn_ps = out_ps[0:E, 1, :, :].rearrange("e t d -> e (t d)")
            acc_ready = k.sem("e1_acc_ready")
            a_ready, b_ready, silu_done, hidden_done = (k.sem("e1_a_ready"), k.sem("e1_b_ready"), k.sem("e1_silu_done"),
                                                        k.sem("e1_hidden_done"))

            def up(pe, e, s, f, uses):
                pe.wait_ge(up_loaded[s], 32 * (uses + 1))
                first = isinstance(e, int) and e == 0 and f == 0
                for w, ps, ready, used in ((w1, a_ps, a_ready, silu_done), (w2, b_ps, b_ready, hidden_done)):
                    if not first:
                        pe.wait_ge(used, 2 * e + f)
                    for h in range(2):
                        ins = nc.tensor.matmul(ps[:, h * HALF:(h + 1) * HALF], w[:, s, f * P:(f + 1) * P],
                                               k.x_T[:, h * HALF:(h + 1) * HALF], start=True, stop=True)
                    ins.then_inc(ready, 1)

            def down(pe, e, s, uses, part):
                if part == 0:
                    pe.wait_ge(hidden_done, 2 * e + 2)
                    pe.wait_ge(down_loaded[s], 16 * (uses + 1))
                    if not (isinstance(uses, int) and uses == 0):
                        pe.wait_ge(added[s], uses)
                for t in range(part * NT // 2, (part + 1) * NT // 2):
                    for f in range(2):
                        ins = nc.tensor.matmul(out_ps[:, s, t, :], hidden[:, s, f, t * P:(t + 1) * P], w3[:, s, f, :],
                                               start=(f == 0), stop=(f == 1))
                if part:
                    ins.then_inc(out_done, 1)

            def activate(act, e, s, f):
                act.wait_ge(a_ready, 2 * e + f + 1)
                if not (isinstance(e, int) and e == 0):
                    act.wait_ge(hidden_done, 2 * e + f - 1)
                nc.scalar.activation(gate_act[:, f, :], a_ps[:], ACT.Silu,
                                     bias=b1[:, bass.ds(2 * e + f, 1)]).then_inc(silu_done, 1)

            def combine(dve, e, s, f):
                dve.wait_ge(b_ready, 2 * e + f + 1)
                dve.wait_ge(silu_done, 2 * e + f + 1)
                nc.vector.scalar_tensor_tensor(out=hidden[:, s, f, :], in0=b_ps[:], scalar=b2[:, bass.ds(2 * e + f, 1)],
                                               in1=gate_act[:, f, :], op0=ALU.add, op1=ALU.mult).then_inc(hidden_done, 1)

            def add_up(dve, e, s, uses):
                dve.wait_ge(out_done, e + 1)
                if not (isinstance(e, int) and e == 0):
                    dve.wait_ge(added[1 - s], uses + s)
                for t in range(NT):
                    ins = nc.vector.scalar_tensor_tensor(out=acc[:, t, :], in0=out_ps[:, s, t, :],
                                                         scalar=gates[:, t, bass.ds(e, 1)], in1=acc[:, t, :],
                                                         op0=ALU.mult, op1=ALU.add)
                ins.then_inc(added[s], 1)

            def load_early(sp):
                for s in range(2):
                    load_up(sp, s, s)
                    load_down(sp, s, s)

            def score(pe):
                for t in range(NT):
                    ins = nc.tensor.matmul(score_ps[:, t, :], k.x_T[:, t * P:(t + 1) * P], wg[:], start=True, stop=True)
                ins.then_inc(scores_ready, 1)

            def turn_gates(pe):
                pe.wait_ge(gates_ready, 1)
                for t in range(NT):
                    ins = nc.tensor.transpose(turn_ps[:, t * P:(t + 1) * P], gates[:, t, :], k.ident[:])
                ins.then_inc(turned, 1)
                pe.wait_ge(turn_copied, 1)
                for t in range(NT):
                    ins = nc.tensor.matmul(b3_ps[:, t, :], gates_T[:, t * P:(t + 1) * P], b3[:], start=True, stop=True)
                ins.then_inc(b3_ready, 1)

            def raise_scores(act):
                act.wait_ge(shifted, 1)
                nc.scalar.activation(raised[:], raised[:], ACT.Exp).then_inc(exp_ready, 1)
                nc.scalar.preload_act_table(ACT.Silu)

            def copy_gates(act):
                act.wait_ge(turned, 1)
                nc.scalar.copy(gates_T[:], turn_ps).then_inc(turn_copied, 1)

            def choose_gates(dve):
                link = k.chain(dve)
                nc.vector.memset(scores[:, :, E:E + PADS], LOWEST)
                nc.vector.memset(wanted[:], LOWEST)
                dve.wait_ge(scores_ready, 1)
                link(nc.vector.tensor_copy(scores[:, :, 0:E], score_ps))
                choose(nc, link, scores, E, PADS, TOP, LOWEST, top8, wanted, left, chosen[:])
                nc.vector.tensor_tensor(raised[:], scores[:, :, 0:E], top8[:, :, 0:1].to_broadcast([P, NT, E]),
                                        ALU.subtract).then_inc(shifted, 1)
                dve.wait_ge(exp_ready, 1)
                link(nc.vector.tensor_tensor(raised[:], raised[:], chosen[:], ALU.mult))
                link(nc.vector.tensor_reduce(total[:], raised[:], AX.X, ALU.add))
                link(nc.vector.reciprocal(total[:], total[:]))
                nc.vector.tensor_tensor(gates[:], raised[:], total[:].unsqueeze(2).to_broadcast([P, NT, E]),
                                        ALU.mult).then_inc(gates_ready, 1)

            def start_sum(dve):
                dve.wait_ge(b3_ready, 1)
                nc.vector.tensor_tensor(acc[:], b3_ps, k.x_tok[:], ALU.add).then_inc(acc_ready, 1)

            with nc.Block() as block:
                @block.sync
                def _(sp):
                    load_early(sp)
                    with nc.sync.Fori(1, E // 2) as p:
                        for s in range(2):
                            sp.wait_ge(b_ready, 4 * p + 2 * s - 2)
                            load_up(sp, 2 * p + s, s)
                            if s == 1:
                                sp.wait_ge(out_done, 2 * p - 1)
                                load_down(sp, 2 * p, 0)
                        sp.wait_ge(out_done, 2 * p)
                        load_down(sp, 2 * p + 1, 1)

                def pe_step(pe, e, s, uses, prev_uses):
                    up(pe, e, s, 0, uses)
                    down(pe, e - 1, 1 - s, prev_uses, 0)
                    up(pe, e, s, 1, uses)
                    down(pe, e - 1, 1 - s, prev_uses, 1)

                @block.tensor
                def _(pe):
                    score(pe)
                    for f in range(2):
                        up(pe, 0, 0, f, 0)
                    turn_gates(pe)
                    pe.wait_ge(acc_ready, 1)
                    pe_step(pe, 1, 1, 0, 0)
                    with nc.tensor.Fori(1, E // 2) as p:
                        pe_step(pe, 2 * p, 0, p, p - 1)
                        pe_step(pe, 2 * p + 1, 1, p, p)
                    for part in range(2):
                        down(pe, E - 1, 1, E // 2 - 1, part)

                @block.scalar
                def _(act):
                    raise_scores(act)
                    activate(act, 0, 0, 0)
                    activate(act, 0, 0, 1)
                    copy_gates(act)
                    activate(act, 1, 1, 0)
                    activate(act, 1, 1, 1)
                    with nc.scalar.Fori(1, E // 2) as p:
                        for s in range(2):
                            for f in range(2):
                                activate(act, 2 * p + s, s, f)

                @block.vector
                def _(dve):
                    choose_gates(dve)
                    for f in range(2):
                        combine(dve, 0, 0, f)
                    start_sum(dve)
                    for f in range(2):
                        combine(dve, 1, 1, f)
                    dve.wait_ge(acc_ready, 1)
                    add_up(dve, 0, 0, 0)
                    with nc.vector.Fori(1, E // 2) as p:
                        for f in range(2):
                            combine(dve, 2 * p, 0, f)
                        add_up(dve, 2 * p - 1, 1, p - 1)
                        for f in range(2):
                            combine(dve, 2 * p + 1, 1, f)
                        add_up(dve, 2 * p, 0, p)
                    add_up(dve, E - 1, 1, E // 2 - 1)
        residual_norm(k, "norm5", acc, added=True, store=store)


def decoder(nc, dram, out):
    with ExitStack() as ctx:
        k = Core(nc, dram, ctx)
        load_and_constants(k)
        lay_out(k)
        mamba(k)
        context_attention(k)
        experts0(k)
        self_attention(k)
        context_attention1(k)
        experts1(k, store=out.rearrange("b (t p) d -> p (b t) d", p=P))


TRANSPOSED = ["L0_attn_W_in", "L0_attn_W_xproj", "L0_attn_W_dt", "L0_attn_W_out", "L1_xattn_Wk", "L1_xattn_Wv",
              "L1_xattn_Wq", "L1_xattn_Wo", "L1_ffn_Wg",
              "L1_attn_a_q", "L1_attn_a_v"]
PER_FEATURE = ["L0_ffn_sb1", "L0_ffn_rb1", "L1_ffn_b1", "L1_ffn_b2"]


def kernel(**inputs):
    import numpy as _np
    import concourse.bacc as _bacc
    from concourse import mybir as _mybir
    from concourse.bass_utils import run_bass_kernel_spmd as _run

    laid = {n: _np.asarray(a) for n, a in inputs.items()}
    laid["x_T"] = laid["x"][0].T
    laid["ctx_T"] = laid.pop("ctx_1024")[0].T
    for n in TRANSPOSED:
        laid[n + "_T"] = laid.pop(n).T
    for n in ("L1_ffn_W1", "L1_ffn_W2", "L1_ffn_W3"):
        laid[n + "_T"] = laid.pop(n).transpose(0, 2, 1)
    for n in PER_FEATURE:
        laid[n + "_p"] = laid.pop(n).reshape(-1, 2, P).transpose(2, 0, 1).reshape(P, -1)
    nc = _bacc.Bacc("TRN2", target_bir_lowering=False, num_devices=1)
    arrays, dram = {}, {}
    for name, a in laid.items():
        a = _np.ascontiguousarray(a)
        arrays[name] = a
        dram[name] = nc.dram_tensor(name, a.shape, _mybir.dt.from_np(a.dtype), kind="ExternalInput").ap()
    out = nc.dram_tensor("out", (1, T, D), F32, kind="ExternalOutput").ap()
    decoder(nc, dram, out)
    r = _run(nc, [arrays], core_ids=[0])
    return r.results[0]["out"]
```
